# Optimizing a Trainium2 kernel written in Bass

```python
import numpy as np
import jax
import jax.numpy as jnp

def _softmax(x, axis=-1):
    return jax.nn.softmax(x, axis=axis)

def _gelu(x):
    return jax.nn.gelu(x, approximate=True)

def _silu(x):
    return jax.nn.silu(x)

def _sigmoid(x):
    return jax.nn.sigmoid(x)

def _layernorm(x, axis=-1, eps=1e-05):
    m = jnp.mean(x, axis=axis, keepdims=True)
    v = jnp.var(x, axis=axis, keepdims=True)
    return (x - m) / jnp.sqrt(v + eps)

def _scatter_add(tgt, idx, src, axis=0):
    return tgt.at[idx].add(src)

def _segment_sum(src, seg, n):
    return jax.ops.segment_sum(src, seg, n)
kernel_name = 'mk_vit_tower_d1_tok_img256_r4_a581df'

def setup_inputs(seed: int=0):
    np.random.seed(seed)
    _w = jnp.asarray

    def _rec_inputs():
        import jax
        import jax.numpy as jnp
        _rk = jax.random.key(seed)
        x = 7.57192e-06 + 1.00007 * jax.random.normal(jax.random.fold_in(_rk, 1), (16, 3, 224, 224), jnp.float32)
        return x
    x = _rec_inputs()

    def _L0_tok_setup():
        import jax, jax.numpy as jnp
        import numpy as np
        import math
        GRID = 28
        NUM_PATCHES = GRID * GRID
        PATCH = 8
        IN_CH = 3
        HIDDEN = 64
        BATCH = 64

        def build_grid_edges():
            edges = []
            for i in range(GRID):
                for j in range(GRID):
                    cur = i * GRID + j
                    if j < GRID - 1:
                        edges.append([cur, cur + 1])
                    if i < GRID - 1:
                        edges.append([cur, cur + GRID])
            e = np.asarray(edges, dtype=np.int32).T
            e = np.concatenate([e, e[::-1]], axis=1)
            return jnp.asarray(e)

        def sin_positional_encoding(n, d):
            pos = jnp.arange(n, dtype=jnp.float32)[:, None]
            div = jnp.exp(jnp.arange(0, d, 2, dtype=jnp.float32) * (-math.log(10000.0) / d))
            pe = jnp.zeros((n, d), dtype=jnp.float32)
            pe = pe.at[:, 0::2].set(jnp.sin(pos * div))
            pe = pe.at[:, 1::2].set(jnp.cos(pos * div))
            return pe
        key = jax.random.key(seed)
        ks = jax.random.split(key, 8)
        s = 0.02
        return {'x': jax.random.normal(ks[0], (BATCH, IN_CH, 224, 224), dtype=jnp.float32), 'W_embed': jax.random.normal(ks[1], (IN_CH * PATCH * PATCH, HIDDEN), dtype=jnp.float32) * s, 'b_embed': jax.random.normal(ks[2], (HIDDEN,), dtype=jnp.float32) * s, 'W_gcn': jax.random.normal(ks[3], (3, HIDDEN, HIDDEN), dtype=jnp.float32) * s, 'b_gcn': jax.random.normal(ks[4], (3, HIDDEN), dtype=jnp.float32) * s, 'W_out': jax.random.normal(ks[5], (HIDDEN, 64), dtype=jnp.float32) * s, 'b_out': jax.random.normal(ks[6], (64,), dtype=jnp.float32) * s, 'edge_index': build_grid_edges()}
    _L0_tok_all = _L0_tok_setup()
    _L0_tok_in = {k: v for k, v in _L0_tok_all.items() if k in ('W_embed', 'b_embed', 'W_gcn', 'b_gcn', 'W_out', 'b_out', 'edge_index')}
    del _L0_tok_all

    def _L0_attn_setup():
        import jax, jax.numpy as jnp
        import numpy as np
        B_SZ, T, H, N, L = (4, 128, 64, 64, 4)
        EPS = 1e-05

        def _hippo(n):
            i = np.arange(n)[:, None]
            j = np.arange(n)[None, :]
            A = np.where(i >= j, (-1.0) ** (i - j) * np.sqrt((2 * i + 1.0) * (2 * j + 1.0)), 0.0)
            A = A / (1.1 * np.linalg.norm(A, 2))
            return A.astype(np.float32)

        def _xavier(key, shape):
            fan_in, fan_out = (shape[1], shape[0])
            a = float(np.sqrt(6.0 / (fan_in + fan_out)))
            return jax.random.uniform(key, shape, jnp.float32, -a, a)

        def _ln(x):
            m = jnp.mean(x, -1, keepdims=True)
            v = jnp.mean((x - m) ** 2, -1, keepdims=True)
            return (x - m) / jnp.sqrt(v + EPS)

        def _ssm_layer(h, A, B, C, D):
            Cbar = C.mean(0)
            BT = B.T
            DT = D.T

            def step(state, u):
                y = jnp.einsum('bnh,n->bh', state, Cbar) + u @ DT
                new_state = jnp.einsum('nm,bmh->bnh', A, state) + (u @ BT)[:, :, None]
                return (new_state, y)
            state0 = jnp.zeros((h.shape[0], A.shape[0], h.shape[2]), h.dtype)
            _, ys = jax.lax.scan(step, state0, jnp.swapaxes(h, 0, 1))
            y = jnp.swapaxes(ys, 0, 1)
            y = jax.nn.gelu(y, approximate=False) + h
            return _ln(y)
        key = jax.random.key(seed)
        ks = jax.random.split(key, 8)
        x = jax.random.normal(ks[0], (B_SZ, T, H), jnp.float32)
        A = jnp.broadcast_to(jnp.asarray(_hippo(N)), (L, N, N))
        Bm = jnp.stack([_xavier(jax.random.fold_in(ks[1], l), (N, H)) for l in range(L)])
        Cm = jnp.stack([_xavier(jax.random.fold_in(ks[2], l), (H, N)) for l in range(L)])
        Dm = jnp.stack([_xavier(jax.random.fold_in(ks[3], l), (H, H)) for l in range(L)])
        Win = _xavier(ks[4], (H, H))
        bin_ = jnp.zeros((H,), jnp.float32)
        Wout = _xavier(ks[5], (H, H))
        bout = jnp.zeros((H,), jnp.float32)
        return {'x': x, 'Win': Win, 'bin_': bin_, 'Wout': Wout, 'bout': bout, 'A': A, 'Bm': Bm, 'Cm': Cm, 'Dm': Dm}
    _L0_attn_all = _L0_attn_setup()
    _L0_attn_in = {k: v for k, v in _L0_attn_all.items() if k in ('Win', 'bin_', 'Wout', 'bout', 'A', 'Bm', 'Cm', 'Dm')}
    del _L0_attn_all

    def _L0_ffn_setup():
        import jax, jax.numpy as jnp
        import numpy as np
        B, S, D = (8, 1024, 64)
        H = 4 * D
        CAPACITY = 0.5
        key = jax.random.key(seed)
        ks = jax.random.split(key, 6)
        x = jax.random.normal(ks[0], (B, S, D), dtype=jnp.float32)
        attention_mask = jnp.zeros((B, 1, 1, S), dtype=jnp.float32)
        wr = jax.random.normal(ks[1], (D, 1), dtype=jnp.float32) * 0.02
        br = jnp.zeros((1,), dtype=jnp.float32)
        w1 = jax.random.normal(ks[2], (D, H), dtype=jnp.float32) * 0.02
        b1 = jnp.zeros((H,), dtype=jnp.float32)
        w2 = jax.random.normal(ks[3], (H, D), dtype=jnp.float32) * 0.02
        b2 = jnp.zeros((D,), dtype=jnp.float32)
        return {'x': x, 'attention_mask': attention_mask, 'wr': wr, 'br': br, 'w1': w1, 'b1': b1, 'w2': w2, 'b2': b2}
    _L0_ffn_all = _L0_ffn_setup()
    _L0_ffn_in = {k: v for k, v in _L0_ffn_all.items() if k in ('attention_mask', 'wr', 'br', 'w1', 'b1', 'w2', 'b2')}
    del _L0_ffn_all
    return {'x': x, 'L0_tok_W_embed': _L0_tok_in['W_embed'], 'L0_tok_b_embed': _L0_tok_in['b_embed'], 'L0_tok_W_gcn': _L0_tok_in['W_gcn'], 'L0_tok_b_gcn': _L0_tok_in['b_gcn'], 'L0_tok_W_out': _L0_tok_in['W_out'], 'L0_tok_b_out': _L0_tok_in['b_out'], 'L0_tok_edge_index': _L0_tok_in['edge_index'], 'L0_attn_Win': _L0_attn_in['Win'], 'L0_attn_bin_': _L0_attn_in['bin_'], 'L0_attn_Wout': _L0_attn_in['Wout'], 'L0_attn_bout': _L0_attn_in['bout'], 'L0_attn_A': _L0_attn_in['A'], 'L0_attn_Bm': _L0_attn_in['Bm'], 'L0_attn_Cm': _L0_attn_in['Cm'], 'L0_attn_Dm': _L0_attn_in['Dm'], 'L0_ffn_attention_mask': _L0_ffn_in['attention_mask'], 'L0_ffn_wr': _L0_ffn_in['wr'], 'L0_ffn_br': _L0_ffn_in['br'], 'L0_ffn_w1': _L0_ffn_in['w1'], 'L0_ffn_b1': _L0_ffn_in['b1'], 'L0_ffn_w2': _L0_ffn_in['w2'], 'L0_ffn_b2': _L0_ffn_in['b2']}

def reference(x, L0_tok_W_embed, L0_tok_b_embed, L0_tok_W_gcn, L0_tok_b_gcn, L0_tok_W_out, L0_tok_b_out, L0_tok_edge_index, L0_attn_Win, L0_attn_bin_, L0_attn_Wout, L0_attn_bout, L0_attn_A, L0_attn_Bm, L0_attn_Cm, L0_attn_Dm, L0_ffn_attention_mask, L0_ffn_wr, L0_ffn_br, L0_ffn_w1, L0_ffn_b1, L0_ffn_w2, L0_ffn_b2):
    import jax
    import jax.numpy as jnp

    def _L0_tok_ref(x, W_embed, b_embed, W_gcn, b_gcn, W_out, b_out, edge_index):
        import jax, jax.numpy as jnp
        import numpy as np
        import math
        GRID = 28
        NUM_PATCHES = GRID * GRID
        PATCH = 8
        IN_CH = 3
        HIDDEN = 64
        BATCH = 64

        def build_grid_edges():
            edges = []
            for i in range(GRID):
                for j in range(GRID):
                    cur = i * GRID + j
                    if j < GRID - 1:
                        edges.append([cur, cur + 1])
                    if i < GRID - 1:
                        edges.append([cur, cur + GRID])
            e = np.asarray(edges, dtype=np.int32).T
            e = np.concatenate([e, e[::-1]], axis=1)
            return jnp.asarray(e)

        def sin_positional_encoding(n, d):
            pos = jnp.arange(n, dtype=jnp.float32)[:, None]
            div = jnp.exp(jnp.arange(0, d, 2, dtype=jnp.float32) * (-math.log(10000.0) / d))
            pe = jnp.zeros((n, d), dtype=jnp.float32)
            pe = pe.at[:, 0::2].set(jnp.sin(pos * div))
            pe = pe.at[:, 1::2].set(jnp.cos(pos * div))
            return pe
        B = x.shape[0]
        N = NUM_PATCHES
        p = x.reshape(B, IN_CH, GRID, PATCH, GRID, PATCH)
        p = p.transpose(0, 2, 4, 1, 3, 5).reshape(B, N, IN_CH * PATCH * PATCH)
        h = p @ W_embed + b_embed + sin_positional_encoding(N, HIDDEN)[None]
        src, dst = (edge_index[0], edge_index[1])
        deg = jnp.zeros((N,), dtype=h.dtype).at[dst].add(1.0) + 1.0
        dinv = deg ** (-0.5)
        enorm = (dinv[src] * dinv[dst])[None, :, None]
        snorm = (1.0 / deg)[None, :, None]
        for i in range(3):
            hw = h @ W_gcn[i]
            agg = hw * snorm
            agg = agg.at[:, dst].add(hw[:, src] * enorm)
            h = jax.nn.relu(agg + b_gcn[i])
        return h @ W_out + b_out

    def _L0_attn_ref(x, Win, bin_, Wout, bout, A, Bm, Cm, Dm):
        import jax, jax.numpy as jnp
        import numpy as np
        B_SZ, T, H, N, L = (4, 128, 64, 64, 4)
        EPS = 1e-05

        def _hippo(n):
            i = np.arange(n)[:, None]
            j = np.arange(n)[None, :]
            A = np.where(i >= j, (-1.0) ** (i - j) * np.sqrt((2 * i + 1.0) * (2 * j + 1.0)), 0.0)
            A = A / (1.1 * np.linalg.norm(A, 2))
            return A.astype(np.float32)

        def _xavier(key, shape):
            fan_in, fan_out = (shape[1], shape[0])
            a = float(np.sqrt(6.0 / (fan_in + fan_out)))
            return jax.random.uniform(key, shape, jnp.float32, -a, a)

        def _ln(x):
            m = jnp.mean(x, -1, keepdims=True)
            v = jnp.mean((x - m) ** 2, -1, keepdims=True)
            return (x - m) / jnp.sqrt(v + EPS)

        def _ssm_layer(h, A, B, C, D):
            Cbar = C.mean(0)
            BT = B.T
            DT = D.T

            def step(state, u):
                y = jnp.einsum('bnh,n->bh', state, Cbar) + u @ DT
                new_state = jnp.einsum('nm,bmh->bnh', A, state) + (u @ BT)[:, :, None]
                return (new_state, y)
            state0 = jnp.zeros((h.shape[0], A.shape[0], h.shape[2]), h.dtype)
            _, ys = jax.lax.scan(step, state0, jnp.swapaxes(h, 0, 1))
            y = jnp.swapaxes(ys, 0, 1)
            y = jax.nn.gelu(y, approximate=False) + h
            return _ln(y)
        h = x @ Win.T + bin_
        for l in range(L):
            h = _ssm_layer(h, A[l], Bm[l], Cm[l], Dm[l])
        h = _ln(h)
        return h @ Wout.T + bout

    def _L0_ffn_ref(x, attention_mask, wr, br, w1, b1, w2, b2):
        import jax, jax.numpy as jnp
        import numpy as np
        B, S, D = (8, 1024, 64)
        H = 4 * D
        CAPACITY = 0.5
        b, s, d = x.shape
        weights = (jnp.einsum('bsd,do->bso', x, wr) + br)[..., 0]
        k = max(1, int(CAPACITY * s))
        kk = k - 1 if k > 1 else 1
        _, idx = jax.lax.top_k(weights, k)
        sel_idx = idx[:, :kk]
        sel = jnp.take_along_axis(x, sel_idx[:, :, None], axis=1)
        h = jax.nn.gelu(jnp.einsum('bkd,dh->bkh', sel, w1) + b1)
        y = jnp.einsum('bkh,hd->bkd', h, w2) + b2
        w_sel = jnp.take_along_axis(weights, sel_idx, axis=1)
        y = y * w_sel[..., None]
        batch_idx = jnp.arange(b)[:, None]
        processed = jnp.zeros_like(x).at[batch_idx, sel_idx].set(y)
        return processed + x
    h = _L0_tok_ref(x, L0_tok_W_embed, L0_tok_b_embed, L0_tok_W_gcn, L0_tok_b_gcn, L0_tok_W_out, L0_tok_b_out, L0_tok_edge_index)
    h = h + _L0_attn_ref(_layernorm(h, axis=-1), L0_attn_Win, L0_attn_bin_, L0_attn_Wout, L0_attn_bout, L0_attn_A, L0_attn_Bm, L0_attn_Cm, L0_attn_Dm)
    h = h + _L0_ffn_ref(_layernorm(h, axis=-1), L0_ffn_attention_mask, L0_ffn_wr, L0_ffn_br, L0_ffn_w1, L0_ffn_b1, L0_ffn_w2, L0_ffn_b2)
    return h

_drawn_inputs = setup_inputs


def setup_inputs(seed=0):
    import zlib

    import numpy as np

    out = dict(_drawn_inputs(seed))
    spreads = {'L0_attn_bin_': (0.0, 0.1),
     'L0_attn_bout': (0.0, 0.1),
     'L0_ffn_b1': (0.0, 0.8),
     'L0_ffn_b2': (0.0, 0.8)}
    factors = {'x': 8.0,
     'L0_tok_W_embed': 8.0,
     'L0_tok_b_embed': 8.0,
     'L0_tok_W_gcn': 2.9,
     'L0_attn_A': 7.111,
     'L0_ffn_wr': 6.461,
     'L0_ffn_w1': 8.0,
     'L0_ffn_w2': 8.0}
    for name, (base, spread) in spreads.items():
        noise = np.random.default_rng([zlib.crc32(name.encode()), seed]).standard_normal(out[name].shape)
        drawn = base * np.exp(spread * noise) if base else spread * noise
        out[name] = jnp.asarray(drawn.astype(out[name].dtype))
    for name, factor in factors.items():
        out[name] = (out[name] * factor).astype(out[name].dtype)
    return out
```

```python
from contextlib import ExitStack

import concourse.bass as bass
from concourse import mybir

F32 = mybir.dt.float32
BF16 = mybir.dt.bfloat16
I32 = mybir.dt.int32
ALU = mybir.AluOpType
ACT = mybir.ActivationFunctionType
AX = mybir.AxisListType

NB = 16
NP = NB // 2
HP = NP // 2
GRID = 28
N = GRID * GRID
TT = 112
NT = N // TT
HN = N // 2
CH = 64
LC = 28
NCH = N // LC
NG = 3
NL = 4
NE = 4 * GRID * (GRID - 1)
EC = 28
EP = NE // EC
ZW = LC + CH
QB = CH + 1
LEVELS = 5
SWC = LEVELS * CH + LC + CH
KK = N // 2 - 1
UNITS = 2 * NT
EPS = 1e-5
RADIX = [29, 26, 23, 20, 17, 14, 11, 8, 5, 2, 0]


def tower(nc, x, w_embed, b_embed, w_gcn, b_gcn, w_tok, b_tok, edges, w_in, b_in, w_out, b_out,
          A, B, C, D, wr, br, w1, b1, w2, b2, c_ident, c_sel, c_tri, c_sum, c_pos, c_digit, out):
    ctx = ExitStack()
    with ctx:
        def sb(name, shape, dt=F32):
            return ctx.enter_context(nc.sbuf_tensor(name, shape, dt))

        def sem(name):
            return ctx.enter_context(nc.semaphore(name))

        PS = ctx.enter_context(nc.psum_tensor("PS", [128, 8, 512], F32))

        UC = sb("UC", [128, NP, N])
        UCF = UC[:, :, :].rearrange("p g n -> p (g n)")
        BIG = sb("BIG", [128, 2 * NT * NB * CH])
        T = BIG[0:TT, 0:NT * NB * CH].rearrange("p (k b c) -> p k b c", k=NT, b=NB)
        RES = BIG[0:TT, NT * NB * CH:].rearrange("p (k b c) -> p k b c", k=NT, b=NB)
        HW = BIG[0:TT, 0:NT * NB * CH].rearrange("p (k g m) -> p k g m", k=NT, g=NP)
        Q0 = 2 * NT * NB * CH - NL * (LC + 1) * QB
        Q = BIG[0:CH, Q0:].rearrange("p (l q c) -> p l q c", l=NL, q=LC + 1)
        XS = sb("XS", [128, 2 * 2 * 1792])
        XIN = XS[0:84, :].rearrange("p (s w) -> p s w", s=2)
        XP = BIG[0:84, 0:7168].rearrange("p (s g q) -> p s g q", s=2, g=GRID)
        HID = XS[:, 0:8 * N].rearrange("p (s c n) -> p s c n", s=2, c=4)
        XTB = sb("XTB", [128, 2 * 3 * HN])
        XT = XTB[:, :].rearrange("p (s c g i) -> p s c g i", s=2, c=3, g=14)
        ONE = XTB[:, :].bitcast(BF16)
        EYEW = ONE[0:TT, 0:2 * N]
        OSRC = ONE[0:EP, 2 * N:4 * N].rearrange("p (s n) -> p s n", s=2)
        ODST = ONE[0:EP, 4 * N:4 * N + 2 * HN].rearrange("p (s n) -> p s n", s=2)
        GEL = XTB[0:TT, 0:1024].rearrange("p (s c) -> p s c", s=2)
        CM = sb("CM", [128, NT * N])
        ADJ = CM[0:TT, :].rearrange("p (k n) -> p k n", k=NT)
        RW = CM[:, 0:2 * LC * ZW].rearrange("p (a q z) -> p a q z", a=2, q=LC)
        R = sb("R", [128, NL, LC, QB])
        SWA = sb("SWA", [128, NL, SWC])
        SWS = sb("SWS", [128, LEVELS, 128])
        SW = sb("SW", [128, 2, LC + CH])
        POS = sb("POS", [128, N])
        IOTA = sb("IOTA", [128, N])
        IDENT = sb("IDENT", [128, 128])
        II = sb("II", [64, 128])
        SELF = sb("SELF", [24, 512], BF16)
        TRI = sb("TRI", [TT, 2 * TT], BF16)
        SUMM = sb("SUMM", [128, 129])
        DIG = sb("DIG", [128, len(RADIX)], I32)
        ONES = sb("ONES", [128, 129])
        WE = sb("WE", [128, 3, 128])
        WG = sb("WG", [128, NG, 128])
        WL = sb("WL", [128, 3, 128])
        RF = R[:, :, :, :].rearrange("p l q c -> p (l q c)")
        W1 = RF[:, 0:512].rearrange("p (q m) -> p q m", q=4)
        W2 = RF[:, 512:1024].rearrange("p (q m) -> p q m", q=4)
        WR = RF[:, 1024:2048].rearrange("p (g m) -> p g m", g=NP)
        BIAS = sb("BIAS", [128, 10])
        BROW = sb("BROW", [TT, 4, CH])
        U2 = UC[0:64, :, :].rearrange("p g n -> p (g n)")
        PAR = U2[:, 0:2048].rearrange("p (l m c) -> p l m c", l=NL, m=4)
        WIO = U2[:, 2048:2304].rearrange("p (m c) -> p m c", m=2)
        PN = U2[:, 2304:2816].rearrange("p (t l c) -> p t l c", t=2, l=NL)
        PNN = U2[:, 2816:3328].rearrange("p (l c) -> p l c", l=NL)
        EI = sb("EI", [EP, 2, EC], I32)
        EF = sb("EF", [EP, 2, EC])
        DG = sb("DG", [TT, 4, NT])
        DIAG = XTB[0:TT, 0:N].rearrange("p (k t) -> p k t", k=NT)
        DROW = sb("DROW", [128, N])
        AGG = XS[:, 0:2 * N].rearrange("p (s n) -> p s n", s=2)
        ST = POS[0:TT, 0:672].rearrange("p (h u s) -> p h u s", h=2, s=6)
        LNS = sb("LNS", [TT, 5, 56])
        MEAN = sb("MEAN", [TT, 2, 56])
        RSTD = sb("RSTD", [TT, 2, 56])
        ES = sb("ES", [TT, 128])
        SC = sb("SC", [128, 2, HP, LC + 1])
        SX = sb("SX", [128, HP, LC])
        ZF = sb("ZF", [TT, 3, 56])
        ZB = sb("ZB", [TT, 3, 56], BF16)
        Z3 = sb("Z3", [24, 2, N], BF16)
        WROW = CM[:, 0:N]
        JUNK = CM[:, N:2 * N]
        GTR = CM[0:NB, 2 * N:3 * N]
        EQR = CM[0:NB, 3 * N:4 * N]
        KEY = sb("KEY", [128, 4], I32)
        CNT = sb("CNT", [128, 2])
        PREF = sb("PREF", [128, 2], I32)
        WTOK = sb("WTOK", [TT, NT, NB])
        GEB = sb("GEB", [TT, 2, NT, NB], BF16)
        GSUM = sb("GSUM", [TT, NB])
        GSB = sb("GSB", [TT, NB], BF16)
        WM = sb("WM", [TT, NT, NB])
        YT = XS[0:TT, 8 * N:8 * N + 512]
        SF = IOTA[0:24, 0:512]

        par_in = sem("par_in")
        wts_in = sem("wts_in")
        mlp_in = sem("mlp_in")
        zeroed = sem("zeroed")
        edge_in = sem("edge_in")
        x_in = [sem("x_in0"), sem("x_in1")]
        x_perm = sem("x_perm")
        pre_mm = sem("pre_mm")
        pre_ev = sem("pre_ev")
        eye_set = sem("eye_set")
        hot = sem("hot")
        hot_mm = sem("hot_mm")
        adj_ev = sem("adj_ev")
        deg_mm = sem("deg_mm")
        dve_ch = sem("dve_ch")
        pool_ch = sem("pool_ch")
        emb_t = sem("emb_t")
        emb_tv = sem("emb_tv")
        emb_tw = sem("emb_tw")
        emb_mm = sem("emb_mm")
        emb_ev = sem("emb_ev")
        hw_mm = sem("hw_mm")
        hw_ev = sem("hw_ev")
        agg_mm = sem("agg_mm")
        agg_sc = sem("agg_sc")
        h_ready = sem("h_ready")
        tok_mm = sem("tok_mm")
        tok_ev = sem("tok_ev")
        gel_used = sem("gel_used")
        t_ready = sem("t_ready")
        tp_mm = sem("tp_mm")
        uc_ready = sem("uc_ready")
        conv_mm = sem("conv_mm")
        es_ev = sem("es_ev")
        scan_mm = sem("scan_mm")
        scan_ev = sem("scan_ev")
        z_mm = sem("z_mm")
        z_ev = sem("z_ev")
        z_split = sem("z_split")
        z_in = sem("z_in")
        staged = sem("staged")
        res_b = sem("res_b")
        r_mm = sem("r_mm")
        cnt_rd = sem("cnt_rd")
        rad_mm = sem("rad_mm")
        msk_rd = sem("msk_rd")
        msk_mm = sem("msk_mm")
        wm_rd = sem("wm_rd")
        f_mm = sem("f_mm")
        f_ev = sem("f_ev")
        y_mm = sem("y_mm")
        y_ev = sem("y_ev")
        stored = sem("stored")

        block = ctx.enter_context(nc.Block())

        prep = []

        def product(mms, copies, after):
            prep.append((mms, copies, after))
            return len(prep) - 1

        def bank(i):
            return PS[:, i % 8, :]

        def build_prep():
            p = len(prep)
            b = bank(p)
            last = product([(b[0:64, l:l + 1], PAR[:, l, 2, 0:64], ONES[0:64, 128:129]) for l in range(NL)],
                           [(Q[:, l, 0, 64:65], b[0:64, l:l + 1]) for l in range(NL)], -1)
            b = bank(len(prep))
            product([(b[:, 64 * j:64 * j + 64], WIO[:, j, :], IDENT[0:64, 0:64]) for j in range(2)],
                    [(WL[64 * a:64 * a + 64, 1 + j, 64 * a:64 * a + 64], b[64 * a:64 * a + 64, 64 * j:64 * j + 64])
                     for j in range(2) for a in range(2)], -1)
            b = bank(len(prep))
            product([(b[:, 64 * l:64 * l + 64], PAR[:, l, 3, :], IDENT[0:64, 0:64]) for l in range(NL)],
                    [(SWA[:, :, LEVELS * CH + LC:SWC], b[:, 0:256].rearrange("p (l c) -> p l c", l=NL))], -1)
            power = [PAR[:, l, 0, 0:64] for l in range(NL)]
            m = 1
            while m < LC + 1:
                w = min(m, LC + 1 - m)
                for l in range(NL):
                    for q in range(0, w, 7):
                        n = min(7, w - q)
                        b = bank(len(prep))
                        o = b[0:64, 0:n * QB].rearrange("p (q c) -> p q c", q=n)
                        step = product([(o, power[l], Q[:, l, q:q + n, :])],
                                       [(Q[:, l, m + q:m + q + n, :], o)], last)
                if 2 * m < LC + 1:
                    b = bank(len(prep))
                    turn = (m.bit_length()) % 2
                    step = product([(b[0:64, 64 * l:64 * l + 64], Q[:, l, m, 0:64], power[l]) for l in range(NL)],
                                   [(PN[:, turn, :, :], b[0:64, 0:256].rearrange("p (l c) -> p l c", l=NL))], step)
                    power = [PN[:, turn, l, :] for l in range(NL)]
                last = step
                m *= 2
            for l in range(NL):
                for q in range(0, LC, 7):
                    b = bank(len(prep))
                    o = b[:, 0:7 * QB].rearrange("p (q c) -> p q c", q=7)
                    product([(o, PAR[:, l, 1, :], Q[:, l, q:q + 7, :])], [(R[:, l, q:q + 7, :], o)], last)
            b = bank(len(prep))
            product([(b[:, LC * l:LC * l + LC], II[:, :], Q[:, l, 0:LC, 64]) for l in range(NL)],
                    [(SWA[:, :, LEVELS * CH:LEVELS * CH + LC], b[:, 0:NL * LC].rearrange("p (l c) -> p l c", l=NL))], last)
            b = bank(len(prep))
            last = product([(b[0:64, 128 * l:128 * l + 128], Q[:, l, LC, 0:64], II[:, :]) for l in range(NL)],
                           [(PNN[:, :, :], b[0:64, :].rearrange("p (l c) -> p l c", l=NL))], last)
            b = bank(len(prep))
            last = product([(b[:, 64 * l:64 * l + 64], II[:, :], Q[:, l, LC, 0:64]) for l in range(NL)],
                           [(SWA[:, :, 0:64], b[:, 0:256].rearrange("p (l c) -> p l c", l=NL))], last)
            for r in range(1, LEVELS):
                b = bank(len(prep))
                nxt = product([(b[:, 64 * l:64 * l + 64], PNN[:, l, :], SWA[0:64, l, 64 * r - 64:64 * r]) for l in range(NL)],
                              [(SWA[:, :, 64 * r:64 * r + 64], b[:, 0:256].rearrange("p (l c) -> p l c", l=NL))], last)
                if r < LEVELS - 1:
                    b = bank(len(prep))
                    last = product([(b[0:64, 128 * l:128 * l + 128], SWA[0:64, l, 64 * r - 64:64 * r], PNN[:, l, :]) for l in range(NL)],
                                   [(PNN[:, :, :], b[0:64, :].rearrange("p (l c) -> p l c", l=NL))], nxt)
                else:
                    last = nxt

        build_prep()
        NPREP = len(prep)

        x_v = x.rearrange("b c (g i) w -> b (c g) (i w)", i=8)
        out_v = out.rearrange("b (k p) c -> p k b c", p=TT)

        loads = [
            (IDENT[:, :], c_ident), (II[:, 0:64], c_ident[0:64, 0:64]), (II[:, 64:128], c_ident[0:64, 0:64]),
            (SUMM[:, :], c_sum), (POS[0:64, :], c_pos), (POS[64:128, :], c_pos), (DIG[:, :], c_digit),
            (BROW[:, 0, :], b_tok.partition_broadcast(TT)), (BROW[:, 1, :], b_in.partition_broadcast(TT)),
            (BROW[:, 2, :], b_out.partition_broadcast(TT)), (BROW[:, 3, :], b2.partition_broadcast(TT)),
            (BIAS[:, 8:9], br.partition_broadcast(128)),
            (WIO[:, 0, 0:64], w_in), (WIO[:, 0, 64:128], w_in), (WIO[:, 1, 0:64], w_out), (WIO[:, 1, 64:128], w_out),
        ]
        for a in range(2):
            s = slice(64 * a, 64 * a + 64)
            loads += [
                (BIAS[s, 0:1], b_embed.unsqueeze(1)), (BIAS[s, 1:4], b_gcn.rearrange("l c -> c l")),
                (BIAS[s, 4:8], b1.rearrange("(q c) -> c q", c=64)),
                (WE[s, :, s], w_embed.rearrange("(c q) m -> q c m", c=3)),
                (WG[s, :, s], w_gcn.rearrange("l c m -> c l m")),
                (WL[s, 0, s], w_tok),
            ]
        sel_f = SF
        tri_f = IOTA[0:TT, 512:512 + 2 * TT]

        @block.sync
        def _(sp):
            for l in range(NL):
                sp.dma_start(PAR[:, l, 0, 0:64], A[l]).then_inc(par_in, 16)
                sp.dma_start(PAR[:, l, 1, 0:64], B[l]).then_inc(par_in, 16)
                sp.dma_start(PAR[:, l, 1, 64:128], B[l]).then_inc(par_in, 16)
                sp.dma_start(PAR[:, l, 2, 0:64], C[l]).then_inc(par_in, 16)
                sp.dma_start(PAR[:, l, 3, 0:64], D[l]).then_inc(par_in, 16)
                sp.dma_start(PAR[:, l, 3, 64:128], D[l]).then_inc(par_in, 16)
                sp.dma_start(Q[:, l, 0, 0:64], c_ident[0:64, 0:64]).then_inc(par_in, 16)
            sp.dma_start(EI[:, :, :], edges.rearrange("s (p j) -> p s j", p=EP)).then_inc(edge_in, 16)
            sp.dma_start(sel_f[0:24, :], c_sel).then_inc(edge_in, 16)
            sp.dma_start(tri_f[:, 0:TT], c_tri).then_inc(edge_in, 16)
            for i in range(2):
                for a in range(2):
                    sp.dma_start(XIN[:, i, a * 1792:a * 1792 + 1792], x_v[2 * i + a]).then_inc(x_in[i], 16)
            sp.wait_ge(zeroed, 1)
            for dst, src in loads:
                sp.dma_start(dst, src, allow_slow_non_contiguous=True).then_inc(wts_in, 16)
            for g in range(2, NP):
                sp.wait_ge(x_perm, g - 1)
                for a in range(2):
                    sp.dma_start(XIN[:, g % 2, a * 1792:a * 1792 + 1792], x_v[2 * g + a]).then_inc(x_in[g % 2], 16)
            for l in range(NL):
                for h in range(2):
                    sp.wait_ge(z_split, 2 * l + h + 1)
                    if l > 0:
                        sp.wait_ge(tok_mm, (1 + l) * UNITS + (h + 1) * NT)
                    for part in range(3):
                        for a in range(2):
                            dst = Z3[8 * part + a:8 * part + 8:2, h, :].rearrange("g (c j) -> g c j", j=LC)
                            sp.dma_start(dst, ZB[:, part, LC * a:LC * a + LC]).then_inc(z_in, 16)
            sp.wait_ge(zeroed, 3)
            for a in range(2):
                s = slice(64 * a, 64 * a + 64)
                sp.dma_start(W1[s, :, s], w1.rearrange("c (q m) -> c q m", m=64)).then_inc(mlp_in, 16)
                sp.dma_start(W2[s, :, s], w2.rearrange("(q c) m -> c q m", c=64)).then_inc(mlp_in, 16)
                for g in range(NP):
                    sp.dma_start(WR[s, g, 2 * g + a:128:16], wr.broadcast_to([64, 8]),
                                 allow_slow_non_contiguous=True).then_inc(mlp_in, 16)
            for g in range(NP):
                sp.wait_ge(y_ev, 2 * g + 2)
                for a in range(2):
                    sp.dma_start(out_v[:, :, 2 * g + a, :], T[:, :, 2 * g + a, :]).then_inc(stored, 16)
            sp.wait_ge(stored, 16 * NB)

        NLOADS = len(loads)
        NMLP = NB + 4

        def unit(k, h):
            return k, slice(8 * h, 8 * h + 8)

        @block.tensor
        def _(pe):
            mm = nc.tensor.matmul
            SXF = SX[:, :, :].rearrange("p g c -> p (g c)")

            pe.wait_ge(par_in, 16 * 7 * NL)
            pe.wait_ge(wts_in, 16 * NLOADS)
            pe.wait_ge(zeroed, 2)
            for n, (mms, _, after) in enumerate(prep):
                need = max(after, n - 8)
                if need >= 0:
                    pe.wait_ge(pre_ev, need + 1)
                for o, lhsT, rhs in mms:
                    last = mm(o, lhsT, rhs, start=True, stop=True)
                last.then_inc(pre_mm, 1)
            pe.wait_ge(pre_ev, NPREP)

            pe.wait_ge(eye_set, 3)
            for s in range(2):
                if s:
                    pe.wait_ge(adj_ev, NT)
                for k in range(NT):
                    w0 = N - TT * k + HN * s
                    last = mm(PS[0:TT, k, 0:HN], EYEW[:, N:N + TT], EYEW[:, w0:w0 + HN], start=True, stop=True)
                if s == 0:
                    last.then_inc(hot_mm, 2)
                with nc.tensor.Fori(0, EC // 2) as c:
                    for j in range(2):
                        pe.wait_ge(hot, c * 2 + (s * EC + j + 1))
                        for k in range(NT):
                            last = mm(PS[0:TT, k, 0:HN], OSRC[:, j, TT * k:TT * k + TT], ODST[:, j, :],
                                      start=False, stop=True, skip_group_check=True)
                        last.then_inc(hot_mm, 1)
            pe.wait_ge(adj_ev, 2 * NT)
            for k in range(NT):
                for j in range(NT):
                    last = mm(PS[0:TT, 0, k:k + 1], ADJ[:, j, TT * k:TT * k + TT], ONES[0:TT, 0:1],
                              start=(j == 0), stop=(j == NT - 1))
            last.then_inc(deg_mm, 1)
            pe.wait_ge(eye_set, 4)
            for k in range(NT):
                last = mm(PS[:, 1 + k // 4, TT * (k % 4):TT * (k % 4) + TT], ONES[0:TT, 0:128], DIAG[:, k, :],
                          start=True, stop=True)
                if k == 0:
                    last.then_inc(emb_mm, 2)
            last.then_inc(deg_mm, 1)
            pe.wait_ge(eye_set, 5)

            def embed_pair(i, s):
                pe.wait_ge(x_perm, i * 2 + s + 1)
                for half in range(2):
                    for q in range(3):
                        for t in range(5 if q < 2 else 4):
                            col = 14 * half + 5 * q + t
                            last = nc.tensor.transpose(PS[:, q, 84 * t:84 * t + 84], XP[:, s, col, :], IDENT[0:84, 0:84])
                        last.then_inc(emb_t, 1)
                    pe.wait_ge(emb_tv, i * 8 + 4 * s + 2 * half + 2)
                    pe.wait_ge(emb_tw, i * 4 + 2 * s + half + 1)
                    e = 2 * s + half
                    pe.wait_ge(emb_ev, i * 4 + (e + 1))
                    for c in range(3):
                        last = mm(PS[:, 4 + e % 2, 0:HN], WE[:, c, :], XT[:, half, c, :, :],
                                  start=(c == 0), stop=(c == 2))
                    last.then_inc(emb_mm, 1)

            with nc.tensor.Fori(0, NP // 2) as i:
                embed_pair(i, 0)
                embed_pair(i, 1)

            for l in range(NG):
                for h in range(2):
                    if l == 0:
                        pe.wait_ge(emb_ev, 2 * NP + 2)
                    else:
                        pe.wait_ge(h_ready, (l - 1) * NP + HP * (h + 1))
                    for k in range(NT):
                        n = l * UNITS + h * NT + k
                        if n >= 2:
                            pe.wait_ge(hw_ev, n - 1)
                        for g in range(HP):
                            last = mm(PS[0:TT, n % 2, 128 * g:128 * g + 128], UC[:, HP * h + g, TT * k:TT * k + TT],
                                      WG[:, l, :], start=True, stop=True)
                        last.then_inc(hw_mm, 1)
                for g in range(NP):
                    n = l * NP + g
                    pe.wait_ge(hw_ev, l * UNITS + (g // HP + 1) * NT)
                    if n >= 2:
                        pe.wait_ge(agg_sc, n - 1)
                    for s in range(2):
                        for k in range(NT):
                            last = mm(PS[:, 4 + 2 * (n % 2) + s, 0:HN], HW[:, k, g, :], ADJ[:, k, HN * s:HN * s + HN],
                                      start=(k == 0), stop=(k == NT - 1))
                    last.then_inc(agg_mm, 1)

            def tok_stage(s, w, ready):
                for h in range(2):
                    for k in range(NT):
                        n = s * UNITS + h * NT + k
                        ready(h, k)
                        if n >= 2:
                            pe.wait_ge(tok_ev, n - 1)
                        for g in range(HP):
                            last = mm(PS[0:TT, n % 2, 128 * g:128 * g + 128], UC[:, HP * h + g, TT * k:TT * k + TT],
                                      w, start=True, stop=True)
                        last.then_inc(tok_mm, 1)

            def transposes(r, h):
                for k in range(NT):
                    n = r * UNITS + h * NT + k
                    if r == 1:
                        pe.wait_ge(tok_ev, n + 1)
                    else:
                        pe.wait_ge(t_ready, (n - UNITS if r else n) + 1)
                    if not isinstance(n, int) or n >= 2:
                        pe.wait_ge(uc_ready, n - 1)
                    for g in range(HP):
                        last = nc.tensor.transpose(PS[:, 2 + (h * NT + k) % 2, TT * g:TT * g + TT],
                                                   T[:, k, 8 * h + 2 * g:8 * h + 2 * g + 2, :], IDENT[0:TT, 0:TT])
                    last.then_inc(tp_mm, 1)

            tok_stage(0, WL[:, 0, :], lambda h, k: pe.wait_ge(h_ready, (NG - 1) * NP + HP * (h + 1)))
            for h in range(2):
                transposes(0, h)
            tok_stage(1, WL[:, 1, :], lambda h, k: pe.wait_ge(uc_ready, h * NT + k + 1))
            for h in range(2):
                transposes(1, h)

            def mixer_half(l, h):
                pe.wait_ge(uc_ready, (l + 1) * UNITS + (h + 1) * NT)
                pe.wait_ge(staged, l + 1)
                if not isinstance(l, int) or l > 0:
                    pe.wait_ge(z_ev, 2 * l + h - 1)
                for p in range(LC):
                    last = mm(PS[0:TT, 4 + h, 0:2 * ZW], UCF[:, HP * N * h + LC - 1 - p:HP * N * (h + 1):LC], RW[:, :, p, :],
                              start=(p == 0), stop=(p == LC - 1))
                last.then_inc(conv_mm, 1)
                pe.wait_ge(es_ev, 2 * l + h + 1)
                m0 = 6 * (2 * l + h)
                if not isinstance(l, int) or l > 0 or h > 0:
                    pe.wait_ge(scan_ev, m0)
                nc.tensor.transpose(PS[:, 6, 0:TT], ES[:, :], IDENT[0:TT, 0:TT]).then_inc(scan_mm, 1)
                for r in range(LEVELS):
                    sh = 1 << r
                    pe.wait_ge(scan_ev, m0 + r + 1)
                    o = PS[:, 6 + (r + 1) % 2, 0:TT].rearrange("p (g c) -> p g c", g=HP)
                    mm(o, IDENT[:, :], SC[:, r % 2, :, 1:LC + 1], start=True, stop=True)
                    mm(o[:, :, sh:LC], SWS[:, r, :], SC[:, r % 2, :, 1:LC + 1 - sh],
                       start=False, stop=True, skip_group_check=True).then_inc(scan_mm, 1)
                pe.wait_ge(scan_ev, m0 + 6)
                for a in range(2):
                    last = mm(PS[0:TT, 4 + h, ZW * a:ZW * a + LC], SXF,
                              SW[:, a, 0:LC], start=False, stop=True, skip_group_check=True)
                last.then_inc(z_mm, 1)
                pe.wait_ge(z_in, 96 * (2 * l + h + 1))
                for k in range(NT):
                    n = (2 + l) * UNITS + h * NT + k
                    pe.wait_ge(tok_ev, n - 1)
                    b = PS[0:TT, (h * NT + k) % 2, :]
                    mm(b, Z3[:, h, TT * k:TT * k + TT], SELF[:, :], start=True, stop=True)
                    for g in range(HP):
                        last = mm(b[:, 128 * g:128 * g + 128], UC[:, HP * h + g, TT * k:TT * k + TT],
                                  SW[:, :, LC:LC + CH], start=False, stop=True, skip_group_check=True)
                    last.then_inc(tok_mm, 1)

            for l in range(NL):
                mixer_half(l, 0)
                if l > 0:
                    transposes(l + 1, 1)
                mixer_half(l, 1)
                transposes(l + 2, 0)
            transposes(NL + 1, 1)
            tok_stage(6, WL[:, 2, :], lambda h, k: pe.wait_ge(uc_ready, 5 * UNITS + h * NT + k + 1))
            for h in range(2):
                transposes(6, h)

            pe.wait_ge(uc_ready, 7 * UNITS)
            pe.wait_ge(mlp_in, 16 * NMLP)
            for s in range(2):
                for g in range(NP):
                    last = mm(PS[:, 4 + s, 0:HN], WR[:, g, :], UC[:, g, HN * s:HN * s + HN],
                              start=(g == 0), stop=(g == NP - 1))
            last.then_inc(r_mm, 1)

            def radix(r):
                pe.wait_ge(cnt_rd, r + 1)
                mm(PS[:, 6, 0:1], SUMM[:, 0:128], CNT[:, 1:2], start=True, stop=True).then_inc(rad_mm, 1)

            def mlp_pair(g):
                for q in range(4):
                    for s in range(2):
                        n = 8 * g + 2 * q + s
                        if n >= 2:
                            pe.wait_ge(f_ev, n - 1)
                        mm(PS[:, n % 2, 0:HN], W1[:, q, :], UC[:, g, HN * s:HN * s + HN],
                           start=True, stop=True).then_inc(f_mm, 1)
                for s in range(2):
                    n = 2 * g + s
                    pe.wait_ge(f_ev, 8 * g + 8)
                    if n >= 2:
                        pe.wait_ge(y_ev, n - 1)
                    for k in range(4 * s, min(4 * s + 4, NT)):
                        for q in range(4):
                            last = mm(PS[0:TT, 2 + s, 128 * (k - 4 * s):128 * (k - 4 * s) + 128],
                                      HID[:, g % 2, q, TT * k:TT * k + TT], W2[:, q, :], start=(q == 0), stop=(q == 3))
                    last.then_inc(y_mm, 1)

            for r in range(len(RADIX)):
                radix(r)
            pe.wait_ge(msk_rd, 1)
            for v, row in enumerate((WROW[0:NB, :], GTR, EQR)):
                for k in range(NT):
                    last = nc.tensor.transpose(PS[0:TT, 4 + v, NB * k:NB * k + NB], row[:, TT * k:TT * k + TT],
                                               IDENT[0:NB, 0:NB])
            last.then_inc(msk_mm, 1)
            pe.wait_ge(msk_rd, 2)
            o = PS[0:TT, 7, 0:NT * NB].rearrange("p (k b) -> p k b", k=NT)
            mm(o, TRI[:, 0:TT], GEB[:, 1, :, :], start=True, stop=True)
            for k in range(NT - 1):
                mm(o[:, k + 1:NT, :], TRI[:, TT:2 * TT],
                   GEB[:, 1, k:k + 1, :].broadcast_to([TT, NT - 1 - k, NB]), start=False, stop=True, skip_group_check=True)
            mm(o, TRI[:, TT:2 * TT], GSB[:, :].unsqueeze(1).broadcast_to([TT, NT, NB]), start=False, stop=True,
               skip_group_check=True).then_inc(msk_mm, 1)
            for g in range(NP):
                mlp_pair(g)

        @block.scalar
        def _(act):
            with nc.scalar.Fori(0, NP // 2) as i:
                for s in range(2):
                    for half in range(2):
                        act.wait_ge(emb_mm, i * 4 + (2 * s + half + 1))
                        for q in (0, 2):
                            act.wait_ge(emb_t, i * 12 + 6 * s + 3 * half + q + 1)
                            n = 5 if q < 2 else 4
                            dst = XT[:, half, :, 5 * q:5 * q + n, :]
                            src = PS[:, q, 0:84 * n].rearrange("p (g c i) -> p c g i", g=n, c=3)
                            nc.scalar.copy(dst, src).then_inc(emb_tv, 1)
            for l in range(NG):
                for g in range(NP):
                    n = l * NP + g
                    act.wait_ge(agg_sc, n + 1)
                    nc.scalar.activation(UC[:, g, :], AGG[:, n % 2, :], ACT.Relu,
                                         bias=BIAS[:, 1 + l:2 + l]).then_inc(h_ready, 1)

            def to_uc(r, h):
                for k in range(NT):
                    n = r * UNITS + h * NT + k
                    act.wait_ge(tp_mm, n + 1)
                    nc.scalar.copy(UC[:, HP * h:HP * h + HP, TT * k:TT * k + TT],
                                   PS[:, 2 + (h * NT + k) % 2, 0:HP * TT].rearrange("p (g t) -> p g t", g=HP))\
                        .then_inc(uc_ready, 1)

            for r in range(2):
                for h in range(2):
                    to_uc(r, h)

            def mixer_half(l, h):
                act.wait_ge(conv_mm, 2 * l + h + 1)
                if not isinstance(l, int) or l > 0 or h > 0:
                    act.wait_ge(scan_mm, 6 * (2 * l + h))
                nc.scalar.copy(ES[:, :].rearrange("p (a c) -> p a c", a=2),
                               PS[0:TT, 4 + h, 0:2 * ZW].rearrange("p (a z) -> p a z", a=2)[:, :, LC:ZW]).then_inc(es_ev, 1)
                m0 = 6 * (2 * l + h)
                for r in range(6):
                    act.wait_ge(scan_mm, m0 + r + 1)
                    if r < 2:
                        act.wait_ge(zeroed, 2)
                        if not isinstance(l, int) or l > 0 or h > 0:
                            act.wait_ge(z_mm, 2 * l + h)
                    src = PS[:, 6 + r % 2, 0:TT].rearrange("p (g c) -> p g c", g=HP)
                    if r < LEVELS:
                        nc.scalar.copy(SC[:, r % 2, :, 1:LC + 1], src).then_inc(scan_ev, 1)
                    else:
                        nc.scalar.copy(SX[:, :, 1:LC], src[:, :, 0:LC - 1]).then_inc(scan_ev, 1)
                act.wait_ge(z_mm, 2 * l + h + 1)
                if not isinstance(l, int) or l > 0 or h > 0:
                    act.wait_ge(z_split, 2 * l + h)
                nc.scalar.copy(ZF[:, 0, :].rearrange("p (a j) -> p a j", a=2),
                               PS[0:TT, 4 + h, 0:2 * ZW].rearrange("p (a z) -> p a z", a=2)[:, :, 0:LC]).then_inc(z_ev, 1)
                for k in range(NT):
                    n = (2 + l) * UNITS + h * NT + k
                    u = l * UNITS + h * NT + k
                    act.wait_ge(tok_mm, n + 1)
                    if not isinstance(l, int) or u >= 2:
                        act.wait_ge(gel_used, u - 1)
                    nc.scalar.activation(GEL[:, (h * NT + k) % 2, :], PS[0:TT, (h * NT + k) % 2, :], ACT.Gelu).then_inc(tok_ev, 1)

            for l in range(NL):
                mixer_half(l, 0)
                if l > 0:
                    to_uc(l + 1, 1)
                mixer_half(l, 1)
                to_uc(l + 2, 0)
            to_uc(NL + 1, 1)
            for h in range(2):
                to_uc(6, h)
            for g in range(NP):
                if g >= 2:
                    act.wait_ge(y_mm, 2 * g - 2)
                for q in range(4):
                    for s in range(2):
                        n = 8 * g + 2 * q + s
                        act.wait_ge(f_mm, n + 1)
                        nc.scalar.activation(HID[:, g % 2, q, HN * s:HN * s + HN], PS[:, n % 2, 0:HN],
                                             ACT.Gelu_apprx_tanh, bias=BIAS[:, 4 + q:5 + q]).then_inc(f_ev, 1)

        @block.gpsimd
        def _(pool):
            chain = [0]

            def link(ins):
                chain[0] += 1
                ins.then_inc(pool_ch, 1)
                pool.wait_ge(pool_ch, chain[0])

            g_ = nc.gpsimd
            for buf in (WE, WG, WL):
                link(g_.memset(buf[:], 0.0))
            g_.memset(ONES[:, 0:128], 1.0)
            link(g_.memset(BIAS[:, :], 0.0))
            g_.memset(ONES[:, 128:129], 1.0 / CH).then_inc(zeroed, 1)
            g_.memset(SW[:, :, :], 0.0)
            g_.memset(SWS[:, :, :], 0.0)
            g_.memset(SX[:, :, :], 0.0)
            g_.memset(SC[:, :, :, :], 0.0).then_inc(zeroed, 1)
            link(g_.memset(EYEW[:, :], 0.0))
            link(g_.affine_select(out=EYEW[:, :], in_=EYEW[:, :], compare_op=ALU.not_equal, fill=1.0, base=N,
                             pattern=[[-1, 2 * N]], channel_multiplier=1))
            pool.wait_ge(edge_in, 48)
            link(g_.tensor_copy(SELF[:, :], sel_f[0:24, :]))
            link(g_.tensor_copy(TRI[:, 0:TT], tri_f[:, 0:TT]))
            link(g_.memset(TRI[:, TT:2 * TT], 1.0))
            link(g_.iota(IOTA[:, :], pattern=[[1, N]], base=0, channel_multiplier=0,
                         allow_small_or_imprecise_dtypes=True))
            g_.memset(GSUM[:, :], 0.0).then_inc(eye_set, 2)

            for g in range(NP):
                pool.wait_ge(x_in[g % 2], 32 * (g // 2 + 1))
                if g == 0:
                    pool.wait_ge(pre_ev, NPREP)
                    pool.wait_ge(pre_mm, NPREP)
                if g >= 2:
                    pool.wait_ge(emb_t, 6 * (g - 1))
                g_.tensor_copy(XP[:, g % 2, :, :].rearrange("p g (a j) -> p g a j", a=16),
                               XIN[:, g % 2, :].rearrange("p (a g j) -> p g a j", a=16, g=GRID)).then_inc(x_perm, 1)

            def stage(l):
                for a in range(2):
                    s = slice(64 * a, 64 * a + 64)
                    g_.tensor_copy(SWS[s, :, s], SWA[s, l, 0:LEVELS * CH].rearrange("p (r c) -> p r c", r=LEVELS))
                    link(g_.tensor_copy(SW[s, a, :], SWA[s, l, LEVELS * CH:SWC]))
                    flat = RW[s, a, :, :].rearrange("p q z -> p (q z)")
                    diag = bass.AP(tensor=flat.tensor, offset=flat.offset + LC, ap=[list(flat.ap[0]), [ZW - 1, LC], [1, LC]])
                    link(g_.tensor_copy(diag, R[s, l, :, CH].unsqueeze(1).broadcast_to([64, LC, LC])))
                    ins = g_.tensor_copy(RW[s, a, :, LC:ZW], R[s, l, :, 0:CH])
                    if a == 0:
                        link(ins)
                ins.then_inc(staged, 1)
                pool.wait_ge(staged, l + 1)

            pool.wait_ge(agg_mm, NG * NP)
            link(g_.memset(RW[:, :, :, :], 0.0))
            pool.wait_ge(pre_ev, NPREP)
            stage(0)
            for h in range(2):
                pool.wait_ge(t_ready, (h + 1) * NT)
                rv = RES[:, :, 8 * h:8 * h + 8, :]
                for k in range(NT):
                    ins = g_.tensor_tensor(rv[:, k], rv[:, k], BROW[:, 2, :].unsqueeze(1).broadcast_to([TT, 8, CH]), ALU.add)
                ins.then_inc(res_b, 1)
            for l in range(NL):
                for h in range(2):
                    pool.wait_ge(z_ev, 2 * l + h + 1)
                    if l > 0 or h > 0:
                        pool.wait_ge(z_in, 96 * (2 * l + h))
                    link(g_.tensor_copy(ZB[:, 0, :], ZF[:, 0, :]))
                    link(g_.tensor_tensor(ZF[:, 1, :], ZF[:, 0, :], ZB[:, 0, :], ALU.subtract))
                    link(g_.tensor_copy(ZB[:, 1, :], ZF[:, 1, :]))
                    g_.tensor_tensor(ZB[:, 2, :], ZF[:, 1, :], ZB[:, 1, :], ALU.subtract).then_inc(z_split, 1)
                    for k in range(NT):
                        u = l * UNITS + h * NT + k
                        pool.wait_ge(tok_ev, 2 * UNITS + u + 1)
                        tv = T[:, k, 8 * h:8 * h + 8, :]
                        g_.tensor_tensor(tv, tv, GEL[:, (h * NT + k) % 2, :].rearrange("p (b c) -> p b c", b=8),
                                         ALU.add).then_inc(gel_used, 1)
                if l + 1 < NL:
                    pool.wait_ge(tok_mm, (3 + l) * UNITS)
                    stage(l + 1)
                    if l + 2 == NL:
                        g_.memset(RF[:, 0:2048], 0.0).then_inc(zeroed, 1)
            for h in range(2):
                pool.wait_ge(t_ready, 5 * UNITS + (h + 1) * NT)
                for k in range(NT):
                    rv = RES[:, k, 8 * h:8 * h + 8, :]
                    ins = g_.tensor_tensor(rv, rv, T[:, k, 8 * h:8 * h + 8, :], ALU.add)
                ins.then_inc(res_b, 1)

        @block.vector
        def _(dve):
            chain = [0]
            v_ = nc.vector

            def link(ins):
                chain[0] += 1
                ins.then_inc(dve_ch, 1)
                dve.wait_ge(dve_ch, chain[0])

            def rsqrt(v, y, t):
                link(v_.tensor_scalar(t.bitcast(I32), v.bitcast(I32), 1, None, ALU.logical_shift_right))
                link(v_.tensor_scalar(y.bitcast(I32), t.bitcast(I32), -1.0, float(0x5f3759df), ALU.mult, ALU.add))
                for _ in range(3):
                    link(v_.scalar_tensor_tensor(out=t, in0=y, scalar=-0.5, in1=y, op0=ALU.mult, op1=ALU.mult))
                    link(v_.tensor_tensor(t, t, v, ALU.mult))
                    link(v_.scalar_tensor_tensor(out=y, in0=t, scalar=1.5, in1=y, op0=ALU.add, op1=ALU.mult))

            for n, (_, copies, _) in enumerate(prep):
                dve.wait_ge(pre_mm, n + 1)
                for dst, src in copies:
                    ins = v_.tensor_copy(dst, src)
                ins.then_inc(pre_ev, 1)

            dve.wait_ge(edge_in, 48)
            v_.tensor_copy(EF[:, :, :], EI[:, :, :]).then_inc(eye_set, 1)
            dve.wait_ge(eye_set, 3)
            for s in range(2):
                with nc.vector.Fori(0, EC // 2) as c:
                    for j in range(2):
                        dve.wait_ge(hot_mm, c * 2 + (s * EC + j + 1))
                        v_.tensor_scalar(OSRC[:, j, :], IOTA[0:EP, :], EF[:, 0, bass.ds(c * 2 + j, 1)], None, ALU.is_equal)
                        v_.tensor_scalar(ODST[:, j, :], IOTA[0:EP, HN * s:HN * s + HN], EF[:, 1, bass.ds(c * 2 + j, 1)], None,
                                         ALU.is_equal).then_inc(hot, 1)
                dve.wait_ge(hot_mm, (s + 1) * EC + 2)
                for k in range(NT):
                    v_.tensor_copy(ADJ[:, k, HN * s:HN * s + HN], PS[0:TT, k, 0:HN]).then_inc(adj_ev, 1)
            dve.wait_ge(deg_mm, 1)
            link(v_.tensor_copy(DG[:, 0, :], PS[0:TT, 0, 0:NT]))
            rsqrt(DG[:, 0, :], DG[:, 1, :], DG[:, 2, :])
            for k in range(NT):
                ins = v_.tensor_scalar(DIAG[:, k, :], IDENT[0:TT, 0:TT], DG[:, 1, k:k + 1], None, ALU.mult)
            ins.then_inc(eye_set, 1)
            dve.wait_ge(deg_mm, 2)
            v_.tensor_copy(DROW[:, 0:4 * TT], PS[:, 1, 0:4 * TT]).then_inc(emb_ev, 2)
            v_.tensor_copy(DROW[:, 4 * TT:N], PS[:, 2, 0:3 * TT]).then_inc(eye_set, 1)

            with nc.vector.Fori(0, NP // 2) as i:
                for s in range(2):
                    for half in range(2):
                        e = 2 * s + half
                        dve.wait_ge(emb_mm, i * 4 + (e + 1))
                        dve.wait_ge(emb_t, i * 12 + 6 * s + 3 * half + 2)
                        v_.tensor_copy(XT[:, half, :, 5:10, :],
                                       PS[:, 1, 0:420].rearrange("p (g c i) -> p c g i", g=5, c=3)).then_inc(emb_tw, 1)
                        dve.wait_ge(emb_mm, i * 4 + (e + 3))
                        dst = UC[:, bass.ds(i * 2 + s, 1), :].rearrange("p a (i g) -> p (a g) i", i=GRID)[:, 14 * half:14 * half + 14, :]
                        pos = POS[:, :].rearrange("p (i g) -> p g i", i=GRID)[:, 14 * half:14 * half + 14, :]
                        src = PS[:, 4 + e % 2, 0:HN].rearrange("p (g i) -> p g i", g=14)
                        v_.scalar_tensor_tensor(out=dst, in0=src, scalar=BIAS[:, 0:1], in1=pos, op0=ALU.add,
                                                op1=ALU.add).then_inc(emb_ev, 1)

            for l in range(NG):
                for h in range(2):
                    for k in range(NT):
                        n = l * UNITS + h * NT + k
                        dve.wait_ge(hw_mm, n + 1)
                        if h == 0 and k == 0 and l > 0:
                            dve.wait_ge(agg_mm, l * NP)
                        v_.tensor_scalar(HW[:, k, HP * h:HP * h + HP, :].rearrange("p g m -> p (g m)"), PS[0:TT, n % 2, :],
                                         DG[:, 1, k:k + 1], None, ALU.mult).then_inc(hw_ev, 1)
                for g in range(NP):
                    n = l * NP + g
                    dve.wait_ge(agg_mm, n + 1)
                    if n >= 2:
                        dve.wait_ge(h_ready, n - 1)
                    b0 = 4 + 2 * (n % 2)
                    v_.tensor_tensor(AGG[:, n % 2, :].rearrange("p (s j) -> p s j", s=2), PS[:, b0:b0 + 2, 0:HN],
                                     DROW[:, :].rearrange("p (s j) -> p s j", s=2), ALU.mult).then_inc(agg_sc, 1)

            def norm(h, src, ready, done):
                for k in range(NT):
                    ready(h, k)
                    for b in range(8):
                        ins = v_.bn_stats(ST[:, h, 8 * k + b, :], src[:, k, 8 * h + b, :])
                link(ins)
                me, mo = ST[:, h, :, 1], ST[:, h, :, 4]
                m = MEAN[:, h, :]
                diff, var, tmp = LNS[:, 0, :], LNS[:, 1, :], LNS[:, 2, :]
                v_.tensor_tensor(diff, me, mo, ALU.subtract)
                v_.tensor_tensor(LNS[:, 3, :], me, mo, ALU.add)
                link(v_.tensor_tensor(var, ST[:, h, :, 2], ST[:, h, :, 5], ALU.add))
                v_.tensor_scalar(m, LNS[:, 3, :], 0.5, None, ALU.mult)
                v_.tensor_tensor(LNS[:, 4, :], diff, diff, ALU.mult)
                link(v_.tensor_scalar(tmp, var, 1.0 / CH, EPS, ALU.mult, ALU.add))
                link(v_.scalar_tensor_tensor(out=var, in0=LNS[:, 4, :], scalar=0.25, in1=tmp, op0=ALU.mult, op1=ALU.add))
                rsqrt(var, RSTD[:, h, :], tmp)
                for k in range(NT):
                    for b in range(8):
                        u = 8 * k + b
                        ins = v_.tensor_scalar(T[:, k, 8 * h + b, :], src[:, k, 8 * h + b, :], MEAN[:, h, u:u + 1],
                                               RSTD[:, h, u:u + 1], ALU.subtract, ALU.mult)
                    if done:
                        ins.then_inc(t_ready, 1)
                if not done:
                    link(ins)

            def row(j):
                return BROW[:, j, :].unsqueeze(1).broadcast_to([TT, 8, CH])

            none = lambda h, k: None
            for h in range(2):
                for k in range(NT):
                    n = h * NT + k
                    dve.wait_ge(tok_mm, n + 1)
                    v_.tensor_tensor(RES[:, k, 8 * h:8 * h + 8, :], PS[0:TT, n % 2, :].rearrange("p (b c) -> p b c", b=8),
                                     row(0), ALU.add).then_inc(tok_ev, 1)
            for h in range(2):
                norm(h, RES, lambda h, k: dve.wait_ge(tok_ev, h * NT + k + 1), True)
            for h in range(2):
                for k in range(NT):
                    n = UNITS + h * NT + k
                    dve.wait_ge(tok_mm, n + 1)
                    v_.tensor_tensor(T[:, k, 8 * h:8 * h + 8, :], PS[0:TT, n % 2, :].rearrange("p (b c) -> p b c", b=8),
                                     row(1), ALU.add).then_inc(tok_ev, 1)
            for l in range(NL):
                for h in range(2):
                    norm(h, T, lambda h, k: dve.wait_ge(gel_used, l * UNITS + h * NT + k + 1), l + 1 < NL)
                    if l + 1 == NL:
                        norm(h, T, none, True)
            for h in range(2):
                for k in range(NT):
                    n = 6 * UNITS + h * NT + k
                    dve.wait_ge(tok_mm, n + 1)
                    dve.wait_ge(res_b, h + 1)
                    rv = RES[:, k, 8 * h:8 * h + 8, :]
                    v_.tensor_tensor(rv, PS[0:TT, n % 2, :].rearrange("p (b c) -> p b c", b=8), rv, ALU.add).then_inc(tok_ev, 1)
            for h in range(2):
                norm(h, RES, lambda h, k: dve.wait_ge(tok_ev, 6 * UNITS + h * NT + k + 1), True)

            dve.wait_ge(r_mm, 1)
            link(v_.tensor_scalar(WROW.rearrange("p (s j) -> p s j", s=2), PS[:, 4:6, 0:HN], BIAS[:, 8:9], None, ALU.add))
            link(v_.memset(PREF[:, :], 0))
            for r, sh in enumerate(RADIX):
                tail = r == len(RADIX) - 1
                link(v_.tensor_tensor(KEY[:, 0:1], PREF[:, 0:1], DIG[:, r:r + 1], ALU.bitwise_or))
                link(v_.tensor_scalar(KEY[:, 1:2], KEY[:, 0:1], 31, -1, ALU.arith_shift_right, ALU.bitwise_xor))
                link(v_.tensor_scalar(KEY[:, 2:3], KEY[:, 1:2], -2147483648, None, ALU.bitwise_or))
                link(v_.tensor_tensor(KEY[:, 3:4], KEY[:, 2:3], KEY[:, 0:1], ALU.bitwise_xor))
                link(v_.tensor_scalar(JUNK, WROW, KEY[:, 3:4].bitcast(F32), 0.0, ALU.is_ge, ALU.add, accum_out=CNT[:, 0:1]))
                v_.tensor_scalar(CNT[:, 1:2], CNT[:, 0:1], SUMM[:, 128:129], 0.5 if tail else 1.0, ALU.is_ge, ALU.mult).then_inc(cnt_rd, 1)
                dve.wait_ge(rad_mm, r + 1)
                link(v_.tensor_scalar(PREF[:, 1:2], PS[:, 6, 0:1], -1.0, None, ALU.add))
                if sh:
                    link(v_.tensor_scalar(PREF[:, 1:2], PREF[:, 1:2], sh, None, ALU.logical_shift_left))
                link(v_.tensor_tensor(PREF[:, 0:1], PREF[:, 0:1], PREF[:, 1:2], ALU.bitwise_or))
            link(v_.tensor_scalar(KEY[:, 1:2], PREF[:, 0:1], 31, -1, ALU.arith_shift_right, ALU.bitwise_xor))
            link(v_.tensor_scalar(KEY[:, 2:3], KEY[:, 1:2], -2147483648, None, ALU.bitwise_or))
            link(v_.tensor_tensor(KEY[:, 3:4], KEY[:, 2:3], PREF[:, 0:1], ALU.bitwise_xor))
            thr = KEY[0:NB, 3:4].bitcast(F32)
            v_.tensor_scalar(GTR, WROW[0:NB, :], thr, None, ALU.is_gt)
            v_.tensor_scalar(EQR, WROW[0:NB, :], thr, None, ALU.is_equal).then_inc(msk_rd, 1)
            dve.wait_ge(msk_mm, 1)
            v_.tensor_copy(WTOK[:, :, :].rearrange("p k b -> p (k b)"), PS[0:TT, 4, 0:TT])
            v_.tensor_copy(GEB[:, 0, :, :].rearrange("p k b -> p (k b)"), PS[0:TT, 5, 0:TT])
            link(v_.tensor_copy(GEB[:, 1, :, :].rearrange("p k b -> p (k b)"), PS[0:TT, 6, 0:TT]))
            link(v_.tensor_reduce(GSUM[:, :], GEB[:, 0, :, :].rearrange("p k b -> p b k"), AX.X, ALU.add))
            v_.tensor_copy(GSB[:, :], GSUM[:, :]).then_inc(msk_rd, 1)
            dve.wait_ge(msk_mm, 2)
            few = YT[:, 0:TT].rearrange("p (k b) -> p k b", k=NT)
            o = PS[0:TT, 7, 0:NT * NB].rearrange("p (k b) -> p k b", k=NT)
            link(v_.scalar_tensor_tensor(out=few, in0=o, scalar=float(KK), in1=GEB[:, 1, :, :], op0=ALU.is_lt, op1=ALU.mult))
            link(v_.tensor_tensor(few, few, GEB[:, 0, :, :], ALU.add))
            link(v_.tensor_tensor(WM[:, :, :], few, WTOK[:, :, :], ALU.mult))

            for g in range(NP):
                for s in range(2):
                    nk = 4 if s == 0 else 3
                    dve.wait_ge(y_mm, 2 * g + s + 1)
                    if g == 0 and s == 0:
                        dve.wait_ge(res_b, 4)
                        dve.wait_ge(tp_mm, 7 * UNITS)
                    if g or s:
                        dve.wait_ge(y_ev, 2 * g + s)
                    src = PS[0:TT, 2 + s, 0:128 * nk].rearrange("p (k c) -> p k c", c=CH)
                    yt = YT[:, 0:128 * nk]
                    y3 = yt.rearrange("p (k c) -> p k c", c=CH)
                    link(v_.tensor_tensor(y3, src, BROW[:, 3, :].unsqueeze(1).broadcast_to([TT, 2 * nk, CH]), ALU.add))
                    y4 = yt.rearrange("p (k a c) -> p k a c", a=2, c=CH)
                    k0 = 4 * s
                    link(v_.tensor_tensor(y4, y4, WM[:, k0:k0 + nk, 2 * g:2 * g + 2].unsqueeze(3).broadcast_to([TT, nk, 2, CH]), ALU.mult))
                    v_.tensor_tensor(T[:, k0:k0 + nk, 2 * g:2 * g + 2, :], y4, RES[:, k0:k0 + nk, 2 * g:2 * g + 2, :],
                                     ALU.add).then_inc(y_ev, 1)


_INS = ["x", "L0_tok_W_embed", "L0_tok_b_embed", "L0_tok_W_gcn", "L0_tok_b_gcn", "L0_tok_W_out", "L0_tok_b_out",
        "L0_tok_edge_index", "L0_attn_Win", "L0_attn_bin_", "L0_attn_Wout", "L0_attn_bout", "L0_attn_A", "L0_attn_Bm",
        "L0_attn_Cm", "L0_attn_Dm", "L0_ffn_wr", "L0_ffn_br", "L0_ffn_w1", "L0_ffn_b1", "L0_ffn_w2", "L0_ffn_b2"]


def _shape_constants():
    import numpy as np
    pos = np.arange(N, dtype=np.float32)[:, None]
    div = np.exp(np.arange(0, CH, 2, dtype=np.float32) * np.float32(-np.log(10000.0) / CH)).astype(np.float32)
    ang = (pos * div).astype(np.float32).astype(np.float64)
    pe = np.zeros((N, CH), np.float32)
    pe[:, 0::2] = np.sin(ang)
    pe[:, 1::2] = np.cos(ang)
    sel = np.zeros((24, 512), np.float32)
    for r in range(24):
        sel[r, 64 * (r % 8):64 * (r % 8) + 64] = 1.0
    tri = np.triu(np.ones((TT, TT), np.float32), 1)
    same = np.equal(np.arange(128)[:, None] % NB, np.arange(128)[None, :] % NB).astype(np.float32)
    d = (np.arange(128) // NB).astype(np.int64)[:, None]
    digit = np.concatenate([(d << s if s else d & 3) for s in RADIX], 1)
    reach = np.where(d == 0, 0, KK).astype(np.float32)
    digit[:NB] = 0x00800000
    digit = (digit & 0xFFFFFFFF).astype(np.uint32).view(np.int32)
    same = np.concatenate([same, reach], 1)
    return {"ident": np.eye(128, dtype=np.float32), "sel": sel, "tri": tri, "sum": same,
            "pos": np.ascontiguousarray(pe.T), "digit": np.ascontiguousarray(digit)}


def kernel(**inputs):
    import numpy as np
    import concourse.bacc as bacc
    from concourse.bass_utils import run_bass_kernel_spmd

    nc = bacc.Bacc("TRN2", target_bir_lowering=False, num_devices=1)
    arrays, args = {}, []
    given = [(n, inputs[n]) for n in _INS] + list(_shape_constants().items())
    for name, value in given:
        a = np.ascontiguousarray(value)
        arrays[f"in_{name}"] = a
        args.append(nc.dram_tensor(f"in_{name}", a.shape, mybir.dt.from_np(a.dtype), kind="ExternalInput").ap())
    out = nc.dram_tensor("out_0", (NB, N, CH), F32, kind="ExternalOutput").ap()
    tower(nc, *args, out)
    r = run_bass_kernel_spmd(nc, [arrays], core_ids=[0])
    return r.results[0]["out_0"]
```

```python
from contextlib import ExitStack

import concourse.bass as bass
from concourse import mybir

F32 = mybir.dt.float32
BF16 = mybir.dt.bfloat16
I32 = mybir.dt.int32
ALU = mybir.AluOpType
ACT = mybir.ActivationFunctionType
AX = mybir.AxisListType

NB = 16
NP = NB // 2
HP = NP // 2
GRID = 28
N = GRID * GRID
TT = 112
NT = N // TT
HN = N // 2
CH = 64
LC = 28
NCH = N // LC
NG = 3
NL = 4
NE = 4 * GRID * (GRID - 1)
EC = 28
EP = NE // EC
ZW = LC + CH
QB = CH + 1
LEVELS = 5
SWC = LEVELS * CH + LC + CH
KK = N // 2 - 1
UNITS = 2 * NT
EPS = 1e-5
RADIX = [29, 26, 23, 20, 17, 14, 11, 8, 5, 2, 0]
BW = TT + 2 * GRID
YB0 = 2
HALVES = 2 * NP
GH = GRID // 2
SCAN = LEVELS + 2


def tower(nc, x, w_embed, b_embed, w_gcn, b_gcn, w_tok, b_tok, edges, w_in, b_in, w_out, b_out,
          A, B, C, D, wr, br, w1, b1, w2, b2,
          c_ident, c_sel, c_tri, c_sum, c_pos, c_digit, c_edges, c_band, c_deg, out):
    ctx = ExitStack()
    with ctx:
        def sb(name, shape, dt=F32):
            return ctx.enter_context(nc.sbuf_tensor(name, shape, dt))

        def sem(name):
            return ctx.enter_context(nc.semaphore(name))

        PS = ctx.enter_context(nc.psum_tensor("PS", [128, 8, 512], F32))

        TOK = NT * NB * CH
        UC = sb("UC", [128, NP, N])
        UCF = UC[:, :, :].rearrange("p g n -> p (g n)")
        BIG = sb("BIG", [128, 2 * TOK])
        T = BIG[0:TT, 0:TOK].rearrange("p (k b c) -> p k b c", k=NT, b=NB)
        RES = BIG[0:TT, TOK:].rearrange("p (k b c) -> p k b c", k=NT, b=NB)
        HW = BIG[0:TT, 0:TOK].rearrange("p (k g m) -> p k g m", k=NT, g=NP)
        XP = BIG[0:84, 0:7168].rearrange("p (s g q) -> p s g q", s=4, g=GH)
        IOTA = BIG[:, 0:N]
        EF = BIG[0:EP, N:N + 2 * EC].rearrange("p (s j) -> p s j", s=2)
        CM = sb("CM", [128, NT * N])
        ADJ = CM[0:TT, :].rearrange("p (k n) -> p k n", k=NT)
        RW = CM[:, 0:2 * LC * ZW].rearrange("p (a q z) -> p a q z", a=2, q=LC)
        QC = (LC + 1) * QB
        Q = [BIG[0:CH, TOK + QC * l:TOK + QC * l + QC].rearrange("p (q c) -> p q c", c=QB) for l in range(NL - 1)]
        Q.append(CM[0:CH, 3328:3328 + QC].rearrange("p (q c) -> p q c", c=QB))
        r0 = TOK + 3 * QC
        PNN = BIG[0:CH, r0:r0 + 512].rearrange("p (l c) -> p l c", l=NL)
        sel_f = BIG[0:24, r0 + 512:r0 + 1024]
        tri_f = BIG[0:TT, r0 + 1024:r0 + 1024 + TT]
        EI = BIG[0:EP, r0 + 1136:r0 + 1192].bitcast(I32)
        EC_GRID = BIG[0:EP, r0 + 1192:r0 + 1248].bitcast(I32)
        PAR = CM[0:CH, 0:2048].rearrange("p (m l c) -> p m l c", m=4, l=NL)
        WIO = CM[0:CH, 2048:2304].rearrange("p (m c) -> p m c", m=2)
        PP = CM[0:CH, 2304:3328].rearrange("p (t k l c) -> p t k l c", t=2, k=2, l=NL)
        XS = sb("XS", [128, 2 * 2 * 1792])
        XIN = XS[0:84, :].rearrange("p (s w) -> p s w", s=2)
        AGG = XS[:, 0:2 * N].rearrange("p (s n) -> p s n", s=2)
        HID = XS[:, 0:8 * N].rearrange("p (s c n) -> p s c n", s=2, c=4)
        few = XS[0:TT, 8 * N:8 * N + TT].rearrange("p (k b) -> p k b", k=NT)
        XTB = sb("XTB", [128, 2 * 3 * HN])
        XT = XTB[:, :].rearrange("p (s c g i) -> p s c g i", s=2, c=3, g=GH)
        ONE = XTB[:, :].bitcast(BF16)
        EYEW = ONE[0:TT, 0:2 * N]
        OSRC = ONE[0:EP, 2 * N:4 * N].rearrange("p (s n) -> p s n", s=2)
        ODST = ONE[0:EP, 4 * N:4 * N + 2 * HN].rearrange("p (s n) -> p s n", s=2)
        DIAG = XTB[0:TT, 0:N].rearrange("p (k t) -> p k t", k=NT)
        GEL = XTB[0:TT, 0:1024].rearrange("p (s c) -> p s c", s=2)
        R = sb("R", [128, NL, LC, QB])
        RF = R[:, :, :, :].rearrange("p l q c -> p (l q c)")
        W1 = RF[:, 0:512].rearrange("p (q m) -> p q m", q=4)
        W2 = RF[:, 512:1024].rearrange("p (q m) -> p q m", q=4)
        WR = RF[:, 1024:2048].rearrange("p (g d b) -> p g d b", g=NP, d=8)
        SWS = sb("SWS", [128, NL, LEVELS, 128])
        SW = sb("SW", [128, NL, 2, LC + CH])
        POS = sb("POS", [128, N])
        ST = POS[0:TT, 0:672].rearrange("p (h u s) -> p h u s", h=2, s=6)
        IDENT = sb("IDENT", [128, 128])
        II = sb("II", [64, 128])
        SELF = sb("SELF", [24, 512], BF16)
        TRI = sb("TRI", [TT, 2 * TT], BF16)
        SUMM = sb("SUMM", [128, 129])
        DIG = sb("DIG", [128, len(RADIX)], I32)
        ONES = sb("ONES", [128, 129])
        BAND = sb("BAND", [TT, BW])
        WE = sb("WE", [128, 3, 128])
        WG = sb("WG", [128, NG, 128])
        WL = sb("WL", [128, 3, 128])
        BIAS = sb("BIAS", [128, 10])
        BROW = sb("BROW", [TT, 5, CH])
        DG = sb("DG", [TT, 4, NT])
        DROW = sb("DROW", [128, N])
        NE_ = sb("NE_", [EP, 2])
        FLAG = sb("FLAG", [1, 1], I32)
        LNS = sb("LNS", [TT, 6, 56])
        MEAN = sb("MEAN", [TT, 2, 56])
        RSTD = sb("RSTD", [TT, 2, 56])
        ES = sb("ES", [TT, 128])
        SC = sb("SC", [128, 2, HP, LC + 1])
        SX = sb("SX", [128, HP, LC])
        ZF = sb("ZF", [TT, 2, 56])
        ZB = sb("ZB", [TT, 3, 56], BF16)
        Z3 = sb("Z3", [24, 2, N], BF16)
        WROW = CM[:, 0:N]
        JUNK = CM[:, N:2 * N]
        GTR = CM[0:NB, 2 * N:3 * N]
        EQR = CM[0:NB, 3 * N:4 * N]
        KEY = sb("KEY", [128, 4], I32)
        CNT = sb("CNT", [128, 2])
        PREF = sb("PREF", [128, 2], I32)
        WTOK = sb("WTOK", [TT, NT, NB])
        GEB = sb("GEB", [TT, 2, NT, NB], BF16)
        GSUM = sb("GSUM", [TT, NB])
        GSB = sb("GSB", [TT, NB], BF16)
        WM = sb("WM", [TT, NT, NB])

        first_in = sem("first_in")
        par_in = sem("par_in")
        wts_in = sem("wts_in")
        late_in = sem("late_in")
        mlp_in = sem("mlp_in")
        wr_set = sem("wr_set")
        zeroed = sem("zeroed")
        x_in = [sem("x_in0"), sem("x_in1")]
        perm_a = sem("perm_a")
        perm_v = sem("perm_v")
        perm_p = sem("perm_p")
        flag_mm = sem("flag_mm")
        flag_set = sem("flag_set")
        pre_mm = sem("pre_mm")
        pre_ev = sem("pre_ev")
        eye_set = sem("eye_set")
        hot = sem("hot")
        hot_mm = sem("hot_mm")
        adj_ev = sem("adj_ev")
        deg_mm = sem("deg_mm")
        dg_set = sem("dg_set")
        row_mm = sem("row_mm")
        row_ev = sem("row_ev")
        pool_gen = sem("pool_gen")
        dve_gen = sem("dve_gen")
        dve_ch = sem("dve_ch")
        pool_ch = sem("pool_ch")
        emb_t = sem("emb_t")
        emb_tv = sem("emb_tv")
        emb_tw = sem("emb_tw")
        emb_mm = sem("emb_mm")
        emb_ev = sem("emb_ev")
        hw_mm = sem("hw_mm")
        hw_ev = sem("hw_ev")
        agg_mm = sem("agg_mm")
        agg_sc = sem("agg_sc")
        h_ready = sem("h_ready")
        tok_mm = sem("tok_mm")
        tok_ev = sem("tok_ev")
        gel_used = sem("gel_used")
        t_ready = sem("t_ready")
        tp_mm = sem("tp_mm")
        uc_ready = sem("uc_ready")
        toep = sem("toep")
        taps_in = sem("taps_in")
        conv_mm = sem("conv_mm")
        es_ev = sem("es_ev")
        scan_mm = sem("scan_mm")
        scan_ev = sem("scan_ev")
        z_mm = sem("z_mm")
        z_ev = sem("z_ev")
        z_split = sem("z_split")
        z_in = sem("z_in")
        res_b = sem("res_b")
        r_mm = sem("r_mm")
        cnt_rd = sem("cnt_rd")
        rad_mm = sem("rad_mm")
        msk_rd = sem("msk_rd")
        msk_mm = sem("msk_mm")
        f_mm = sem("f_mm")
        f_ev = sem("f_ev")
        y_mm = sem("y_mm")
        y_ev = sem("y_ev")
        o_done = sem("o_done")
        stored = sem("stored")

        block = ctx.enter_context(nc.Block())

        prep, level_end = [], []

        def bank():
            return PS[:, 4 + len(prep) % 4, :]

        def product(mms, copies, after):
            prep.append((mms, copies, after))
            return len(prep) - 1

        def level():
            level_end.append(len(prep))
            return len(prep) - 1

        def layers(ap):
            return ap.rearrange("p (l c) -> p l c", l=NL)

        def blocks(dst, src):
            return [(dst(slice(64 * a, 64 * a + 64), a), src(slice(64 * a, 64 * a + 64))) for a in range(2)]

        def build_prep():
            b = bank()
            product([(b[0:64, l:l + 1], PAR[:, 2, l, 0:64], ONES[0:64, 128:129]) for l in range(NL)],
                    [(Q[l][:, 0, CH:QB], b[0:64, l:l + 1]) for l in range(NL)], -1)
            b = bank()
            product([(b[0:64, 64 * l:64 * l + 64], PAR[:, 0, l, 0:64], IDENT[0:64, 0:64]) for l in range(NL)],
                    [(PP[:, 0, 1, :, :], layers(b[0:64, 0:256])), (PP[:, 0, 0, :, :], PAR[:, 0, :, 0:64])], -1)
            b = bank()
            product([(b[:, 64 * j:64 * j + 64], WIO[:, j, :], IDENT[0:64, 0:64]) for j in range(2)],
                    [c for j in range(2) for c in blocks(lambda s, a: WL[s, 1 + j, s], lambda s: b[s, 64 * j:64 * j + 64])], -1)
            b = bank()
            product([(b[:, 64 * l:64 * l + 64], PAR[:, 3, l, :], IDENT[0:64, 0:64]) for l in range(NL)],
                    blocks(lambda s, a: SW[s, :, a, LC:LC + CH], lambda s: layers(b[s, 0:256])), -1)
            last = level()
            m, turn = 1, 0
            while m < LC + 1:
                w = min(m, LC + 1 - m)
                if 2 * m < LC + 1:
                    b = bank()
                    p, pt = PP[:, turn, 0], PP[:, turn, 1]
                    product([(b[0:64, 64 * l:64 * l + 64], pt[:, l, :], p[:, l, :]) for l in range(NL)] +
                            [(b[0:64, 256 + 64 * l:320 + 64 * l], p[:, l, :], pt[:, l, :]) for l in range(NL)],
                            [(PP[:, 1 - turn, :, :, :], b[0:64, :].rearrange("p (k l c) -> p k l c", k=2, l=NL))], last)
                for l in range(NL):
                    for q in range(0, w, 7):
                        n = min(7, w - q)
                        b = bank()
                        o = b[0:64, 0:n * QB].rearrange("p (q c) -> p q c", q=n)
                        product([(o, PP[:, turn, 0, l, :], Q[l][:, q:q + n, :])], [(Q[l][:, m + q:m + q + n, :], o)], last)
                    if l % 2 and w > 7:
                        level()
                if w <= 7:
                    level()
                last = len(prep) - 1
                turn = 1 - turn
                m *= 2
            powers = last
            b1_ = bank()
            product([(b1_[0:64, 128 * l:128 * l + 128], Q[l][:, LC, 0:CH], II[:, :]) for l in range(NL)],
                    [(PNN[:, :, :], layers(b1_[0:64, :]))], powers)
            b = bank()
            product([(b[:, 64 * l:64 * l + 64], II[:, :], Q[l][:, LC, 0:CH]) for l in range(NL)],
                    blocks(lambda s, a: SWS[s, :, 0, s], lambda s: layers(b[s, 0:256])), powers)
            b2_ = bank()
            product([(b2_[:, LC * l:LC * l + LC], II[:, :], Q[l][:, 0:LC, CH]) for l in range(NL)],
                    blocks(lambda s, a: SW[s, :, a, 0:LC], lambda s: layers(b2_[s, 0:NL * LC])), powers)
            last = level()
            for r in range(1, LEVELS):
                b = bank()
                product([(b[:, 64 * l:64 * l + 64], PNN[:, l, :], SWS[0:64, l, r - 1, 0:64]) for l in range(NL)],
                        blocks(lambda s, a: SWS[s, :, r, s], lambda s: layers(b[s, 0:256])), last)
                if r < LEVELS - 1:
                    c = bank()
                    product([(c[0:64, 128 * l:128 * l + 128], SWS[0:64, l, r - 1, 0:64], PNN[:, l, :]) for l in range(NL)],
                            [(PNN[:, :, :], layers(c[0:64, :]))], len(prep) - 1)
                l = r - 1
                for q in range(0, LC, 7):
                    c = bank()
                    o = c[:, 0:7 * QB].rearrange("p (q c) -> p q c", q=7)
                    product([(o, PAR[:, 1, l, :], Q[l][:, q:q + 7, :])], [(R[:, l, q:q + 7, :], o)], powers)
                last = level()

        build_prep()
        NPREP = len(prep)

        def prep_level(i):
            lo = level_end[i - 1] if 0 < i <= len(level_end) else 0
            if i >= len(level_end):
                return range(0)
            return range(lo, level_end[i])

        x_v = x.rearrange("b c (g i) w -> b (c g) (i w)", i=8)
        out_v = out.rearrange("b (k p) c -> p k b c", p=TT)
        halves = [slice(0, 64), slice(64, 128)]

        first_loads = [
            (IDENT[:, :], c_ident), (EI, edges.rearrange("s (p j) -> p s j", p=EP)),
            (EC_GRID, c_edges.rearrange("s (p j) -> p s j", p=EP)), (DG[:, 0, :], c_deg), (BAND[:, :], c_band),
        ]
        par_loads = [(PAR[:, m, :, 64 * a:64 * a + 64], w.rearrange("l n c -> n l c"))
                     for m, w, n in ((0, A, 1), (1, B, 2), (2, C, 1), (3, D, 2)) for a in range(n)]
        par_loads += [(WIO[:, j, 64 * a:64 * a + 64], w) for j, w in enumerate((w_in, w_out)) for a in range(2)]
        wts_loads = [(POS[:, :], c_pos)]
        for s in halves:
            wts_loads += [
                (WE[s, :, s], w_embed.rearrange("(c q) m -> q c m", c=3)), (BIAS[s, 0:1], b_embed.unsqueeze(1)),
                (WG[s, :, s], w_gcn.rearrange("l c m -> c l m")), (BIAS[s, 1:4], b_gcn.rearrange("l c -> c l")),
                (WL[s, 0, s], w_tok), (BIAS[s, 4:8], b1.rearrange("(q c) -> c q", c=64)), (BIAS[s, 9:10], wr),
            ]
        late_loads = [
            (sel_f, c_sel), (tri_f, c_tri), (SUMM[:, :], c_sum), (DIG[:, :], c_digit),
            (BROW[:, 0, :], b_tok.partition_broadcast(TT)), (BROW[:, 1, :], b_in.partition_broadcast(TT)),
            (BROW[:, 2, :], b_out.partition_broadcast(TT)), (BROW[:, 3, :], b2.partition_broadcast(TT)),
            (BROW[:, 4, :], b2.partition_broadcast(TT)),
            (BIAS[:, 8:9], br.partition_broadcast(128)),
        ]
        ACT_E, DVE_E, POOL_E = [0, 2], [1], [3]

        def permuted(eng, e):
            n = e // 4
            if e % 4 in ACT_E:
                eng.wait_ge(perm_a, 2 * n + ACT_E.index(e % 4) + 1)
            elif e % 4 in DVE_E:
                eng.wait_ge(perm_v, n + 1)
            else:
                eng.wait_ge(perm_p, n + 1)

        def permute(eng, copy, e, done):
            g = e // 2
            eng.wait_ge(x_in[g % 2], 32 * (g // 2 + 1))
            if e >= 4:
                eng.wait_ge(emb_t, 3 * (e - 3))
            src = XIN[:, g % 2, :].rearrange("p (a g j) -> p g a j", a=16, g=GRID)
            copy(XP[:, e % 4, :, :].rearrange("p g (a j) -> p g a j", a=16),
                 src[:, GH * (e % 2):GH * (e % 2) + GH]).then_inc(done, 1)

        @block.sync
        def _(sp):
            def load_pair(g):
                for a in range(2):
                    sp.dma_start(XIN[:, g % 2, a * 1792:a * 1792 + 1792], x_v[2 * g + a]).then_inc(x_in[g % 2], 16)

            sp.dma_start(*first_loads[0]).then_inc(first_in, 16)
            load_pair(0)
            for dst, src in first_loads[1:]:
                sp.dma_start(dst, src).then_inc(first_in, 16)
            load_pair(1)
            for dst, src in par_loads:
                sp.dma_start(dst, src).then_inc(par_in, 16)
            sp.wait_ge(zeroed, 1)
            for dst, src in wts_loads:
                sp.dma_start(dst, src, allow_slow_non_contiguous=True).then_inc(wts_in, 16)
            for g in range(2, NP):
                permuted(sp, 2 * g - 4)
                permuted(sp, 2 * g - 3)
                load_pair(g)

            def taps(l):
                sp.wait_ge(toep, l + 1)
                for a, s in enumerate(halves):
                    sp.dma_start(RW[s, a, :, LC:ZW], R[s, l, :, 0:CH]).then_inc(taps_in, 16)

            def z_rows(l, h):
                sp.wait_ge(z_split, 2 * l + h + 1)
                if l > 0:
                    sp.wait_ge(tok_mm, (1 + l) * UNITS + (h + 1) * NT)
                for q in range(3):
                    for a in range(2):
                        sp.dma_start(Z3[2 * q + a:24:6, h, :].rearrange("g (c j) -> g c j", j=LC),
                                     ZB[:, q, LC * a:LC * a + LC]).then_inc(z_in, 16)

            taps(0)
            for l in range(NL):
                z_rows(l, 0)
                if l + 1 < NL:
                    taps(l + 1)
                z_rows(l, 1)
            sp.wait_ge(zeroed, 4)
            for s in halves:
                sp.dma_start(W1[s, :, s], w1.rearrange("c (q m) -> c q m", m=64)).then_inc(mlp_in, 16)
                sp.dma_start(W2[s, :, s], w2.rearrange("(q c) m -> c q m", c=64)).then_inc(mlp_in, 16)
            for g in range(NP):
                sp.wait_ge(o_done, g + 1)
                for a in range(2):
                    sp.dma_start(out_v[:, :, 2 * g + a, :], T[:, :, 2 * g + a, :]).then_inc(stored, 16)
            sp.wait_ge(stored, 16 * NB)

        @block.tensor
        def _(pe):
            mm = nc.tensor.matmul
            SXF = SX[:, :, :].rearrange("p g c -> p (g c)")

            def degree_rows(after):
                pe.wait_ge(dg_set, after)
                for k in range(NT):
                    last = mm(PS[:, 6 + k // 4, TT * (k % 4):TT * (k % 4) + TT], ONES[0:TT, 0:128], DIAG[:, k, :],
                              start=True, stop=True)
                last.then_inc(row_mm, 1)

            pe.wait_ge(zeroed, 2)
            pe.wait_ge(flag_mm, 1)
            mm(PS[0:1, 5, 0:1], ONES[0:EP, 0:1], NE_[:, 0:1], start=True, stop=True).then_inc(flag_mm, 1)
            degree_rows(1)
            pe.wait_ge(row_ev, 1)
            pe.wait_ge(flag_set, 1)

            def patches(e):
                permuted(pe, e)
                for q in range(3):
                    if e > 0:
                        if q == 1:
                            pe.wait_ge(emb_tw, e)
                        else:
                            pe.wait_ge(emb_tv, 2 * e - 1 + q // 2)
                    for t in range(5 if q < 2 else 4):
                        last = nc.tensor.transpose(PS[:, q, 84 * t:84 * t + 84], XP[:, e % 4, 5 * q + t, :], IDENT[0:84, 0:84])
                    last.then_inc(emb_t, 1)

            def embed(e):
                pe.wait_ge(emb_tv, 2 * e + 2)
                pe.wait_ge(emb_tw, e + 1)
                if e > 0:
                    pe.wait_ge(emb_ev, e)
                for c in range(3):
                    last = mm(PS[:, 3, 0:HN], WE[:, c, :], XT[:, e % 2, c, :, :], start=(c == 0), stop=(c == 2))
                last.then_inc(emb_mm, 1)

            def prepare(i):
                for n in prep_level(i):
                    mms, _, after = prep[n]
                    need = max(after, n - 4)
                    if need >= 0:
                        pe.wait_ge(pre_ev, need + 1)
                    for o, lhsT, rhs in mms:
                        last = mm(o, lhsT, rhs, start=True, stop=True)
                    last.then_inc(pre_mm, 1)

            patches(0)
            pe.wait_ge(wts_in, 16 * len(wts_loads))
            pe.wait_ge(par_in, 16 * len(par_loads))
            for e in range(HALVES):
                if e + 1 < HALVES:
                    patches(e + 1)
                embed(e)
                prepare(e)
            for i in range(HALVES, len(level_end)):
                prepare(i)
            pe.wait_ge(emb_ev, HALVES)
            pe.wait_ge(pre_ev, NPREP)

            other_graph = nc.tensor.value_load(FLAG[0:1, 0:1], min_val=0, max_val=2 * NE)
            with nc.tensor.If(other_graph > 0):
                pe.wait_ge(eye_set, 1)
                for s in range(2):
                    if s:
                        pe.wait_ge(adj_ev, NT)
                    for k in range(NT):
                        w0 = N - TT * k + HN * s
                        last = mm(PS[0:TT, k, 0:HN], EYEW[:, N:N + TT], EYEW[:, w0:w0 + HN], start=True, stop=True)
                    if s == 0:
                        last.then_inc(hot_mm, 2)
                    with nc.tensor.Fori(0, EC // 2) as c:
                        for j in range(2):
                            pe.wait_ge(hot, c * 2 + (s * EC + j + 1))
                            for k in range(NT):
                                last = mm(PS[0:TT, k, 0:HN], OSRC[:, j, TT * k:TT * k + TT], ODST[:, j, :],
                                          start=False, stop=True, skip_group_check=True)
                            last.then_inc(hot_mm, 1)
                pe.wait_ge(adj_ev, 2 * NT)
                for k in range(NT):
                    for j in range(NT):
                        last = mm(PS[0:TT, 0, k:k + 1], ADJ[:, j, TT * k:TT * k + TT], ONES[0:TT, 0:1],
                                  start=(j == 0), stop=(j == NT - 1))
                last.then_inc(deg_mm, 1)
                degree_rows(2)
                pe.wait_ge(row_ev, 2)

            def hidden(l):
                for h in range(2):
                    if l > 0:
                        pe.wait_ge(h_ready, (l - 1) * NP + HP * (h + 1))
                    for k in range(NT):
                        n = l * UNITS + h * NT + k
                        if n >= 2:
                            pe.wait_ge(hw_ev, n - 1)
                        for g in range(HP):
                            last = mm(PS[0:TT, n % 2, 128 * g:128 * g + 128], UC[:, HP * h + g, TT * k:TT * k + TT],
                                      WG[:, l, :], start=True, stop=True)
                        last.then_inc(hw_mm, 1)

            def aggregate(l, sparse):
                for g in range(NP):
                    n = l * NP + g
                    pe.wait_ge(hw_ev, l * UNITS + (g // HP + 1) * NT)
                    if n >= 2:
                        pe.wait_ge(agg_sc, n - 1)
                    for s in range(2):
                        started = False
                        for k in range(NT):
                            lo, hi = (max(TT * k - GRID, HN * s), min(TT * k + TT + GRID, HN * s + HN)) if sparse else \
                                (HN * s, HN * s + HN)
                            if lo >= hi:
                                continue
                            w = BAND[:, lo - TT * k + GRID:hi - TT * k + GRID] if sparse else ADJ[:, k, lo:hi]
                            last = mm(PS[:, 4 + 2 * (n % 2) + s, lo - HN * s:hi - HN * s], HW[:, k, g, :], w,
                                      start=not started, stop=True, skip_group_check=True)
                            started = True
                    last.then_inc(agg_mm, 1)

            for l in range(NG):
                hidden(l)
                with nc.tensor.If(other_graph > 0):
                    aggregate(l, False)
                with nc.tensor.Else():
                    aggregate(l, True)

            def tok_stage(s, w, h, ready):
                for k in range(NT):
                    n = s * UNITS + h * NT + k
                    ready(k)
                    if n >= 2:
                        pe.wait_ge(tok_ev, n - 1)
                    for g in range(HP):
                        last = mm(PS[0:TT, n % 2, 128 * g:128 * g + 128], UC[:, HP * h + g, TT * k:TT * k + TT],
                                  w, start=True, stop=True)
                    last.then_inc(tok_mm, 1)

            def transposes(r, h):
                for k in range(NT):
                    n = r * UNITS + h * NT + k
                    if r == 1:
                        pe.wait_ge(tok_ev, n + 1)
                    else:
                        pe.wait_ge(t_ready, (n - UNITS if r else n) + 1)
                    if n >= 2:
                        pe.wait_ge(uc_ready, n - 1)
                    for g in range(HP):
                        last = nc.tensor.transpose(PS[:, 2 + n % 2, TT * g:TT * g + TT],
                                                   T[:, k, 8 * h + 2 * g:8 * h + 2 * g + 2, :], IDENT[0:TT, 0:TT])
                    last.then_inc(tp_mm, 1)

            for h in range(2):
                tok_stage(0, WL[:, 0, :], h, lambda k: pe.wait_ge(h_ready, (NG - 1) * NP + HP * (h + 1)))
            for h in range(2):
                transposes(0, h)
                tok_stage(1, WL[:, 1, :], h, lambda k: pe.wait_ge(uc_ready, h * NT + k + 1))
            for h in range(2):
                transposes(1, h)

            def conv(l, h, i0, i1):
                for i in range(i0, i1):
                    p = LC - 1 - i
                    if i == 0:
                        pe.wait_ge(uc_ready, (l + 1) * UNITS + (h + 1) * NT)
                        pe.wait_ge(taps_in, 32 * (l + 1))
                        if l > 0:
                            pe.wait_ge(z_ev, 2 * l + h - 1)
                    j0 = 0 if i == 0 else LC - p
                    o = PS[0:TT, 4 + h, 0:2 * ZW].rearrange("p (a z) -> p a z", a=2)[:, :, j0:ZW]
                    last = mm(o, UCF[:, HP * N * h + i:HP * N * (h + 1):LC], RW[:, :, p, j0:ZW],
                              start=(i == 0), stop=True, skip_group_check=True)
                if i1 == LC:
                    last.then_inc(conv_mm, 1)

            def scan(l, h, step):
                m0 = (SCAN - 1) * (2 * l + h)
                if step == 0:
                    pe.wait_ge(es_ev, 2 * l + h + 1)
                    nc.tensor.transpose(PS[:, 6, 0:TT], ES[:, :], IDENT[0:TT, 0:TT]).then_inc(scan_mm, 1)
                elif step <= LEVELS:
                    r = step - 1
                    sh = 1 << r
                    pe.wait_ge(scan_ev, m0 + r + 1)
                    o = PS[:, 6 + step % 2, 0:TT].rearrange("p (g c) -> p g c", g=HP)
                    mm(o, IDENT[:, :], SC[:, r % 2, :, 1:LC + 1], start=True, stop=True)
                    mm(o[:, :, sh:LC], SWS[:, l, r, :], SC[:, r % 2, :, 1:LC + 1 - sh],
                       start=False, stop=True, skip_group_check=True).then_inc(scan_mm, 1)
                else:
                    pe.wait_ge(scan_ev, m0 + SCAN - 1)
                    mm(PS[0:TT, 4 + h, 0:2 * ZW].rearrange("p (a z) -> p a z", a=2)[:, :, 0:LC], SXF, SW[:, l, :, 0:LC],
                       start=False, stop=True, skip_group_check=True).then_inc(z_mm, 1)

            def mixed(l, h, k):
                n = (2 + l) * UNITS + h * NT + k
                pe.wait_ge(tok_ev, n - 1)
                b = PS[0:TT, n % 2, :]
                for g in range(HP):
                    mm(b[:, 128 * g:128 * g + 128], UC[:, HP * h + g, TT * k:TT * k + TT],
                       SW[:, l, :, LC:LC + CH], start=(g == 0), stop=True, skip_group_check=True)
                if k == 0:
                    pe.wait_ge(z_in, 96 * (2 * l + h + 1))
                mm(b, Z3[:, h, TT * k:TT * k + TT], SELF[:, :], start=False, stop=True,
                   skip_group_check=True).then_inc(tok_mm, 1)

            for l in range(NL):
                conv(l, 0, 0, LC)
                if l > 0:
                    transposes(l + 1, 1)
                for s in range(SCAN):
                    conv(l, 1, 3 * s, 3 * s + 3)
                    scan(l, 0, s)
                conv(l, 1, 3 * SCAN, LC)
                for s in range(SCAN):
                    mixed(l, 0, s)
                    scan(l, 1, s)
                for k in range(NT):
                    mixed(l, 1, k)
                transposes(l + 2, 0)
            tok_stage(6, WL[:, 2, :], 0, lambda k: pe.wait_ge(uc_ready, 5 * UNITS + k + 1))
            transposes(5, 1)
            tok_stage(6, WL[:, 2, :], 1, lambda k: pe.wait_ge(uc_ready, 5 * UNITS + NT + k + 1))

            def radix(r):
                pe.wait_ge(cnt_rd, r + 1)
                mm(PS[:, 6, 0:1], SUMM[:, 0:128], CNT[:, 1:2], start=True, stop=True).then_inc(rad_mm, 1)

            def masks():
                pe.wait_ge(msk_rd, 1)
                for v, row in enumerate((WROW[0:NB, :], GTR, EQR)):
                    for k in range(NT):
                        last = nc.tensor.transpose(PS[0:TT, 4 + v, NB * k:NB * k + NB], row[:, TT * k:TT * k + TT],
                                                   IDENT[0:NB, 0:NB])
                last.then_inc(msk_mm, 1)
                pe.wait_ge(msk_rd, 2)
                o = PS[0:TT, 7, 0:NT * NB].rearrange("p (k b) -> p k b", k=NT)
                mm(o, TRI[:, 0:TT], GEB[:, 1, :, :], start=True, stop=True)
                for k in range(NT - 1):
                    mm(o[:, k + 1:NT, :], TRI[:, TT:2 * TT],
                       GEB[:, 1, k:k + 1, :].broadcast_to([TT, NT - 1 - k, NB]), start=False, stop=True,
                       skip_group_check=True)
                mm(o, TRI[:, TT:2 * TT], GSB[:, :].unsqueeze(1).broadcast_to([TT, NT, NB]), start=False, stop=True,
                   skip_group_check=True).then_inc(msk_mm, 1)

            def up(g, q):
                for s in range(2):
                    n = 8 * g + 2 * q + s
                    if n >= 2:
                        pe.wait_ge(f_ev, n - 1)
                    else:
                        pe.wait_ge(tok_ev, 7 * UNITS)
                    mm(PS[:, n % 2, 0:HN], W1[:, q, :], UC[:, g, HN * s:HN * s + HN],
                       start=True, stop=True).then_inc(f_mm, 1)

            def down(g, s):
                n = 2 * g + s
                pe.wait_ge(f_ev, 8 * g + 8)
                if n >= 2:
                    pe.wait_ge(y_ev, n - 1)
                if n < 2:
                    pe.wait_ge(uc_ready, 7 * UNITS - NT)
                for k in range(4 * s, min(4 * s + 4, NT)):
                    for q in range(4):
                        last = mm(PS[0:TT, YB0 + s, 128 * (k - 4 * s):128 * (k - 4 * s) + 128],
                                  HID[:, g % 2, q, TT * k:TT * k + TT], W2[:, q, :], start=(q == 0), stop=(q == 3))
                last.then_inc(y_mm, 1)

            transposes(6, 0)
            pe.wait_ge(mlp_in, 16 * 4)
            pe.wait_ge(uc_ready, 6 * UNITS + NT)
            for q in range(4):
                up(0, q)
            transposes(6, 1)
            pe.wait_ge(uc_ready, 7 * UNITS)
            pe.wait_ge(wr_set, 1)
            for s in range(2):
                for g in range(NP):
                    last = mm(PS[:, 4 + s, 0:HN], WR[:, g, :, :].rearrange("p d b -> p (d b)"), UC[:, g, HN * s:HN * s + HN],
                              start=(g == 0), stop=(g == NP - 1))
            last.then_inc(r_mm, 1)
            r = 0
            for g in range(NP):
                for part in range(4):
                    if part < 2:
                        if g > 0:
                            up(g, 2 * part)
                            up(g, 2 * part + 1)
                    else:
                        down(g, part - 2)
                    if r < len(RADIX):
                        radix(r)
                        r += 1
                    elif r == len(RADIX):
                        masks()
                        r += 1

        @block.scalar
        def _(act):
            for e in range(-2, HALVES):
                if e + 2 < HALVES and (e + 2) % 4 in ACT_E:
                    permute(act, nc.scalar.copy, e + 2, perm_a)
                if e < 0:
                    continue
                if e >= 2:
                    act.wait_ge(emb_mm, e - 1)
                for q in (0, 2):
                    act.wait_ge(emb_t, 3 * e + q + 1)
                    n = 5 if q < 2 else 4
                    nc.scalar.copy(XT[:, e % 2, :, 5 * q:5 * q + n, :],
                                   PS[:, q, 0:84 * n].rearrange("p (g c i) -> p c g i", g=n, c=3)).then_inc(emb_tv, 1)
            for l in range(NG):
                for g in range(NP):
                    n = l * NP + g
                    act.wait_ge(agg_sc, n + 1)
                    nc.scalar.activation(UC[:, g, :], AGG[:, n % 2, :], ACT.Relu,
                                         bias=BIAS[:, 1 + l:2 + l]).then_inc(h_ready, 1)

            def to_uc(r, h):
                for k in range(NT):
                    n = r * UNITS + h * NT + k
                    act.wait_ge(tp_mm, n + 1)
                    nc.scalar.copy(UC[:, HP * h:HP * h + HP, TT * k:TT * k + TT],
                                   PS[:, 2 + n % 2, 0:HP * TT].rearrange("p (g t) -> p g t", g=HP))\
                        .then_inc(uc_ready, 1)

            for r in range(2):
                for h in range(2):
                    to_uc(r, h)

            def conv_out(l, h):
                return PS[0:TT, 4 + h, 0:2 * ZW].rearrange("p (a z) -> p a z", a=2)

            def states(l, h):
                act.wait_ge(conv_mm, 2 * l + h + 1)
                if l > 0 or h > 0:
                    act.wait_ge(scan_mm, (SCAN - 1) * (2 * l + h))
                nc.scalar.copy(ES[:, :].rearrange("p (a c) -> p a c", a=2), conv_out(l, h)[:, :, LC:ZW]).then_inc(es_ev, 1)

            def scan(l, h, r):
                m0 = (SCAN - 1) * (2 * l + h)
                act.wait_ge(scan_mm, m0 + r + 1)
                src = PS[:, 6 + r % 2, 0:TT].rearrange("p (g c) -> p g c", g=HP)
                if r < LEVELS:
                    nc.scalar.copy(SC[:, r % 2, :, 1:LC + 1], src).then_inc(scan_ev, 1)
                else:
                    if l > 0 or h > 0:
                        act.wait_ge(z_mm, 2 * l + h)
                    nc.scalar.copy(SX[:, :, 1:LC], src[:, :, 0:LC - 1]).then_inc(scan_ev, 1)

            def outputs(l, h):
                act.wait_ge(z_mm, 2 * l + h + 1)
                if l > 0 or h > 0:
                    act.wait_ge(z_split, 2 * l + h)
                nc.scalar.copy(ZF[:, 0, :].rearrange("p (a j) -> p a j", a=2), conv_out(l, h)[:, :, 0:LC]).then_inc(z_ev, 1)

            def gelu(l, h, k):
                n = (2 + l) * UNITS + h * NT + k
                u = l * UNITS + h * NT + k
                act.wait_ge(tok_mm, n + 1)
                if u >= 2:
                    act.wait_ge(gel_used, u - 1)
                nc.scalar.activation(GEL[:, n % 2, :], PS[0:TT, n % 2, :], ACT.Gelu).then_inc(tok_ev, 1)

            act.wait_ge(zeroed, 2)
            for l in range(NL):
                states(l, 0)
                if l > 0:
                    to_uc(l + 1, 1)
                for r in range(SCAN - 1):
                    scan(l, 0, r)
                outputs(l, 0)
                states(l, 1)
                for k in range(NT):
                    gelu(l, 0, k)
                    if k < SCAN - 1:
                        scan(l, 1, k)
                outputs(l, 1)
                for k in range(NT):
                    gelu(l, 1, k)
                to_uc(l + 2, 0)
            to_uc(5, 1)
            to_uc(6, 0)

            def mlp_gelu(g):
                if g >= 2:
                    act.wait_ge(y_mm, 2 * g - 2)
                for q in range(4):
                    for s in range(2):
                        n = 8 * g + 2 * q + s
                        act.wait_ge(f_mm, n + 1)
                        nc.scalar.activation(HID[:, g % 2, q, HN * s:HN * s + HN], PS[:, n % 2, 0:HN],
                                             ACT.Gelu_apprx_tanh, bias=BIAS[:, 4 + q:5 + q]).then_inc(f_ev, 1)

            mlp_gelu(0)
            to_uc(6, 1)
            for g in range(1, NP):
                mlp_gelu(g)

        @block.gpsimd
        def _(pool):
            chain = [0]

            def link(ins):
                chain[0] += 1
                ins.then_inc(pool_ch, 1)
                pool.wait_ge(pool_ch, chain[0])

            g_ = nc.gpsimd
            g_.memset(ONES[:, 0:128], 1.0)
            g_.memset(ONES[:, 128:129], 1.0 / CH)
            g_.memset(WE[:, :, :], 0.0)
            g_.memset(WG[:, :, :], 0.0)
            link(g_.memset(WL[:, :, :], 0.0))
            g_.memset(BIAS[:, :], 0.0).then_inc(zeroed, 1)
            pool.wait_ge(zeroed, 1)
            for dst, src in late_loads:
                pool.dma_start(dst, src).then_inc(late_in, 16)
            pool.wait_ge(first_in, 16 * len(first_loads))
            g_.tensor_copy(II[:, 0:64], IDENT[0:64, 0:64])
            g_.tensor_copy(II[:, 64:128], IDENT[0:64, 0:64])
            for l in range(NL):
                g_.tensor_copy(Q[l][:, 0, 0:CH], IDENT[0:64, 0:64])
            g_.memset(SW[:, :, :, :], 0.0)
            g_.memset(SWS[:, :, :, :], 0.0)
            g_.memset(SX[:, :, :], 0.0)
            link(g_.memset(SC[:, :, :, :], 0.0))
            g_.memset(TRI[:, TT:2 * TT], 1.0).then_inc(zeroed, 1)
            for e in range(HALVES):
                if e % 4 in POOL_E:
                    permute(pool, g_.tensor_copy, e, perm_p)
                if e == 3:
                    pool.wait_ge(perm_p, 1)
                    pool.wait_ge(late_in, 16 * len(late_loads))
                    link(g_.tensor_copy(SELF[:, :], sel_f))
                    link(g_.tensor_copy(TRI[:, 0:TT], tri_f))
            pool.wait_ge(flag_set, 1)
            other_graph = nc.gpsimd.value_load(FLAG[0:1, 0:1], min_val=0, max_val=2 * NE)
            pool.wait_ge(perm_p, HALVES // 4)
            pool.wait_ge(emb_mm, HALVES)
            with nc.gpsimd.If(other_graph > 0):
                g_.memset(EYEW[:, :], 0.0).then_inc(pool_gen, 1)
                pool.wait_ge(pool_gen, 1)
                g_.affine_select(out=EYEW[:, :], in_=EYEW[:, :], compare_op=ALU.not_equal, fill=1.0, base=N,
                                 pattern=[[-1, 2 * N]], channel_multiplier=1).then_inc(pool_gen, 1)
                pool.wait_ge(pool_gen, 2)
                g_.iota(IOTA[:, :], pattern=[[1, N]], base=0, channel_multiplier=0,
                        allow_small_or_imprecise_dtypes=True).then_inc(eye_set, 1)
                pool.wait_ge(eye_set, 1)
            pool.wait_ge(agg_mm, NG * NP)
            g_.memset(RW[:, :, :, :], 0.0).then_inc(zeroed, 1)
            pool.wait_ge(zeroed, 3)
            for h in range(2):
                pool.wait_ge(t_ready, (h + 1) * NT)
                rv = RES[:, :, 8 * h:8 * h + 8, :]
                for k in range(NT):
                    ins = g_.tensor_tensor(rv[:, k], rv[:, k], BROW[:, 2, :].unsqueeze(1).broadcast_to([TT, 8, CH]), ALU.add)
                ins.then_inc(res_b, 1)
            for l in range(NL):
                for h in range(2):
                    pool.wait_ge(z_ev, 2 * l + h + 1)
                    if l > 0 or h > 0:
                        pool.wait_ge(z_in, 96 * (2 * l + h))
                    link(g_.tensor_copy(ZB[:, 0, :], ZF[:, 0, :]))
                    link(g_.tensor_tensor(ZF[:, 1, :], ZF[:, 0, :], ZB[:, 0, :], ALU.subtract))
                    link(g_.tensor_copy(ZB[:, 1, :], ZF[:, 1, :]))
                    g_.tensor_tensor(ZB[:, 2, :], ZF[:, 1, :], ZB[:, 1, :], ALU.subtract).then_inc(z_split, 1)
                    for k in range(NT):
                        u = l * UNITS + h * NT + k
                        pool.wait_ge(tok_ev, 2 * UNITS + u + 1)
                        tv = T[:, k, 8 * h:8 * h + 8, :]
                        g_.tensor_tensor(tv, tv, GEL[:, u % 2, :].rearrange("p (b c) -> p b c", b=8),
                                         ALU.add).then_inc(gel_used, 1)
                if l + 1 == NL:
                    pool.wait_ge(gel_used, NL * UNITS)
                    pool.wait_ge(taps_in, 32 * NL)
                    link(g_.memset(RF[:, 0:2048], 0.0))
                    for a, s in enumerate(halves):
                        flat = RF[s, 1024:2048]
                        diag = bass.AP(tensor=flat.tensor, offset=flat.offset + a,
                                       ap=[list(flat.ap[0]), [8 * NB + 2, NP], [NB, 8]])
                        link(g_.tensor_copy(diag, BIAS[s, 9:10].unsqueeze(2).broadcast_to([64, NP, 8])))
                    g_.memset(GSUM[:, :], 0.0).then_inc(zeroed, 1)
                    pool.wait_ge(zeroed, 4)
                    g_.memset(GSUM[:, :], 0.0).then_inc(wr_set, 1)
                    pool.wait_ge(wr_set, 1)
            for h in range(2):
                pool.wait_ge(t_ready, 5 * UNITS + (h + 1) * NT)
                for k in range(NT):
                    rv = RES[:, k, 8 * h:8 * h + 8, :]
                    ins = g_.tensor_tensor(rv, rv, T[:, k, 8 * h:8 * h + 8, :], ALU.add)
                ins.then_inc(res_b, 1)

        @block.vector
        def _(dve):
            chain = [0]
            v_ = nc.vector

            def link(ins):
                chain[0] += 1
                ins.then_inc(dve_ch, 1)
                dve.wait_ge(dve_ch, chain[0])

            def rsqrt(v, y, t, link=link):
                link(v_.tensor_scalar(t.bitcast(I32), v.bitcast(I32), 1, None, ALU.logical_shift_right))
                link(v_.tensor_scalar(y.bitcast(I32), t.bitcast(I32), -1.0, float(0x5f3759df), ALU.mult, ALU.add))
                for _ in range(3):
                    link(v_.scalar_tensor_tensor(out=t, in0=y, scalar=-0.5, in1=y, op0=ALU.mult, op1=ALU.mult))
                    link(v_.tensor_tensor(t, t, v, ALU.mult))
                    link(v_.scalar_tensor_tensor(out=y, in0=t, scalar=1.5, in1=y, op0=ALU.add, op1=ALU.mult))

            def degree_rows(n, link):
                rsqrt(DG[:, 0, :], DG[:, 1, :], DG[:, 2, :], link)
                for k in range(NT):
                    ins = v_.tensor_scalar(DIAG[:, k, :], IDENT[0:TT, 0:TT], DG[:, 1, k:k + 1], None, ALU.mult)
                ins.then_inc(dg_set, 1)
                dve.wait_ge(row_mm, n)
                v_.tensor_copy(DROW[:, 0:4 * TT], PS[:, 6, 0:4 * TT])
                v_.tensor_copy(DROW[:, 4 * TT:N], PS[:, 7, 0:3 * TT]).then_inc(row_ev, 1)

            dve.wait_ge(first_in, 16 * len(first_loads))
            link(v_.tensor_tensor(EC_GRID.bitcast(F32), EI, EC_GRID, ALU.not_equal))
            v_.tensor_reduce(NE_[:, 0:1], EC_GRID.bitcast(F32), AX.X, ALU.add).then_inc(flag_mm, 1)
            permute(dve, v_.tensor_copy, 1, perm_v)
            dve.wait_ge(flag_mm, 2)
            v_.tensor_copy(FLAG[:, :], PS[0:1, 5, 0:1]).then_inc(flag_set, 1)
            degree_rows(1, link)

            def group(e):
                if e >= 2:
                    dve.wait_ge(emb_mm, e - 1)
                dve.wait_ge(emb_t, 3 * e + 2)
                v_.tensor_copy(XT[:, e % 2, :, 5:10, :],
                               PS[:, 1, 0:420].rearrange("p (g c i) -> p c g i", g=5, c=3)).then_inc(emb_tw, 1)

            def embedded(e):
                dve.wait_ge(emb_mm, e + 1)
                cols = slice(GH * (e % 2), GH * (e % 2) + GH)
                v_.scalar_tensor_tensor(out=UC[:, e // 2, :].rearrange("p (i g) -> p g i", i=GRID)[:, cols, :],
                                        in0=PS[:, 3, 0:HN].rearrange("p (g i) -> p g i", g=GH), scalar=BIAS[:, 0:1],
                                        in1=POS[:, :].rearrange("p (i g) -> p g i", i=GRID)[:, cols, :],
                                        op0=ALU.add, op1=ALU.add).then_inc(emb_ev, 1)

            def prepare(i):
                for n in prep_level(i):
                    dve.wait_ge(pre_mm, n + 1)
                    for dst, src in prep[n][1]:
                        ins = v_.tensor_copy(dst, src)
                    ins.then_inc(pre_ev, 1)

            group(0)
            dve.wait_ge(wts_in, 16 * len(wts_loads))
            for e in range(HALVES):
                if e + 3 < HALVES and (e + 3) % 4 in DVE_E:
                    permute(dve, v_.tensor_copy, e + 3, perm_v)
                if e + 1 < HALVES:
                    group(e + 1)
                embedded(e)
                prepare(e)
            for i in range(HALVES, len(level_end)):
                prepare(i)
            dve.wait_ge(pre_ev, NPREP)

            other_graph = nc.vector.value_load(FLAG[0:1, 0:1], min_val=0, max_val=2 * NE)
            with nc.vector.If(other_graph > 0):
                general = [0]

                def glink(ins):
                    general[0] += 1
                    ins.then_inc(dve_gen, 1)
                    dve.wait_ge(dve_gen, general[0])

                dve.wait_ge(eye_set, 1)
                glink(v_.tensor_copy(EF, EI.rearrange("p (s j) -> p s j", s=2)))
                for s in range(2):
                    with nc.vector.Fori(0, EC // 2) as c:
                        for j in range(2):
                            dve.wait_ge(hot_mm, c * 2 + (s * EC + j + 1))
                            v_.tensor_scalar(OSRC[:, j, :], IOTA[0:EP, :], EF[:, 0, bass.ds(c * 2 + j, 1)], None, ALU.is_equal)
                            v_.tensor_scalar(ODST[:, j, :], IOTA[0:EP, HN * s:HN * s + HN], EF[:, 1, bass.ds(c * 2 + j, 1)],
                                             None, ALU.is_equal).then_inc(hot, 1)
                    dve.wait_ge(hot_mm, (s + 1) * EC + 2)
                    for k in range(NT):
                        v_.tensor_copy(ADJ[:, k, HN * s:HN * s + HN], PS[0:TT, k, 0:HN]).then_inc(adj_ev, 1)
                dve.wait_ge(deg_mm, 1)
                glink(v_.tensor_copy(DG[:, 0, :], PS[0:TT, 0, 0:NT]))
                degree_rows(2, glink)

            for l in range(NG):
                for h in range(2):
                    for k in range(NT):
                        n = l * UNITS + h * NT + k
                        dve.wait_ge(hw_mm, n + 1)
                        if h == 0 and k == 0 and l > 0:
                            dve.wait_ge(agg_mm, l * NP)
                        v_.tensor_scalar(HW[:, k, HP * h:HP * h + HP, :].rearrange("p g m -> p (g m)"), PS[0:TT, n % 2, :],
                                         DG[:, 1, k:k + 1], None, ALU.mult).then_inc(hw_ev, 1)
                for g in range(NP):
                    n = l * NP + g
                    dve.wait_ge(agg_mm, n + 1)
                    if n >= 2:
                        dve.wait_ge(h_ready, n - 1)
                    b0 = 4 + 2 * (n % 2)
                    v_.tensor_tensor(AGG[:, n % 2, :].rearrange("p (s j) -> p s j", s=2), PS[:, b0:b0 + 2, 0:HN],
                                     DROW[:, :].rearrange("p (s j) -> p s j", s=2), ALU.mult).then_inc(agg_sc, 1)

            def norm(h, src, ready, twice=False):
                for k in range(NT):
                    ready(k)
                    for b in range(8):
                        ins = v_.bn_stats(ST[:, h, 8 * k + b, :], src[:, k, 8 * h + b, :])
                link(ins)
                me, mo = ST[:, h, :, 1], ST[:, h, :, 4]
                diff, var, tmp, eps_var = LNS[:, 0, :], LNS[:, 1, :], LNS[:, 2, :], LNS[:, 5, :]
                v_.tensor_tensor(diff, me, mo, ALU.subtract)
                v_.tensor_tensor(LNS[:, 3, :], me, mo, ALU.add)
                link(v_.tensor_tensor(tmp, ST[:, h, :, 2], ST[:, h, :, 5], ALU.add))
                v_.tensor_scalar(MEAN[:, h, :], LNS[:, 3, :], 0.5, None, ALU.mult)
                v_.tensor_tensor(LNS[:, 4, :], diff, diff, ALU.mult)
                link(v_.tensor_scalar(tmp, tmp, 1.0 / CH, None, ALU.mult))
                link(v_.scalar_tensor_tensor(out=var, in0=LNS[:, 4, :], scalar=0.25, in1=tmp, op0=ALU.mult, op1=ALU.add))
                link(v_.tensor_scalar(eps_var, var, EPS, None, ALU.add))
                rsqrt(eps_var, RSTD[:, h, :], tmp)
                if twice:
                    link(v_.tensor_tensor(tmp, RSTD[:, h, :], RSTD[:, h, :], ALU.mult))
                    link(v_.tensor_tensor(tmp, tmp, var, ALU.mult))
                    link(v_.tensor_scalar(eps_var, tmp, EPS, None, ALU.add))
                    rsqrt(eps_var, LNS[:, 3, :], tmp)
                    link(v_.tensor_tensor(RSTD[:, h, :], RSTD[:, h, :], LNS[:, 3, :], ALU.mult))
                for k in range(NT):
                    for b in range(8):
                        u = 8 * k + b
                        ins = v_.tensor_scalar(T[:, k, 8 * h + b, :], src[:, k, 8 * h + b, :], MEAN[:, h, u:u + 1],
                                               RSTD[:, h, u:u + 1], ALU.subtract, ALU.mult)
                    ins.then_inc(t_ready, 1)

            def row(j):
                return BROW[:, j, :].unsqueeze(1).broadcast_to([TT, 8, CH])

            def from_psum(s, h, dst, other):
                for k in range(NT):
                    n = s * UNITS + h * NT + k
                    dve.wait_ge(tok_mm, n + 1)
                    v_.tensor_tensor(dst[:, k, 8 * h:8 * h + 8, :], PS[0:TT, n % 2, :].rearrange("p (b c) -> p b c", b=8),
                                     other(k), ALU.add).then_inc(tok_ev, 1)

            dve.wait_ge(late_in, 16 * len(late_loads))
            from_psum(0, 0, RES, lambda k: row(0))
            from_psum(0, 1, RES, lambda k: row(0))
            norm(0, RES, lambda k: dve.wait_ge(tok_ev, k + 1))
            from_psum(1, 0, T, lambda k: row(1))
            norm(1, RES, lambda k: dve.wait_ge(tok_ev, NT + k + 1))
            from_psum(1, 1, T, lambda k: row(1))

            def toeplitz(l):
                for a, s in enumerate(halves):
                    flat = RW[s, a, :, :].rearrange("p q z -> p (q z)")
                    diag = bass.AP(tensor=flat.tensor, offset=flat.offset + LC, ap=[list(flat.ap[0]), [ZW - 1, LC], [1, LC]])
                    ins = v_.tensor_copy(diag, R[s, l, :, CH].unsqueeze(1).broadcast_to([64, LC, LC]))
                ins.then_inc(toep, 1)

            dve.wait_ge(zeroed, 3)
            toeplitz(0)
            for l in range(NL):
                if l + 1 < NL:
                    dve.wait_ge(conv_mm, 2 * l + 2)
                    toeplitz(l + 1)
                for h in range(2):
                    norm(h, T, lambda k: dve.wait_ge(gel_used, l * UNITS + h * NT + k + 1), l + 1 == NL)
            for h in range(2):
                dve.wait_ge(res_b, h + 1)
                from_psum(6, h, RES, lambda k: RES[:, k, 8 * h:8 * h + 8, :])
                norm(h, RES, lambda k: dve.wait_ge(tok_ev, 6 * UNITS + h * NT + k + 1))

            def threshold(key):
                link(v_.tensor_scalar(KEY[:, 1:2], key, 31, -1, ALU.arith_shift_right, ALU.bitwise_xor))
                link(v_.tensor_scalar(KEY[:, 2:3], KEY[:, 1:2], -2147483648, None, ALU.bitwise_or))
                link(v_.tensor_tensor(KEY[:, 3:4], KEY[:, 2:3], key, ALU.bitwise_xor))

            def radix(r):
                sh = RADIX[r]
                tail = r == len(RADIX) - 1
                link(v_.tensor_tensor(KEY[:, 0:1], PREF[:, 0:1], DIG[:, r:r + 1], ALU.bitwise_or))
                threshold(KEY[:, 0:1])
                link(v_.tensor_scalar(JUNK, WROW, KEY[:, 3:4].bitcast(F32), 0.0, ALU.is_ge, ALU.add, accum_out=CNT[:, 0:1]))
                v_.tensor_scalar(CNT[:, 1:2], CNT[:, 0:1], SUMM[:, 128:129], 0.5 if tail else 1.0, ALU.is_ge,
                                 ALU.mult).then_inc(cnt_rd, 1)

            def digit(r):
                dve.wait_ge(rad_mm, r + 1)
                link(v_.tensor_scalar(PREF[:, 1:2], PS[:, 6, 0:1], -1.0, None, ALU.add))
                if RADIX[r]:
                    link(v_.tensor_scalar(PREF[:, 1:2], PREF[:, 1:2], RADIX[r], None, ALU.logical_shift_left))
                link(v_.tensor_tensor(PREF[:, 0:1], PREF[:, 0:1], PREF[:, 1:2], ALU.bitwise_or))

            def mask_rows():
                threshold(PREF[:, 0:1])
                thr = KEY[0:NB, 3:4].bitcast(F32)
                v_.tensor_scalar(GTR, WROW[0:NB, :], thr, None, ALU.is_gt)
                v_.tensor_scalar(EQR, WROW[0:NB, :], thr, None, ALU.is_equal).then_inc(msk_rd, 1)

            def masks():
                dve.wait_ge(msk_mm, 1)
                v_.tensor_copy(WTOK[:, :, :].rearrange("p k b -> p (k b)"), PS[0:TT, 4, 0:TT])
                v_.tensor_copy(GEB[:, 0, :, :].rearrange("p k b -> p (k b)"), PS[0:TT, 5, 0:TT])
                link(v_.tensor_copy(GEB[:, 1, :, :].rearrange("p k b -> p (k b)"), PS[0:TT, 6, 0:TT]))
                link(v_.tensor_reduce(GSUM[:, :], GEB[:, 0, :, :].rearrange("p k b -> p b k"), AX.X, ALU.add))
                v_.tensor_copy(GSB[:, :], GSUM[:, :]).then_inc(msk_rd, 1)
                dve.wait_ge(msk_mm, 2)
                o = PS[0:TT, 7, 0:NT * NB].rearrange("p (k b) -> p k b", k=NT)
                link(v_.scalar_tensor_tensor(out=few, in0=o, scalar=float(KK), in1=GEB[:, 1, :, :], op0=ALU.is_lt, op1=ALU.mult))
                link(v_.tensor_tensor(few, few, GEB[:, 0, :, :], ALU.add))
                link(v_.tensor_tensor(WM[:, :, :], few, WTOK[:, :, :], ALU.mult))

            def b2_row(nk):
                return BROW[:, 3:5, :].rearrange("p a c -> p (a c)").unsqueeze(1).broadcast_to([TT, nk, 2 * CH])

            def y_out(g, s):
                nk, k0 = (4 if s == 0 else 3), 4 * s
                dve.wait_ge(y_mm, 2 * g + s + 1)
                if s == 0:
                    dve.wait_ge(res_b, 3 + g // HP)
                v_.tensor_tensor(T[:, k0:k0 + nk, 2 * g:2 * g + 2, :].rearrange("p k a c -> p k (a c)"),
                                 PS[0:TT, YB0 + s, 0:128 * nk].rearrange("p (k m) -> p k m", k=nk), b2_row(nk), ALU.add)\
                    .then_inc(y_ev, 1)

            def finish(g):
                dve.wait_ge(y_ev, 2 * g + 2)
                t = T[:, :, 2 * g:2 * g + 2, :]
                link(v_.tensor_tensor(t, t, WM[:, :, 2 * g:2 * g + 2].unsqueeze(3).broadcast_to([TT, NT, 2, CH]), ALU.mult))
                v_.tensor_tensor(t, t, RES[:, :, 2 * g:2 * g + 2, :], ALU.add).then_inc(o_done, 1)

            dve.wait_ge(r_mm, 1)
            link(v_.tensor_scalar(WROW.rearrange("p (s j) -> p s j", s=2), PS[:, 4:6, 0:HN], BIAS[:, 8:9], None, ALU.add))
            link(v_.memset(PREF[:, :], 0))
            r = 0
            masked = 0
            for g in range(NP):
                for part in range(4):
                    if r < len(RADIX):
                        radix(r)
                    elif r == len(RADIX):
                        mask_rows()
                    if part >= 2:
                        y_out(g, part - 2)
                    if r < len(RADIX):
                        digit(r)
                    elif r == len(RADIX):
                        masks()
                    r += 1
                if r > len(RADIX):
                    while masked <= g:
                        finish(masked)
                        masked += 1


_INS = ["x", "L0_tok_W_embed", "L0_tok_b_embed", "L0_tok_W_gcn", "L0_tok_b_gcn", "L0_tok_W_out", "L0_tok_b_out",
        "L0_tok_edge_index", "L0_attn_Win", "L0_attn_bin_", "L0_attn_Wout", "L0_attn_bout", "L0_attn_A", "L0_attn_Bm",
        "L0_attn_Cm", "L0_attn_Dm", "L0_ffn_wr", "L0_ffn_br", "L0_ffn_w1", "L0_ffn_b1", "L0_ffn_w2", "L0_ffn_b2"]


def _shape_constants():
    import numpy as np
    pos = np.arange(N, dtype=np.float32)[:, None]
    div = np.exp(np.arange(0, CH, 2, dtype=np.float32) * np.float32(-np.log(10000.0) / CH)).astype(np.float32)
    ang = (pos * div).astype(np.float32).astype(np.float64)
    pe = np.zeros((N, CH), np.float32)
    pe[:, 0::2] = np.sin(ang)
    pe[:, 1::2] = np.cos(ang)
    sel = np.zeros((24, 512), np.float32)
    for r in range(24):
        b = 2 * (r // 6) + r % 2
        sel[r, CH * b:CH * b + CH] = 1.0
    tri = np.triu(np.ones((TT, TT), np.float32), 1)
    same = np.equal(np.arange(128)[:, None] % NB, np.arange(128)[None, :] % NB).astype(np.float32)
    d = (np.arange(128) // NB).astype(np.int64)[:, None]
    digit = np.concatenate([(d << s if s else d & 3) for s in RADIX], 1)
    reach = np.where(d == 0, 0, KK).astype(np.float32)
    digit[:NB] = 0x00800000
    digit = (digit & 0xFFFFFFFF).astype(np.uint32).view(np.int32)
    same = np.concatenate([same, reach], 1)
    i, j = np.divmod(np.arange(N), GRID)
    pairs = []
    for n in range(N):
        if j[n] < GRID - 1:
            pairs.append((n, n + 1))
        if i[n] < GRID - 1:
            pairs.append((n, n + GRID))
    e = np.array(pairs, np.int32).T
    grid_edges = np.concatenate([e, e[::-1]], 1)
    adj = np.eye(N + 2 * TT, dtype=np.float32)
    for n in range(N + 2 * TT - 1):
        if (n + 1) % GRID:
            adj[n, n + 1] = adj[n + 1, n] = 1
        if n + GRID < N + 2 * TT:
            adj[n, n + GRID] = adj[n + GRID, n] = 1
    band = adj[TT:2 * TT, TT - GRID:2 * TT + GRID]
    deg = 1 + np.bincount(grid_edges[1], minlength=N).astype(np.float32)
    deg = deg.reshape(NT, TT).T
    pos = np.concatenate([pe.T, pe.T], 0)
    tables = {"ident": np.eye(128, dtype=np.float32), "sel": sel, "tri": tri, "sum": same, "pos": pos, "digit": digit,
              "edges": grid_edges, "band": band, "deg": deg}
    return {k: np.ascontiguousarray(v) for k, v in tables.items()}



def kernel(**inputs):
    import numpy as np
    import concourse.bacc as bacc
    from concourse.bass_utils import run_bass_kernel_spmd

    nc = bacc.Bacc("TRN2", target_bir_lowering=False, num_devices=1)
    arrays, args = {}, []
    given = [(n, inputs[n]) for n in _INS] + list(_shape_constants().items())
    for name, value in given:
        a = np.ascontiguousarray(value)
        arrays[f"in_{name}"] = a
        args.append(nc.dram_tensor(f"in_{name}", a.shape, mybir.dt.from_np(a.dtype), kind="ExternalInput").ap())
    out = nc.dram_tensor("out_0", (NB, N, CH), F32, kind="ExternalOutput").ap()
    tower(nc, *args, out)
    r = run_bass_kernel_spmd(nc, [arrays], core_ids=[0])
    return r.results[0]["out_0"]
```

```python
from contextlib import ExitStack

import concourse.bass as bass
from concourse import mybir

F32 = mybir.dt.float32
BF16 = mybir.dt.bfloat16
I32 = mybir.dt.int32
ALU = mybir.AluOpType
ACT = mybir.ActivationFunctionType
AX = mybir.AxisListType

NB = 16
NP = NB // 2
HP = NP // 2
GRID = 28
N = GRID * GRID
TT = 112
NT = N // TT
HN = N // 2
CH = 64
LC = 28
NG = 3
NL = 4
NE = 4 * GRID * (GRID - 1)
EC = 28
EP = NE // EC
ZW = 3 * LC + 4
QB = CH + 1
LEVELS = 5
KK = N // 2 - 1
UNITS = 2 * NT
EPS = 1e-5
RADIX = [29, 26, 23, 20, 17, 14, 11, 8, 5, 2, 0]
BW = TT + 2 * GRID
YB0 = 4
HALVES = 2 * NP
GH = GRID // 2
CHECK = 3
LATE = NP - 2
FIRST = 3
STEPS = 2 * NL
ORDER = {(4, 1): (5, 0), (5, 0): (4, 1)}
TURN = [2, 4, 6, 7, 7, 7, 7, 7]
FEED = [0, 0, 0, 2, 5, 8, 11, LC]
PROJECT = [0, 2, 4, 5, 6, 7, 7, 7]
ACT_UC = 2
DVE_N = 5


def tower(nc, x, w_embed, b_embed, w_gcn, b_gcn, w_tok, b_tok, edges, w_in, b_in, w_out, b_out,
          A, B, C, D, wr, br, w1, b1, w2, b2,
          c_ident, c_tri, c_sum, c_pos, c_digit, c_edges, c_band, c_deg, out):
    ctx = ExitStack()
    with ctx:
        def sb(name, shape, dt=F32):
            return ctx.enter_context(nc.sbuf_tensor(name, shape, dt))

        def sem(name):
            return ctx.enter_context(nc.semaphore(name))

        PS = ctx.enter_context(nc.psum_tensor("PS", [128, 8, 512], F32))

        TOK = NT * NB * CH
        UC = sb("UC", [128, NP, N])
        UCF = UC[:, :, :].rearrange("p g n -> p (g n)")
        BIG = sb("BIG", [128, 2 * TOK])
        T = BIG[0:TT, 0:TOK].rearrange("p (k b c) -> p k b c", k=NT, b=NB)
        RES = BIG[0:TT, TOK:].rearrange("p (k b c) -> p k b c", k=NT, b=NB)
        HW = BIG[0:TT, 0:TOK].rearrange("p (k g m) -> p k g m", k=NT, g=NP)
        XP = BIG[0:84, 0:7168].rearrange("p (s g q) -> p s g q", s=4, g=GH)
        IOTA = BIG[:, 0:N]
        EF = BIG[0:EP, N:N + 2 * EC].rearrange("p (s j) -> p s j", s=2)
        CM = sb("CM", [128, NT * N])
        ADJ = CM[0:TT, :].rearrange("p (k n) -> p k n", k=NT)
        RW = CM[:, 0:LC * 128].rearrange("p (q n) -> p q n", q=LC)
        QC = (LC + 1) * QB
        Q = [BIG[0:CH, TOK + QC * l:TOK + QC * l + QC].rearrange("p (q c) -> p q c", c=QB) for l in range(NL - 1)]
        Q.append(CM[0:CH, 3328:3328 + QC].rearrange("p (q c) -> p q c", c=QB))
        r0 = TOK + 3 * QC
        PNN = BIG[0:CH, r0:r0 + 512].rearrange("p (l c) -> p l c", l=NL)
        DIAG = BIG[0:TT, r0 + 512:r0 + 512 + N].rearrange("p (k t) -> p k t", k=NT)
        tri_f = BIG[0:TT, r0 + 512 + N:r0 + 512 + N + TT]
        e0 = 3328 + QC + 64
        EI = CM[0:EP, e0:e0 + 2 * EC].bitcast(I32)
        EC_GRID = CM[0:EP, e0 + 2 * EC:e0 + 4 * EC].bitcast(I32)
        PAR = CM[0:CH, 0:2048].rearrange("p (m l c) -> p m l c", m=4, l=NL)
        WIO = CM[0:CH, 2048:2304].rearrange("p (m c) -> p m c", m=2)
        PP = CM[0:CH, 2304:3328].rearrange("p (t k l c) -> p t k l c", t=2, k=2, l=NL)
        WOT = CM[0:CH, 3328 + QC:3328 + QC + 64]
        XS = sb("XS", [128, 2 * 2 * 1792])
        XIN = XS[0:84, :].rearrange("p (s w) -> p s w", s=2)
        AGG = XS[:, 0:2 * N].rearrange("p (s n) -> p s n", s=2)
        RZ = XS[:, 0:LC * ZW].rearrange("p (q z) -> p q z", q=LC)
        HID = XS[:, 0:8 * N].rearrange("p (s c n) -> p s c n", s=2, c=4)
        few = XS[0:TT, 8 * N:8 * N + TT].rearrange("p (k b) -> p k b", k=NT)
        XTB = sb("XTB", [128, 2 * 3 * HN])
        XT = XTB[:, :].rearrange("p (s c g i) -> p s c g i", s=2, c=3, g=GH)
        ONE = XTB[:, :].bitcast(BF16)
        EYEW = ONE[0:TT, 0:2 * N]
        OSRC = ONE[0:EP, 2 * N:4 * N].rearrange("p (s n) -> p s n", s=2)
        ODST = ONE[0:EP, 4 * N:4 * N + 2 * HN].rearrange("p (s n) -> p s n", s=2)
        GEL = XTB[0:TT, 0:1024].rearrange("p (s c) -> p s c", s=2)
        R = sb("R", [128, NL, LC, QB])
        RF = R[:, :, :, :].rearrange("p l q c -> p (l q c)")
        W1 = RF[:, 0:512].rearrange("p (q m) -> p q m", q=4)
        W2 = RF[:, 512:1024].rearrange("p (q m) -> p q m", q=4)
        WR = RF[:, 1024:2048].rearrange("p (g d b) -> p g d b", g=NP, d=8)
        SWS = sb("SWS", [128, NL, LEVELS, 128])
        SWD = sb("SWD", [128, NL, 2, CH])
        SWO = sb("SWO", [128, NL, 64])
        POS = sb("POS", [128, N])
        ST = POS[0:TT, 0:672].rearrange("p (h u s) -> p h u s", h=2, s=6)
        IDENT = sb("IDENT", [128, 128])
        II = sb("II", [64, 128])
        CEN = sb("CEN", [64, 128])
        TRI = sb("TRI", [TT, 2 * TT], BF16)
        SUMM = sb("SUMM", [128, 129])
        DIG = sb("DIG", [128, len(RADIX)], I32)
        ONES = sb("ONES", [128, 129])
        BAND = sb("BAND", [TT, BW])
        WE = sb("WE", [128, 3, 128])
        WG = sb("WG", [128, NG, 128])
        WL = sb("WL", [128, 3, 128])
        BIAS = sb("BIAS", [128, 10])
        BROW = sb("BROW", [TT, 5, CH])
        DG = sb("DG", [TT, 4, NT])
        DROW = sb("DROW", [128, N])
        NE_ = sb("NE_", [EP, 2])
        FLAG = sb("FLAG", [1, 1], I32)
        LNS = sb("LNS", [TT, 6, 56])
        MEAN = sb("MEAN", [TT, 2, 56])
        RSTD = sb("RSTD", [TT, 2, 56])
        SC = sb("SC", [128, 2, HP, LC + 1])
        SX = sb("SX", [128, HP, LC])
        ZS = sb("ZS", [64, 2, HP * LC])
        ZT = sb("ZT", [TT, 2, NT, 8])
        EJ = sb("EJ", [64, 4, TT])
        WROW = CM[:, 0:N]
        JUNK = CM[:, N:2 * N]
        GTR = CM[0:NB, 2 * N:3 * N]
        EQR = CM[0:NB, 3 * N:4 * N]
        KEY = sb("KEY", [128, 4], I32)
        CNT = sb("CNT", [128, 2])
        PREF = sb("PREF", [128, 2], I32)
        WTOK = sb("WTOK", [TT, NT, NB])
        GEB = sb("GEB", [TT, 2, NT, NB], BF16)
        GSUM = sb("GSUM", [TT, NB])
        GSB = sb("GSB", [TT, NB], BF16)
        WM = sb("WM", [TT, NT, NB])

        first_in = sem("first_in")
        emb_in = sem("emb_in")
        pos_in = sem("pos_in")
        graph_in = sem("graph_in")
        par_in = sem("par_in")
        wts_in = sem("wts_in")
        late_in = sem("late_in")
        mlp_in = sem("mlp_in")
        wr_set = sem("wr_set")
        zeroed = sem("zeroed")
        x_in = [sem("x_in0"), sem("x_in1")]
        perm_a = sem("perm_a")
        perm_p = sem("perm_p")
        flag_mm = sem("flag_mm")
        flag_set = sem("flag_set")
        pre_mm = sem("pre_mm")
        pre_ev = sem("pre_ev")
        eye_set = sem("eye_set")
        hot = sem("hot")
        hot_mm = sem("hot_mm")
        adj_ev = sem("adj_ev")
        deg_mm = sem("deg_mm")
        dg_set = sem("dg_set")
        row_mm = sem("row_mm")
        row_ev = sem("row_ev")
        pool_gen = sem("pool_gen")
        dve_gen = sem("dve_gen")
        dve_ch = sem("dve_ch")
        pool_ch = sem("pool_ch")
        emb_t = sem("emb_t")
        emb_tv = sem("emb_tv")
        emb_tw = sem("emb_tw")
        emb_mm = sem("emb_mm")
        emb_ev = sem("emb_ev")
        hw_mm = sem("hw_mm")
        hw_ev = sem("hw_ev")
        agg_mm = sem("agg_mm")
        agg_sc = sem("agg_sc")
        h_ready = sem("h_ready")
        tok_mm = sem("tok_mm")
        tok_ev = sem("tok_ev")
        gel_used = sem("gel_used")
        t_ready = sem("t_ready")
        tp_mm = sem("tp_mm")
        uc_ready = sem("uc_ready")
        toep = sem("toep")
        taps_in = sem("taps_in")
        sconv_mm = sem("sconv_mm")
        zconv_mm = sem("zconv_mm")
        scan_mm = sem("scan_mm")
        scan_ev = sem("scan_ev")
        z_mm = sem("z_mm")
        z_ev = sem("z_ev")
        zt_mm = sem("zt_mm")
        zt_ev = sem("zt_ev")
        mean_set = sem("mean_set")
        t_ready_p = sem("t_ready_p")
        res_b = sem("res_b")
        r_mm = sem("r_mm")
        cnt_rd = sem("cnt_rd")
        rad_mm = sem("rad_mm")
        msk_rd = sem("msk_rd")
        msk_mm = sem("msk_mm")
        f_mm = sem("f_mm")
        f_ev = sem("f_ev")
        y_mm = sem("y_mm")
        y_ev = sem("y_ev")
        y_b = sem("y_b")
        w_mm = sem("w_mm")
        w_ev = sem("w_ev")
        y_w = sem("y_w")
        o_done = sem("o_done")
        o_late = sem("o_late")
        stored = sem("stored")

        block = ctx.enter_context(nc.Block())

        prep, level_end = [], []

        def bank():
            return PS[:, 4 + len(prep) % 4, :]

        def product(mms, copies, after):
            prep.append((mms, copies, after))
            return len(prep) - 1

        def level():
            level_end.append(len(prep))
            return len(prep) - 1

        def layers(ap):
            return ap.rearrange("p (l c) -> p l c", l=NL)

        def blocks(dst, src):
            return [(dst(slice(64 * a, 64 * a + 64), a), src(slice(64 * a, 64 * a + 64))) for a in range(2)]

        def build_prep():
            b = bank()
            product([(b[0:64, l:l + 1], PAR[:, 2, l, 0:64], ONES[0:64, 128:129]) for l in range(NL)],
                    [(Q[l][:, 0, CH:QB], b[0:64, l:l + 1]) for l in range(NL)], -1)
            b = bank()
            product([(b[0:64, 64 * l:64 * l + 64], PAR[:, 0, l, 0:64], IDENT[0:64, 0:64]) for l in range(NL)],
                    [(PP[:, 0, 1, :, :], layers(b[0:64, 0:256])), (PP[:, 0, 0, :, :], PAR[:, 0, :, 0:64])], -1)
            b = bank()
            product([(b[:, 64 * j:64 * j + 64], WIO[:, j, :], IDENT[0:64, 0:64]) for j in range(2)],
                    blocks(lambda s, a: WL[s, 1, s], lambda s: b[s, 0:64]) + [(WOT, b[0:64, 64:128])], -1)
            b = bank()
            product([(b[:, 64 * l:64 * l + 64], PAR[:, 3, l, :], IDENT[0:64, 0:64]) for l in range(NL)],
                    blocks(lambda s, a: SWD[s, :, a, :], lambda s: layers(b[s, 0:256])), -1)
            last = level()
            b = bank()
            product([(b[:, 0:64], CEN[:, :], WOT)], blocks(lambda s, a: WL[s, 2, s], lambda s: b[s, 0:64]), last)
            m, turn = 1, 0
            while m < LC + 1:
                w = min(m, LC + 1 - m)
                if 2 * m < LC + 1:
                    b = bank()
                    p, pt = PP[:, turn, 0], PP[:, turn, 1]
                    product([(b[0:64, 64 * l:64 * l + 64], pt[:, l, :], p[:, l, :]) for l in range(NL)] +
                            [(b[0:64, 256 + 64 * l:320 + 64 * l], p[:, l, :], pt[:, l, :]) for l in range(NL)],
                            [(PP[:, 1 - turn, :, :, :], b[0:64, :].rearrange("p (k l c) -> p k l c", k=2, l=NL))], last)
                for l in range(NL):
                    for q in range(0, w, 7):
                        n = min(7, w - q)
                        b = bank()
                        o = b[0:64, 0:n * QB].rearrange("p (q c) -> p q c", q=n)
                        product([(o, PP[:, turn, 0, l, :], Q[l][:, q:q + n, :])], [(Q[l][:, m + q:m + q + n, :], o)], last)
                    if l % 2 and w > 7:
                        level()
                if w <= 7:
                    level()
                last = len(prep) - 1
                turn = 1 - turn
                m *= 2
            powers = last
            b1_ = bank()
            product([(b1_[0:64, 128 * l:128 * l + 128], Q[l][:, LC, 0:CH], II[:, :]) for l in range(NL)],
                    [(PNN[:, :, :], layers(b1_[0:64, :]))], powers)
            b = bank()
            product([(b[:, 64 * l:64 * l + 64], II[:, :], Q[l][:, LC, 0:CH]) for l in range(NL)],
                    blocks(lambda s, a: SWS[s, :, 0, s], lambda s: layers(b[s, 0:256])), powers)
            b2_ = bank()
            product([(b2_[:, LC * l:LC * l + LC], II[:, :], Q[l][:, 0:LC, CH]) for l in range(NL)],
                    blocks(lambda s, a: SWO[s, :, 32 * a:32 * a + LC], lambda s: layers(b2_[s, 0:NL * LC])), powers)
            last = level()
            for r in range(1, LEVELS):
                b = bank()
                product([(b[:, 64 * l:64 * l + 64], PNN[:, l, :], SWS[0:64, l, r - 1, 0:64]) for l in range(NL)],
                        blocks(lambda s, a: SWS[s, :, r, s], lambda s: layers(b[s, 0:256])), last)
                if r < LEVELS - 1:
                    c = bank()
                    product([(c[0:64, 128 * l:128 * l + 128], SWS[0:64, l, r - 1, 0:64], PNN[:, l, :]) for l in range(NL)],
                            [(PNN[:, :, :], layers(c[0:64, :]))], last)
                l = r - 1
                for q in range(0, LC, 7):
                    c = bank()
                    o = c[:, 0:7 * QB].rearrange("p (q c) -> p q c", q=7)
                    product([(o, PAR[:, 1, l, :], Q[l][:, q:q + 7, :])], [(R[:, l, q:q + 7, :], o)], powers)
                last = level()

        build_prep()
        NPREP = len(prep)

        def prep_level(i):
            lo = level_end[i - 1] if 0 < i <= len(level_end) else 0
            if i >= len(level_end):
                return range(0)
            return range(lo, level_end[i])

        x_v = x.rearrange("b c (g i) w -> b (c g) (i w)", i=8)
        out_v = out.rearrange("b (k p) c -> p k b c", p=TT)
        halves = [slice(0, 64), slice(64, 128)]

        emb_loads = [(WE[s, :, s], w_embed.rearrange("(c q) m -> q c m", c=3)) for s in halves]
        pos_loads = [(BIAS[s, 0:1], b_embed.unsqueeze(1)) for s in halves] + [(POS[:, :], c_pos)]
        graph_loads = [
            (EI, edges.rearrange("s (p j) -> p s j", p=EP)), (EC_GRID, c_edges.rearrange("s (p j) -> p s j", p=EP)),
            (BAND[:, :], c_band),
        ]
        par_loads = [(PAR[:, m, :, 64 * a:64 * a + 64], w.rearrange("l n c -> n l c"))
                     for m, w, n in ((0, A, 1), (1, B, 2), (2, C, 1), (3, D, 2)) for a in range(n)]
        par_loads += [(WIO[:, j, 64 * a:64 * a + 64], w) for j, w in enumerate((w_in, w_out)) for a in range(2)]
        wts_loads = []
        for s in halves:
            wts_loads += [
                (WG[s, :, s], w_gcn.rearrange("l c m -> c l m")), (BIAS[s, 1:4], b_gcn.rearrange("l c -> c l")),
                (WL[s, 0, s], w_tok), (BIAS[s, 4:8], b1.rearrange("(q c) -> c q", c=64)), (BIAS[s, 9:10], wr),
            ]
        late_loads = [
            (tri_f, c_tri), (SUMM[:, :], c_sum), (DIG[:, :], c_digit),
            (BROW[:, 0, :], b_tok.partition_broadcast(TT)), (BROW[:, 1, :], b_in.partition_broadcast(TT)),
            (BROW[:, 2, :], b_out.partition_broadcast(TT)), (BROW[:, 3, :], b2.partition_broadcast(TT)),
            (BROW[:, 4, :], b2.partition_broadcast(TT)),
            (BIAS[:, 8:9], br.partition_broadcast(128)),
        ]
        def turned(r, h):
            if r < 2:
                return (2 * h + r) * NT
            q, h = ORDER.get((r - 1, h), (r - 1, h))
            return (q + 1) * UNITS + h * NT

        def normed(eng, q, h, k):
            q, h = ORDER.get((q, h), (q, h))
            if k < DVE_N:
                eng.wait_ge(t_ready, (2 * q + h) * DVE_N + k + 1)
            else:
                eng.wait_ge(t_ready_p, (2 * q + h) * (NT - DVE_N) + k - DVE_N + 1)

        POOL_E = list(range(7, HALVES, 4))
        ACT_E = [e for e in range(HALVES) if e not in POOL_E]

        def permuted(eng, e):
            if e in ACT_E:
                eng.wait_ge(perm_a, ACT_E.index(e) + 1)
            else:
                eng.wait_ge(perm_p, POOL_E.index(e) + 1)

        def permute(eng, copy, e, done):
            g = e // 2
            eng.wait_ge(x_in[g % 2], 32 * (g // 2 + 1))
            if e >= 4:
                eng.wait_ge(emb_t, 3 * (e - 3))
            src = XIN[:, g % 2, :].rearrange("p (a g j) -> p g a j", a=16, g=GRID)
            copy(XP[:, e % 4, :, :].rearrange("p g (a j) -> p g a j", a=16),
                 src[:, GH * (e % 2):GH * (e % 2) + GH]).then_inc(done, 1)

        @block.sync
        def _(sp):
            def load_pair(g):
                for a in range(2):
                    sp.dma_start(XIN[:, g % 2, a * 1792:a * 1792 + 1792], x_v[2 * g + a]).then_inc(x_in[g % 2], 16)

            sp.dma_start(IDENT[:, :], c_ident).then_inc(first_in, 16)
            sp.dma_start(DG[:, 0, :], c_deg).then_inc(first_in, 16)
            load_pair(0)
            sp.wait_ge(zeroed, 1)
            for dst, src in emb_loads:
                sp.dma_start(dst, src, allow_slow_non_contiguous=True).then_inc(emb_in, 16)
            for dst, src in pos_loads:
                sp.dma_start(dst, src, allow_slow_non_contiguous=True).then_inc(pos_in, 16)
            for dst, src in par_loads:
                sp.dma_start(dst, src).then_inc(par_in, 16)
            load_pair(1)
            for dst, src in graph_loads:
                sp.dma_start(dst, src).then_inc(graph_in, 16)
            sp.wait_ge(zeroed, 2)
            for dst, src in wts_loads:
                sp.dma_start(dst, src, allow_slow_non_contiguous=True).then_inc(wts_in, 16)
            for g in range(2, NP):
                permuted(sp, 2 * g - 4)
                permuted(sp, 2 * g - 3)
                load_pair(g)

            for l in range(NL):
                if l > 0:
                    sp.wait_ge(sconv_mm, 2 * l)
                else:
                    sp.wait_ge(zeroed, 3)
                    sp.wait_ge(pre_ev, NPREP)
                for a, s in enumerate(halves):
                    sp.dma_start(RW[s, :, 64 * a:64 * a + 64], R[s, l, :, 0:CH]).then_inc(taps_in, 16)
            sp.wait_ge(zeroed, 5)
            for s in halves:
                sp.dma_start(W1[s, :, s], w1.rearrange("c (q m) -> c q m", m=64)).then_inc(mlp_in, 16)
                sp.dma_start(W2[s, :, s], w2.rearrange("(q c) m -> c q m", c=64)).then_inc(mlp_in, 16)
            for g in range(LATE):
                sp.wait_ge(o_done, g + 1)
                for a in range(2):
                    sp.dma_start(out_v[:, :, 2 * g + a, :], T[:, :, 2 * g + a, :]).then_inc(stored, 16)
            for g, k0, k1 in ((LATE, 0, NT), (NP - 1, 0, 4), (NP - 1, 4, NT)):
                sp.wait_ge(o_late, (1, 2, 3)[(k0 > 0) + (g > LATE)])
                for a in range(2):
                    sp.dma_start(out_v[:, k0:k1, 2 * g + a, :], T[:, k0:k1, 2 * g + a, :]).then_inc(stored, 16)
            sp.wait_ge(stored, 16 * (NB + 2))

        @block.tensor
        def _(pe):
            mm = nc.tensor.matmul
            SXF = SX[:, :, :].rearrange("p g c -> p (g c)")

            def degree_rows(after):
                pe.wait_ge(dg_set, after)
                for k in range(NT):
                    last = mm(PS[:, 6 + k // 4, TT * (k % 4):TT * (k % 4) + TT], ONES[0:TT, 0:128], DIAG[:, k, :],
                              start=True, stop=True)
                last.then_inc(row_mm, 1)

            def grid_check(done):
                pe.wait_ge(pre_ev, done)
                pe.wait_ge(flag_mm, 1)
                mm(PS[0:1, 5, 0:1], ONES[0:EP, 0:1], NE_[:, 0:1], start=True, stop=True).then_inc(flag_mm, 1)
                degree_rows(1)

            def patches(e):
                permuted(pe, e)
                if e == 0:
                    pe.wait_ge(first_in, 32)
                for q in range(3):
                    if e > 0:
                        if q == 1:
                            pe.wait_ge(emb_tw, e)
                        else:
                            pe.wait_ge(emb_tv, 2 * e - 1 + q // 2)
                    for t in range(5 if q < 2 else 4):
                        last = nc.tensor.transpose(PS[:, q, 84 * t:84 * t + 84], XP[:, e % 4, 5 * q + t, :], IDENT[0:84, 0:84])
                    last.then_inc(emb_t, 1)

            def embed(e):
                pe.wait_ge(emb_tv, 2 * e + 2)
                pe.wait_ge(emb_tw, e + 1)
                if e > 0:
                    pe.wait_ge(emb_ev, e)
                for c in range(3):
                    last = mm(PS[:, 3, 0:HN], WE[:, c, :], XT[:, e % 2, c, :, :], start=(c == 0), stop=(c == 2))
                last.then_inc(emb_mm, 1)

            def prepare(i):
                for n in prep_level(i):
                    mms, _, after = prep[n]
                    need = max(after, n - 4)
                    if need >= 0:
                        pe.wait_ge(pre_ev, need + 1)
                    for o, lhsT, rhs in mms:
                        last = mm(o, lhsT, rhs, start=True, stop=True)
                    last.then_inc(pre_mm, 1)

            patches(0)
            pe.wait_ge(emb_in, 16 * len(emb_loads))
            for e in range(HALVES):
                if e + 1 < HALVES:
                    patches(e + 1)
                embed(e)
                if e == CHECK + 1:
                    pe.wait_ge(row_ev, 1)
                    pe.wait_ge(flag_set, 1)
                if e == 0:
                    pe.wait_ge(par_in, 16 * len(par_loads))
                    pe.wait_ge(zeroed, 2)
                prepare(e)
                if e == CHECK:
                    grid_check(level_end[e])
            for i in range(HALVES, len(level_end)):
                prepare(i)
            pe.wait_ge(emb_ev, HALVES)
            pe.wait_ge(pre_ev, NPREP)
            pe.wait_ge(wts_in, 16 * len(wts_loads))
            pe.wait_ge(graph_in, 16 * len(graph_loads))

            other_graph = nc.tensor.value_load(FLAG[0:1, 0:1], min_val=0, max_val=2 * NE)
            with nc.tensor.If(other_graph > 0):
                pe.wait_ge(eye_set, 1)
                for s in range(2):
                    if s:
                        pe.wait_ge(adj_ev, NT)
                    for k in range(NT):
                        w0 = N - TT * k + HN * s
                        last = mm(PS[0:TT, k, 0:HN], EYEW[:, N:N + TT], EYEW[:, w0:w0 + HN], start=True, stop=True)
                    if s == 0:
                        last.then_inc(hot_mm, 2)
                    with nc.tensor.Fori(0, EC // 2) as c:
                        for j in range(2):
                            pe.wait_ge(hot, c * 2 + (s * EC + j + 1))
                            for k in range(NT):
                                last = mm(PS[0:TT, k, 0:HN], OSRC[:, j, TT * k:TT * k + TT], ODST[:, j, :],
                                          start=False, stop=True, skip_group_check=True)
                            last.then_inc(hot_mm, 1)
                pe.wait_ge(adj_ev, 2 * NT)
                for k in range(NT):
                    for j in range(NT):
                        last = mm(PS[0:TT, 0, k:k + 1], ADJ[:, j, TT * k:TT * k + TT], ONES[0:TT, 0:1],
                                  start=(j == 0), stop=(j == NT - 1))
                last.then_inc(deg_mm, 1)
                degree_rows(2)
                pe.wait_ge(row_ev, 2)

            def hidden(l):
                for h in range(2):
                    if l > 0:
                        pe.wait_ge(h_ready, (l - 1) * NP + HP * (h + 1))
                    for k in range(NT):
                        n = l * UNITS + h * NT + k
                        if n >= 2:
                            pe.wait_ge(hw_ev, n - 1)
                        for g in range(HP):
                            last = mm(PS[0:TT, n % 2, 128 * g:128 * g + 128], UC[:, HP * h + g, TT * k:TT * k + TT],
                                      WG[:, l, :], start=True, stop=True)
                        last.then_inc(hw_mm, 1)

            def aggregate(l, sparse, g0, g1):
                for g in range(g0, g1):
                    n = l * NP + g
                    pe.wait_ge(hw_ev, l * UNITS + (g // HP + 1) * NT)
                    if n >= 2:
                        pe.wait_ge(agg_sc, n - 1)
                    for s in range(2):
                        started = False
                        for k in range(NT):
                            lo, hi = (max(TT * k - GRID, HN * s), min(TT * k + TT + GRID, HN * s + HN)) if sparse else \
                                (HN * s, HN * s + HN)
                            if lo >= hi:
                                continue
                            w = BAND[:, lo - TT * k + GRID:hi - TT * k + GRID] if sparse else ADJ[:, k, lo:hi]
                            last = mm(PS[:, 4 + 2 * (n % 2) + s, lo - HN * s:hi - HN * s], HW[:, k, g, :], w,
                                      start=not started, stop=True, skip_group_check=True)
                            started = True
                    last.then_inc(agg_mm, 1)

            def token_major(n, h, k, w):
                for g in range(HP):
                    last = mm(PS[0:TT, n % 2, 128 * g:128 * g + 128], UC[:, HP * h + g, TT * k:TT * k + TT],
                              w, start=True, stop=True)
                last.then_inc(tok_mm, 1)

            def h1_units(h, k0, k1):
                for k in range(k0, k1):
                    n = h * UNITS + k
                    pe.wait_ge(h_ready, (NG - 1) * NP + HP * (h + 1))
                    if n >= 2:
                        pe.wait_ge(tok_ev, n - 1)
                    token_major(n, h, k, WL[:, 0, :])

            def last_aggregates(sparse):
                aggregate(NG - 1, sparse, 0, HP)
                for i in range(HP):
                    h1_units(0, min(3 * i, NT), min(3 * i + 3, NT))
                    aggregate(NG - 1, sparse, HP + i, HP + i + 1)

            for l in range(NG - 1):
                hidden(l)
                with nc.tensor.If(other_graph > 0):
                    aggregate(l, False, 0, NP)
                with nc.tensor.Else():
                    aggregate(l, True, 0, NP)
            hidden(NG - 1)
            with nc.tensor.If(other_graph > 0):
                last_aggregates(False)
            with nc.tensor.Else():
                last_aggregates(True)

            def transposes(r, h, k0=0, k1=NT):
                for k in range(k0, k1):
                    n = turned(r, h) + k
                    if r == 1:
                        pe.wait_ge(tok_ev, h * UNITS + NT + k + 1)
                    else:
                        normed(pe, max(r - 1, 0), h, k)
                    b = 2
                    if r >= 5 and h == 1:
                        b = 6
                        pe.wait_ge(w_ev, NT * (r - 4))
                    if n >= 2:
                        pe.wait_ge(uc_ready, n if k == ACT_UC and r > 1 else n - 1)
                    for g in range(HP):
                        last = nc.tensor.transpose(PS[:, b + n % 2, TT * g:TT * g + TT],
                                                   T[:, k, 8 * h + 2 * g:8 * h + 2 * g + 2, :], IDENT[0:TT, 0:TT])
                    last.then_inc(tp_mm, 1)

            def win_units(h):
                for k in range(NT):
                    n = h * UNITS + NT + k
                    pe.wait_ge(uc_ready, turned(0, h) + k + 1)
                    pe.wait_ge(tok_ev, n - 1)
                    token_major(n, h, k, WL[:, 1, :])

            transposes(0, 0)
            win_units(0)
            h1_units(1, 0, 2)
            transposes(1, 0)

            def state_taps(s, p0, p1):
                l, h = s // 2, s % 2
                for p in range(p0, min(p1, LC)):
                    if p == 0:
                        pe.wait_ge(uc_ready, turned(l + 1, h) + NT)
                        pe.wait_ge(taps_in, 32 * (l + 1))
                        if s > 0:
                            pe.wait_ge(scan_ev, (LEVELS + 1) * s)
                    last = mm(PS[:, 6, 0:TT], RW[:, p, :], UCF[:, HP * N * h + LC - 1 - p:HP * N * (h + 1):LC],
                              start=(p == 0), stop=(p == LC - 1))
                    if p == LC - 1:
                        last.then_inc(sconv_mm, 1)

            def output_taps(s, p0, p1):
                l, h = s // 2, s % 2
                for p in range(p0, min(p1, LC)):
                    if p == 0:
                        pe.wait_ge(toep, l + 1)
                        if s > 1:
                            pe.wait_ge(zt_ev, s - 1)
                    last = mm(PS[0:64, 4 + h, 0:TT], RZ[:, p, 0:64], UCF[:, HP * N * h + LC - 1 - p:HP * N * (h + 1):LC],
                              start=(p == 0), stop=(p == LC - 1))
                    if p == LC - 1:
                        last.then_inc(zconv_mm, 1)

            def scan(s, r):
                sh = 1 << (r - 1)
                pe.wait_ge(scan_ev, (LEVELS + 1) * s + r)
                o = PS[:, 6, 0:TT].rearrange("p (g c) -> p g c", g=HP)
                mm(o[:, :, sh:LC], SWS[:, s // 2, r - 1, :], SC[:, (r - 1) % 2, :, 1:LC + 1 - sh],
                   start=False, stop=True, skip_group_check=True).then_inc(scan_mm, 1)

            def z_states(s):
                pe.wait_ge(scan_ev, (LEVELS + 1) * (s + 1))
                mm(PS[0:64, 4 + s % 2, 0:TT], SWO[:, s // 2, :], SXF, start=False, stop=True,
                   skip_group_check=True).then_inc(z_mm, 1)

            def z_tokens(s):
                pe.wait_ge(z_ev, s + 1)
                zv = ZS[:, :, :].rearrange("p a (g k c) -> p c k g a", g=HP, c=4)
                for c in range(4):
                    last = mm(PS[0:TT, 4 + s % 2, 128:128 + 8 * NT], EJ[:, c, :], zv[:, c], start=(c == 0), stop=(c == 3))
                last.then_inc(zt_mm, 1)

            def advance(s):
                for r in range(1, LEVELS + 1):
                    output_taps(s, 6 * r - 6, 6 * r)
                    scan(s, r)
                before = ((s - 1) // 2 + 2, (s - 1) % 2)
                last_step = s + 1 == STEPS
                if 0 < s and not last_step:
                    transposes(*before, 0, 1)
                if s > 0:
                    direct(s, 0)
                z_states(s)
                if 0 < s and not last_step:
                    transposes(*before, 1, ACT_UC)
                if s > 0:
                    direct(s, 1)
                z_tokens(s)
                if last_step:
                    transposes(*before, 0, ACT_UC)

            def direct(s, k):
                l, h = s // 2, s % 2
                n = 2 * UNITS + s * NT + k
                pe.wait_ge(tok_ev, n - 1)
                token_major(n, h, k, SWD[:, l, :, :])

            def project(h, k):
                w = h * NT + k
                pe.wait_ge(uc_ready, turned(5, h) + k + 1)
                if w >= 2:
                    pe.wait_ge(w_ev, w - 1)
                if h == 1:
                    pe.wait_ge(uc_ready, turned(5, h) + NT)
                for g in range(HP):
                    last = mm(PS[0:TT, 6 + w % 2, 128 * g:128 * g + 128], UC[:, HP * h + g, TT * k:TT * k + TT],
                              WL[:, 2, :], start=True, stop=True)
                last.then_inc(w_mm, 1)

            for k in range(2, NT):
                h1_units(1, k, k + 1)
                state_taps(0, 6 * (k - 2), 6 * (k - 1))
            advance(0)
            transposes(0, 1)
            win_units(1)
            transposes(1, 1)
            for s in range(STEPS):
                last_step = s + 1 == STEPS
                for k in range(NT):
                    if k >= 2 or s == 0:
                        direct(s, k)
                    if last_step and k == 0:
                        transposes((s - 1) // 2 + 2, (s - 1) % 2, ACT_UC, NT)
                    if 0 < s and not last_step:
                        transposes((s - 1) // 2 + 2, (s - 1) % 2, TURN[k], TURN[k + 1])
                    if not last_step:
                        feed = FEED if s > 0 else range(0, LC + 1, LC // NT)
                        state_taps(s + 1, feed[k], feed[k + 1])
                    else:
                        for unit in range(PROJECT[k], PROJECT[k + 1]):
                            project(0, unit)
                if not last_step:
                    advance(s + 1)

            def radix(r):
                pe.wait_ge(cnt_rd, r + 1)
                mm(PS[:, 7, 0:1], SUMM[:, 0:128], CNT[:, 1:2], start=True, stop=True).then_inc(rad_mm, 1)

            def masks():
                pe.wait_ge(msk_rd, 1)
                for v, row in enumerate((WROW[0:NB, :], GTR, EQR)):
                    for k in range(NT):
                        last = nc.tensor.transpose(PS[0:TT, 6, TT * v + NB * k:TT * v + NB * k + NB], row[:, TT * k:TT * k + TT],
                                                   IDENT[0:NB, 0:NB])
                last.then_inc(msk_mm, 1)

            def ranks():
                pe.wait_ge(msk_rd, 2)
                o = PS[0:TT, 7, 0:NT * NB].rearrange("p (k b) -> p k b", k=NT)
                mm(o, TRI[:, 0:TT], GEB[:, 1, :, :], start=True, stop=True)
                for k in range(NT - 1):
                    mm(o[:, k + 1:NT, :], TRI[:, TT:2 * TT],
                       GEB[:, 1, k:k + 1, :].broadcast_to([TT, NT - 1 - k, NB]), start=False, stop=True,
                       skip_group_check=True)
                mm(o, TRI[:, TT:2 * TT], GSB[:, :].unsqueeze(1).broadcast_to([TT, NT, NB]), start=False, stop=True,
                   skip_group_check=True).then_inc(msk_mm, 1)

            def up(g, q):
                for s in range(2):
                    n = 8 * g + 2 * q + s
                    if n >= 4:
                        pe.wait_ge(f_ev, n - 3)
                    else:
                        pe.wait_ge(tok_ev, 6 * UNITS)
                    mm(PS[:, n % 4, 0:HN], W1[:, q, :], UC[:, g, HN * s:HN * s + HN],
                       start=True, stop=True).then_inc(f_mm, 1)

            def down(g, s):
                n = 2 * g + s
                pe.wait_ge(f_ev, 8 * g + 8)
                if n >= 2:
                    pe.wait_ge(y_ev, n if g == LATE else n - 1)
                for k in range(4 * s, min(4 * s + 4, NT)):
                    for q in range(4):
                        last = mm(PS[0:TT, YB0 + s, 128 * (k - 4 * s):128 * (k - 4 * s) + 128],
                                  HID[:, g % 2, q, TT * k:TT * k + TT], W2[:, q, :], start=(q == 0), stop=(q == 3))
                last.then_inc(y_mm, 1)

            def pair(g, part):
                if part % 2:
                    down(g, part // 2)
                elif g + 1 < NP:
                    up(g + 1, part)
                    up(g + 1, part + 1)

            transposes(6, 0)
            pe.wait_ge(mlp_in, 16 * 4)
            pe.wait_ge(uc_ready, turned(6, 0) + NT)
            for q in range(4):
                up(0, q)
            for g in range(FIRST):
                for part in range(4):
                    pair(g, part)
                if g == 0:
                    transposes(5, 1)
                    for k in range(NT):
                        project(1, k)
            transposes(6, 1)
            pe.wait_ge(uc_ready, 7 * UNITS)
            pe.wait_ge(wr_set, 1)
            for s in range(2):
                for g in range(NP):
                    last = mm(PS[:, 6 + s, 0:HN], WR[:, g, :, :].rearrange("p d b -> p (d b)"), UC[:, g, HN * s:HN * s + HN],
                              start=(g == 0), stop=(g == NP - 1))
            last.then_inc(r_mm, 1)
            r = 0
            for g in range(FIRST, NP):
                for part in range(4):
                    pair(g, part)
                    if r < len(RADIX):
                        radix(r)
                    elif r == len(RADIX):
                        masks()
                    elif r == len(RADIX) + 1:
                        ranks()
                    r += 1

        @block.scalar
        def _(act):
            for e in range(2):
                permute(act, nc.scalar.copy, e, perm_a)
            for e in range(HALVES):
                if e >= 2:
                    act.wait_ge(emb_mm, e - 1)
                for q in (0, 2):
                    act.wait_ge(emb_t, 3 * e + q + 1)
                    n = 5 if q < 2 else 4
                    nc.scalar.copy(XT[:, e % 2, :, 5 * q:5 * q + n, :],
                                   PS[:, q, 0:84 * n].rearrange("p (g c i) -> p c g i", g=n, c=3)).then_inc(emb_tv, 1)
                if e + 2 in ACT_E:
                    permute(act, nc.scalar.copy, e + 2, perm_a)
            act.wait_ge(wts_in, 16 * len(wts_loads))
            def relu(l, g):
                n = l * NP + g
                act.wait_ge(agg_sc, n + 1)
                nc.scalar.activation(UC[:, g, :], AGG[:, n % 2, :], ACT.Relu, bias=BIAS[:, 1 + l:2 + l]).then_inc(h_ready, 1)

            for l in range(NG):
                for g in range(NP if l + 1 < NG else HP + 2):
                    relu(l, g)

            def to_uc(r, h, k0=0, k1=NT):
                for k in range(k0, k1):
                    n = turned(r, h) + k
                    act.wait_ge(tp_mm, n + 1)
                    nc.scalar.copy(UC[:, HP * h:HP * h + HP, TT * k:TT * k + TT],
                                   PS[:, (6 if r >= 5 and h == 1 else 2) + n % 2, 0:HP * TT].rearrange("p (g t) -> p g t", g=HP))\
                        .then_inc(uc_ready, 1)

            to_uc(0, 0)
            for g in range(HP + 2, NP):
                relu(NG - 1, g)
            to_uc(1, 0)

            def scan(s, r):
                if r == 0:
                    act.wait_ge(sconv_mm, s + 1)
                else:
                    act.wait_ge(scan_mm, LEVELS * s + r)
                src = PS[:, 6, 0:TT].rearrange("p (g c) -> p g c", g=HP)
                if r < LEVELS:
                    nc.scalar.copy(SC[:, r % 2, :, 1:LC + 1], src).then_inc(scan_ev, 1)
                else:
                    nc.scalar.copy(SX[:, :, 1:LC], src[:, :, 0:LC - 1]).then_inc(scan_ev, 1)

            def z_out(s):
                act.wait_ge(z_mm, s + 1)
                for a in range(2):
                    rows = slice(32 * a, 32 * a + 32)
                    ins = nc.scalar.copy(ZS[rows, a, :], PS[rows, 4 + s % 2, 0:TT])
                ins.then_inc(z_ev, 1)

            def z_tokens(s):
                act.wait_ge(zt_mm, s + 1)
                if s > 1:
                    act.wait_ge(tok_ev, 2 * UNITS + (s - 1) * NT)
                nc.scalar.copy(ZT[:, s % 2, :, :].rearrange("p k b -> p (k b)"),
                               PS[0:TT, 4 + s % 2, 128:128 + 8 * NT]).then_inc(zt_ev, 1)

            def advance(s):
                for r in range(LEVELS + 1):
                    scan(s, r)
                before = ((s - 1) // 2 + 2, (s - 1) % 2)
                last_step = s + 1 == STEPS
                if 0 < s and not last_step:
                    to_uc(*before, 0, 1)
                z_out(s)
                if 0 < s and not last_step:
                    to_uc(*before, 1, ACT_UC)
                z_tokens(s)
                if last_step:
                    to_uc(*before, 0, ACT_UC)

            def gelu(s, k):
                n = 2 * UNITS + s * NT + k
                u = s * NT + k
                act.wait_ge(tok_mm, n + 1)
                if u >= 2:
                    act.wait_ge(gel_used, u - 1)
                for b in range(8):
                    ins = nc.scalar.activation(GEL[:, n % 2, CH * b:CH * b + CH], PS[0:TT, n % 2, CH * b:CH * b + CH],
                                               ACT.Gelu, bias=ZT[:, s % 2, k, b:b + 1])
                ins.then_inc(tok_ev, 1)

            act.wait_ge(zeroed, 3)
            advance(0)
            to_uc(0, 1)
            to_uc(1, 1)
            for s in range(STEPS):
                act.wait_ge(zt_ev, s + 1)
                for k in range(NT):
                    gelu(s, k)
                if s + 1 < STEPS:
                    advance(s + 1)
            def mlp_gelu(g, q0):
                if g >= 2:
                    act.wait_ge(y_mm, 2 * g - 2)
                for q in range(q0, q0 + 2):
                    for s in range(2):
                        n = 8 * g + 2 * q + s
                        act.wait_ge(f_mm, n + 1)
                        nc.scalar.activation(HID[:, g % 2, q, HN * s:HN * s + HN], PS[:, n % 4, 0:HN],
                                             ACT.Gelu_apprx_tanh, bias=BIAS[:, 4 + q:5 + q]).then_inc(f_ev, 1)

            def y_out(g, s):
                nk, k0 = (4 if s == 0 else 3), 4 * s
                act.wait_ge(y_mm, 2 * g + s + 1)
                if s == 0:
                    act.wait_ge(res_b, 3 + g // HP)
                nc.scalar.copy(T[:, k0:k0 + nk, 2 * g:2 * g + 2, :].rearrange("p k a c -> p k (a c)"),
                               PS[0:TT, YB0 + s, 0:128 * nk].rearrange("p (k m) -> p k m", k=nk)).then_inc(y_ev, 1)

            to_uc(6, 0)
            mlp_gelu(0, 0)
            mlp_gelu(0, 2)
            for g in range(NP):
                if g == FIRST:
                    to_uc(6, 1)
                for part in range(2):
                    if g + 1 < NP:
                        mlp_gelu(g + 1, 2 * part)
                    if g < LATE:
                        y_out(g, part)
                if g == 0:
                    to_uc(5, 1)

        @block.gpsimd
        def _(pool):
            chain = [0]

            def link(ins):
                chain[0] += 1
                ins.then_inc(pool_ch, 1)
                pool.wait_ge(pool_ch, chain[0])

            g_ = nc.gpsimd
            g_.memset(WE[:, :, :], 0.0)
            g_.memset(BIAS[:, :], 0.0).then_inc(zeroed, 1)
            g_.memset(ONES[:, 0:128], 1.0)
            g_.memset(ONES[:, 128:129], 1.0 / CH)
            pool.wait_ge(first_in, 32)
            g_.tensor_copy(II[:, 0:64], IDENT[0:64, 0:64])
            g_.tensor_copy(II[:, 64:128], IDENT[0:64, 0:64])
            for a in range(2):
                g_.tensor_scalar(CEN[:, 64 * a:64 * a + 64], IDENT[0:64, 0:64], -1.0 / CH, None, ALU.add)
            for l in range(NL):
                g_.tensor_copy(Q[l][:, 0, 0:CH], IDENT[0:64, 0:64])
            g_.memset(WG[:, :, :], 0.0)
            g_.memset(WL[:, :, :], 0.0)
            g_.memset(SWD[:, :, :, :], 0.0)
            g_.memset(SWO[:, :, :], 0.0)
            link(g_.memset(SWS[:, :, :, :], 0.0))
            g_.memset(TRI[:, TT:2 * TT], 1.0).then_inc(zeroed, 1)
            pool.wait_ge(zeroed, 2)
            for dst, src in late_loads:
                pool.dma_start(dst, src).then_inc(late_in, 16)
            def mixer_tables():
                g_.memset(SX[:, :, :], 0.0)
                link(g_.memset(SC[:, :, :, :], 0.0))
                g_.memset(ZS[:, :, :], 0.0)
                link(g_.memset(EJ[:, :, :], 0.0))
                for a in range(2):
                    rows = slice(32 * a, 32 * a + LC)
                    link(g_.tensor_copy(EJ[rows, :, :].rearrange("p c (d j) -> p (c d) j", j=LC)[:, 0:16:5, :],
                                        IDENT[rows, rows].unsqueeze(1).broadcast_to([LC, 4, LC])))

            mixer_tables()
            pool.wait_ge(late_in, 16 * len(late_loads))
            link(g_.tensor_copy(TRI[:, 0:TT], tri_f))
            for e in POOL_E:
                permute(pool, g_.tensor_copy, e, perm_p)
            pool.wait_ge(flag_set, 1)
            other_graph = nc.gpsimd.value_load(FLAG[0:1, 0:1], min_val=0, max_val=2 * NE)
            pool.wait_ge(perm_p, len(POOL_E))
            pool.wait_ge(emb_mm, HALVES)
            with nc.gpsimd.If(other_graph > 0):
                g_.memset(EYEW[:, :], 0.0).then_inc(pool_gen, 1)
                pool.wait_ge(pool_gen, 1)
                g_.affine_select(out=EYEW[:, :], in_=EYEW[:, :], compare_op=ALU.not_equal, fill=1.0, base=N,
                                 pattern=[[-1, 2 * N]], channel_multiplier=1).then_inc(pool_gen, 1)
                pool.wait_ge(pool_gen, 2)
                g_.iota(IOTA[:, :], pattern=[[1, N]], base=0, channel_multiplier=0,
                        allow_small_or_imprecise_dtypes=True).then_inc(eye_set, 1)
                pool.wait_ge(eye_set, 1)
            pool.wait_ge(agg_mm, NG * NP)
            g_.memset(RW[:, :, :], 0.0).then_inc(zeroed, 1)
            pool.wait_ge(zeroed, 3)

            def mixer_room():
                pool.wait_ge(h_ready, NG * NP)
                g_.memset(RZ[:, :, :], 0.0).then_inc(zeroed, 1)
                pool.wait_ge(zeroed, 4)

            def norm(q, h, src):
                place = ORDER.get((q, h), (q, h))
                pool.wait_ge(mean_set, 2 * place[0] + place[1] + 1)
                for k in range(DVE_N, NT):
                    t = T[:, k, 8 * h:8 * h + 8, :]
                    mean, rstd = (v[:, h, 8 * k:8 * k + 8].unsqueeze(2).broadcast_to([TT, 8, CH]) for v in (MEAN, RSTD))
                    link(g_.tensor_tensor(t, src[:, k, 8 * h:8 * h + 8, :], mean, ALU.subtract))
                    g_.tensor_tensor(t, t, rstd, ALU.mult).then_inc(t_ready_p, 1)

            for h in range(2):
                norm(0, h, RES)
                if h == 0:
                    mixer_room()
                pool.wait_ge(t_ready, (h + 1) * DVE_N)
                rv = RES[:, :, 8 * h:8 * h + 8, :]
                for k in range(NT):
                    ins = g_.tensor_tensor(rv[:, k], rv[:, k], BROW[:, 2, :].unsqueeze(1).broadcast_to([TT, 8, CH]), ALU.add)
                ins.then_inc(res_b, 1)

            def mlp_room():
                pool.wait_ge(taps_in, 32 * NL)
                pool.wait_ge(toep, NL)
                link(g_.memset(RF[:, 0:1024], 0.0))
                g_.memset(RF[:, 1024:2048], 0.0).then_inc(zeroed, 1)
                pool.wait_ge(zeroed, 5)
                for a, s in enumerate(halves):
                    flat = RF[s, 1024:2048]
                    diag = bass.AP(tensor=flat.tensor, offset=flat.offset + a,
                                   ap=[list(flat.ap[0]), [8 * NB + 2, NP], [NB, 8]])
                    link(g_.tensor_copy(diag, BIAS[s, 9:10].unsqueeze(2).broadcast_to([64, NP, 8])))
                g_.memset(GSUM[:, :], 0.0).then_inc(wr_set, 1)
                pool.wait_ge(wr_set, 1)

            def last_norm(h):
                norm(5, h, RES)
                for k in (DVE_N - 1, NT - 1):
                    normed(pool, 5, h, k)
                for k in range(NT):
                    rv = RES[:, k, 8 * h:8 * h + 8, :]
                    ins = g_.tensor_tensor(rv, rv, T[:, k, 8 * h:8 * h + 8, :], ALU.add)
                ins.then_inc(res_b, 1)

            def b2_added(g):
                pool.wait_ge(y_ev, 2 * g + 2)
                t = T[:, :, 2 * g:2 * g + 2, :].rearrange("p k a c -> p k (a c)")
                row = BROW[:, 3:5, :].rearrange("p a c -> p (a c)").unsqueeze(1).broadcast_to([TT, NT, 2 * CH])
                g_.tensor_tensor(t, t, row, ALU.add).then_inc(y_b, 1)

            for s in range(STEPS):
                l, h = s // 2, s % 2
                if s == STEPS - 2:
                    mlp_room()
                for k in range(NT):
                    u = s * NT + k
                    pool.wait_ge(tok_ev, 2 * UNITS + u + 1)
                    tv = T[:, k, 8 * h:8 * h + 8, :]
                    g_.tensor_tensor(tv, tv, GEL[:, u % 2, :].rearrange("p (b c) -> p b c", b=8),
                                     ALU.add).then_inc(gel_used, 1)
                if s == STEPS - 1:
                    last_norm(0)
                norm(1 + l, h, T)
            b2_added(0)
            last_norm(1)
            for g in range(1, LATE):
                b2_added(g)
            for g in range(LATE):
                pool.wait_ge(y_w, g + 1)
                t = T[:, :, 2 * g:2 * g + 2, :]
                g_.tensor_tensor(t, t, RES[:, :, 2 * g:2 * g + 2, :], ALU.add).then_inc(o_done, 1)

        @block.vector
        def _(dve):
            chain = [0]
            v_ = nc.vector

            def link(ins):
                chain[0] += 1
                ins.then_inc(dve_ch, 1)
                dve.wait_ge(dve_ch, chain[0])

            def rsqrt(v, y, t, link=link):
                link(v_.tensor_scalar(t.bitcast(I32), v.bitcast(I32), 1, None, ALU.logical_shift_right))
                link(v_.tensor_scalar(y.bitcast(I32), t.bitcast(I32), -1.0, float(0x5f3759df), ALU.mult, ALU.add))
                for _ in range(3):
                    link(v_.scalar_tensor_tensor(out=t, in0=y, scalar=-0.5, in1=y, op0=ALU.mult, op1=ALU.mult))
                    link(v_.tensor_tensor(t, t, v, ALU.mult))
                    link(v_.scalar_tensor_tensor(out=y, in0=t, scalar=1.5, in1=y, op0=ALU.add, op1=ALU.mult))

            def degree_diagonal(link):
                rsqrt(DG[:, 0, :], DG[:, 1, :], DG[:, 2, :], link)
                for k in range(NT):
                    ins = v_.tensor_scalar(DIAG[:, k, :], IDENT[0:TT, 0:TT], DG[:, 1, k:k + 1], None, ALU.mult)
                ins.then_inc(dg_set, 1)

            def degree_rows(n):
                dve.wait_ge(row_mm, n)
                v_.tensor_copy(DROW[:, 0:4 * TT], PS[:, 6, 0:4 * TT])
                v_.tensor_copy(DROW[:, 4 * TT:N], PS[:, 7, 0:3 * TT]).then_inc(row_ev, 1)

            def grid_edges():
                dve.wait_ge(graph_in, 16 * len(graph_loads))
                link(v_.tensor_tensor(EC_GRID.bitcast(F32), EI, EC_GRID, ALU.not_equal))
                v_.tensor_reduce(NE_[:, 0:1], EC_GRID.bitcast(F32), AX.X, ALU.add).then_inc(flag_mm, 1)

            def grid_check():
                dve.wait_ge(flag_mm, 2)
                v_.tensor_copy(FLAG[:, :], PS[0:1, 5, 0:1]).then_inc(flag_set, 1)
                degree_rows(1)

            dve.wait_ge(first_in, 32)
            degree_diagonal(link)
            def group(e):
                if e >= 2:
                    dve.wait_ge(emb_mm, e - 1)
                dve.wait_ge(emb_t, 3 * e + 2)
                v_.tensor_copy(XT[:, e % 2, :, 5:10, :],
                               PS[:, 1, 0:420].rearrange("p (g c i) -> p c g i", g=5, c=3)).then_inc(emb_tw, 1)

            def embedded(e):
                dve.wait_ge(emb_mm, e + 1)
                cols = slice(GH * (e % 2), GH * (e % 2) + GH)
                v_.scalar_tensor_tensor(out=UC[:, e // 2, :].rearrange("p (i g) -> p g i", i=GRID)[:, cols, :],
                                        in0=PS[:, 3, 0:HN].rearrange("p (g i) -> p g i", g=GH), scalar=BIAS[:, 0:1],
                                        in1=POS[:, :].rearrange("p (i g) -> p g i", i=GRID)[:, cols, :],
                                        op0=ALU.add, op1=ALU.add).then_inc(emb_ev, 1)

            def prepare(i):
                for n in prep_level(i):
                    dve.wait_ge(pre_mm, n + 1)
                    for dst, src in prep[n][1]:
                        ins = v_.tensor_copy(dst, src)
                    ins.then_inc(pre_ev, 1)

            group(0)
            dve.wait_ge(pos_in, 16 * len(pos_loads))
            for e in range(HALVES):
                if e + 1 < HALVES:
                    group(e + 1)
                embedded(e)
                if e == CHECK - 1:
                    grid_edges()
                prepare(e)
                if e == CHECK:
                    grid_check()
            for i in range(HALVES, len(level_end)):
                prepare(i)
            dve.wait_ge(pre_ev, NPREP)

            other_graph = nc.vector.value_load(FLAG[0:1, 0:1], min_val=0, max_val=2 * NE)
            with nc.vector.If(other_graph > 0):
                general = [0]

                def glink(ins):
                    general[0] += 1
                    ins.then_inc(dve_gen, 1)
                    dve.wait_ge(dve_gen, general[0])

                dve.wait_ge(eye_set, 1)
                glink(v_.tensor_copy(EF, EI.rearrange("p (s j) -> p s j", s=2)))
                for s in range(2):
                    with nc.vector.Fori(0, EC // 2) as c:
                        for j in range(2):
                            dve.wait_ge(hot_mm, c * 2 + (s * EC + j + 1))
                            v_.tensor_scalar(OSRC[:, j, :], IOTA[0:EP, :], EF[:, 0, bass.ds(c * 2 + j, 1)], None, ALU.is_equal)
                            v_.tensor_scalar(ODST[:, j, :], IOTA[0:EP, HN * s:HN * s + HN], EF[:, 1, bass.ds(c * 2 + j, 1)],
                                             None, ALU.is_equal).then_inc(hot, 1)
                    dve.wait_ge(hot_mm, (s + 1) * EC + 2)
                    for k in range(NT):
                        v_.tensor_copy(ADJ[:, k, HN * s:HN * s + HN], PS[0:TT, k, 0:HN]).then_inc(adj_ev, 1)
                dve.wait_ge(deg_mm, 1)
                glink(v_.tensor_copy(DG[:, 0, :], PS[0:TT, 0, 0:NT]))
                degree_diagonal(glink)
                degree_rows(2)

            def scale(l, g):
                n = l * NP + g
                dve.wait_ge(agg_mm, n + 1)
                if n >= 2:
                    dve.wait_ge(h_ready, n - 1)
                b0 = 4 + 2 * (n % 2)
                v_.tensor_tensor(AGG[:, n % 2, :].rearrange("p (s j) -> p s j", s=2), PS[:, b0:b0 + 2, 0:HN],
                                 DROW[:, :].rearrange("p (s j) -> p s j", s=2), ALU.mult).then_inc(agg_sc, 1)

            for l in range(NG):
                for h in range(2):
                    for k in range(NT):
                        n = l * UNITS + h * NT + k
                        dve.wait_ge(hw_mm, n + 1)
                        if h == 0 and k == 0 and l > 0:
                            dve.wait_ge(agg_mm, l * NP)
                        v_.tensor_scalar(HW[:, k, HP * h:HP * h + HP, :].rearrange("p g m -> p (g m)"), PS[0:TT, n % 2, :],
                                         DG[:, 1, k:k + 1], None, ALU.mult).then_inc(hw_ev, 1)
                for g in range(NP if l + 1 < NG else HP):
                    scale(l, g)

            def statistics(q, h, src, k, twice=False):
                if k == 0 and q > 0:
                    normed(dve, q - 1, h, NT - 1)
                for b in range(8):
                    ins = v_.bn_stats(ST[:, h, 8 * k + b, :], src[:, k, 8 * h + b, :])
                if k + 1 == NT:
                    link(ins)

            def deviations(h, u, twice):
                me, mo, mean, rstd = ST[:, h, u, 1], ST[:, h, u, 4], MEAN[:, h, u], RSTD[:, h, u]
                diff, var, tmp, total, square, eps_var = (LNS[:, i, u] for i in range(6))
                v_.tensor_tensor(diff, me, mo, ALU.subtract)
                v_.tensor_tensor(total, me, mo, ALU.add)
                link(v_.tensor_tensor(tmp, ST[:, h, u, 2], ST[:, h, u, 5], ALU.add))
                v_.tensor_scalar(mean, total, 0.5, None, ALU.mult)
                v_.tensor_tensor(square, diff, diff, ALU.mult)
                link(v_.tensor_scalar(tmp, tmp, 1.0 / CH, None, ALU.mult))
                link(v_.scalar_tensor_tensor(out=var, in0=square, scalar=0.25, in1=tmp, op0=ALU.mult, op1=ALU.add))
                link(v_.tensor_scalar(eps_var, var, EPS, None, ALU.add))
                rsqrt(eps_var, rstd, tmp)
                if twice:
                    link(v_.tensor_tensor(tmp, rstd, rstd, ALU.mult))
                    link(v_.tensor_tensor(tmp, tmp, var, ALU.mult))
                    link(v_.tensor_scalar(eps_var, tmp, EPS, None, ALU.add))
                    rsqrt(eps_var, total, tmp)
                    link(v_.tensor_tensor(rstd, rstd, total, ALU.mult))

            def normalise(h, src, k0, k1):
                mean, rstd = (v[:, h, :].rearrange("p (k b) -> p k b", b=8).unsqueeze(3).broadcast_to([TT, NT, 8, CH])
                              for v in (MEAN, RSTD))
                t = T[:, :, 8 * h:8 * h + 8, :]
                for k in range(k0, k1 + 1):
                    if k < k1:
                        chain[0] += 1
                        v_.tensor_tensor(t[:, k], src[:, k, 8 * h:8 * h + 8, :], mean[:, k], ALU.subtract).then_inc(dve_ch, 1)
                    if k > k0:
                        dve.wait_ge(dve_ch, chain[0] - (k < k1))
                        v_.tensor_tensor(t[:, k - 1], t[:, k - 1], rstd[:, k - 1], ALU.mult).then_inc(t_ready, 1)

            def norm(q, h, src, ready=None, twice=False):
                if ready:
                    for k in range(NT):
                        ready(k)
                        statistics(q, h, src, k, twice)
                deviations(h, slice(0, 8 * NT), twice)
                v_.tensor_copy(LNS[:, 3, 0:1], LNS[:, 4, 0:1]).then_inc(mean_set, 1)
                normalise(h, src, 0, DVE_N)

            def row(j):
                return BROW[:, j, :].unsqueeze(1).broadcast_to([TT, 8, CH])

            def from_psum(n, h, k, dst, other):
                dve.wait_ge(tok_mm, n + 1)
                v_.tensor_tensor(dst[:, k, 8 * h:8 * h + 8, :], PS[0:TT, n % 2, :].rearrange("p (b c) -> p b c", b=8),
                                 other, ALU.add).then_inc(tok_ev, 1)

            def h1_unit(h, k):
                n = h * UNITS + k
                from_psum(n, h, k, RES, row(0))
                dve.wait_ge(tok_ev, n + 1)
                statistics(0, h, RES, k)

            def toeplitz(l):
                for a, s in enumerate(halves):
                    flat = RZ[s, :, :].rearrange("p q z -> p (q z)")
                    diag = bass.AP(tensor=flat.tensor, offset=flat.offset + LC + 32 * a,
                                   ap=[list(flat.ap[0]), [ZW - 1, LC], [1, LC]])
                    link(v_.tensor_copy(diag, R[s, l, :, CH].unsqueeze(1).broadcast_to([64, LC, LC])))
                v_.memset(RZ[halves[1], :, 60:64], 0.0)
                v_.memset(RZ[halves[0], :, LC:60], 0.0).then_inc(toep, 1)

            dve.wait_ge(late_in, 16 * len(late_loads))
            for i in range(3):
                for k in range(3 * i, min(3 * i + 3, NT)):
                    h1_unit(0, k)
                if i < 2:
                    scale(NG - 1, HP + i)
            norm(0, 0, RES)
            for g in range(HP + 2, NP):
                scale(NG - 1, g)
            for k in range(NT):
                from_psum(NT + k, 0, k, T, row(1))
            dve.wait_ge(zeroed, 4)
            toeplitz(0)
            for k in range(NT):
                h1_unit(1, k)
            norm(0, 1, RES)
            for k in range(NT):
                from_psum(UNITS + NT + k, 1, k, T, row(1))

            def to_uc(r, h):
                for k in range(ACT_UC, NT):
                    n = turned(r, h) + k
                    dve.wait_ge(tp_mm, n + 1)
                    v_.tensor_copy(UC[:, HP * h:HP * h + HP, TT * k:TT * k + TT],
                                   PS[:, 2 + n % 2, 0:HP * TT].rearrange("p (g t) -> p g t", g=HP)).then_inc(uc_ready, 1)

            def last_norm(h):
                dve.wait_ge(res_b, h + 1)
                for k in range(NT):
                    w = h * NT + k
                    dve.wait_ge(w_mm, w + 1)
                    rv = RES[:, k, 8 * h:8 * h + 8, :]
                    v_.tensor_tensor(rv, PS[0:TT, 6 + w % 2, :].rearrange("p (b c) -> p b c", b=8), rv, ALU.add).then_inc(w_ev, 1)
                    dve.wait_ge(w_ev, w + 1)
                    statistics(5, h, RES, k)
                norm(5, h, RES)

            for s in range(STEPS):
                if s == STEPS - 1:
                    last_norm(0)
                if s % 2 and s + 1 < STEPS:
                    dve.wait_ge(zconv_mm, s + 1)
                    toeplitz(s // 2 + 1)
                norm(1 + s // 2, s % 2, T, lambda k: dve.wait_ge(gel_used, s * NT + k + 1), s // 2 + 1 == NL)
                if s + 1 < STEPS:
                    to_uc(s // 2 + 2, s % 2)
            last_norm(1)

            def threshold(key):
                link(v_.tensor_scalar(KEY[:, 1:2], key, 31, -1, ALU.arith_shift_right, ALU.bitwise_xor))
                link(v_.tensor_scalar(KEY[:, 2:3], KEY[:, 1:2], -2147483648, None, ALU.bitwise_or))
                link(v_.tensor_tensor(KEY[:, 3:4], KEY[:, 2:3], key, ALU.bitwise_xor))

            def radix(r):
                sh = RADIX[r]
                tail = r == len(RADIX) - 1
                link(v_.tensor_tensor(KEY[:, 0:1], PREF[:, 0:1], DIG[:, r:r + 1], ALU.bitwise_or))
                threshold(KEY[:, 0:1])
                link(v_.tensor_scalar(JUNK, WROW, KEY[:, 3:4].bitcast(F32), 0.0, ALU.is_ge, ALU.add, accum_out=CNT[:, 0:1]))
                v_.tensor_scalar(CNT[:, 1:2], CNT[:, 0:1], SUMM[:, 128:129], 0.5 if tail else 1.0, ALU.is_ge,
                                 ALU.mult).then_inc(cnt_rd, 1)

            def digit(r):
                dve.wait_ge(rad_mm, r + 1)
                link(v_.tensor_scalar(PREF[:, 1:2], PS[:, 7, 0:1], -1.0, None, ALU.add))
                if RADIX[r]:
                    link(v_.tensor_scalar(PREF[:, 1:2], PREF[:, 1:2], RADIX[r], None, ALU.logical_shift_left))
                link(v_.tensor_tensor(PREF[:, 0:1], PREF[:, 0:1], PREF[:, 1:2], ALU.bitwise_or))

            def mask_rows():
                threshold(PREF[:, 0:1])
                thr = KEY[0:NB, 3:4].bitcast(F32)
                v_.tensor_scalar(GTR, WROW[0:NB, :], thr, None, ALU.is_gt)
                v_.tensor_scalar(EQR, WROW[0:NB, :], thr, None, ALU.is_equal).then_inc(msk_rd, 1)

            def masks():
                dve.wait_ge(msk_mm, 1)
                v_.tensor_copy(WTOK[:, :, :].rearrange("p k b -> p (k b)"), PS[0:TT, 6, 0:TT])
                v_.tensor_copy(GEB[:, 0, :, :].rearrange("p k b -> p (k b)"), PS[0:TT, 6, TT:2 * TT])
                link(v_.tensor_copy(GEB[:, 1, :, :].rearrange("p k b -> p (k b)"), PS[0:TT, 6, 2 * TT:3 * TT]))
                link(v_.tensor_reduce(GSUM[:, :], GEB[:, 0, :, :].rearrange("p k b -> p b k"), AX.X, ALU.add))
                v_.tensor_copy(GSB[:, :], GSUM[:, :]).then_inc(msk_rd, 1)
                dve.wait_ge(msk_mm, 2)
                o = PS[0:TT, 7, 0:NT * NB].rearrange("p (k b) -> p k b", k=NT)
                link(v_.scalar_tensor_tensor(out=few, in0=o, scalar=float(KK), in1=GEB[:, 1, :, :], op0=ALU.is_lt, op1=ALU.mult))
                link(v_.tensor_tensor(few, few, GEB[:, 0, :, :], ALU.add))
                link(v_.tensor_tensor(WM[:, :, :], few, WTOK[:, :, :], ALU.mult))

            def finish(g, k0=0, k1=NT):
                t = T[:, k0:k1, 2 * g:2 * g + 2, :]
                w = WM[:, k0:k1, 2 * g:2 * g + 2].unsqueeze(3).broadcast_to([TT, k1 - k0, 2, CH])
                link(v_.tensor_tensor(t, t, w, ALU.mult))
                v_.tensor_tensor(t, t, RES[:, k0:k1, 2 * g:2 * g + 2, :], ALU.add).then_inc(o_late, 1)

            def y_out(g, s):
                k0, k1 = (0, 4) if s == 0 else (4, NT)
                dve.wait_ge(y_mm, 2 * g + s + 1)
                dve.wait_ge(res_b, 4)
                row = BROW[:, 3:5, :].rearrange("p a c -> p (a c)").unsqueeze(1).broadcast_to([TT, k1 - k0, 2 * CH])
                v_.tensor_tensor(T[:, k0:k1, 2 * g:2 * g + 2, :].rearrange("p k a c -> p k (a c)"),
                                 PS[0:TT, YB0 + s, 0:128 * (k1 - k0)].rearrange("p (k m) -> p k m", m=128),
                                 row, ALU.add).then_inc(y_ev, 1)
                dve.wait_ge(y_ev, 2 * g + s + 1)

            dve.wait_ge(r_mm, 1)
            link(v_.tensor_scalar(WROW.rearrange("p (s j) -> p s j", s=2), PS[:, 6:8, 0:HN], BIAS[:, 8:9], None, ALU.add))
            link(v_.memset(PREF[:, :], 0))
            for r in range(len(RADIX)):
                radix(r)
                digit(r)
            mask_rows()
            masks()
            def weighted(g):
                dve.wait_ge(y_b, g + 1)
                t = T[:, :, 2 * g:2 * g + 2, :]
                v_.tensor_tensor(t, t, WM[:, :, 2 * g:2 * g + 2].unsqueeze(3).broadcast_to([TT, NT, 2, CH]),
                                 ALU.mult).then_inc(y_w, 1)

            for g in range(4):
                weighted(g)
            y_out(LATE, 0)
            weighted(4)
            y_out(LATE, 1)
            weighted(5)
            finish(LATE)
            for s in range(2):
                y_out(NP - 1, s)
                finish(NP - 1, 4 * s, 4 if s == 0 else NT)


_INS = ["x", "L0_tok_W_embed", "L0_tok_b_embed", "L0_tok_W_gcn", "L0_tok_b_gcn", "L0_tok_W_out", "L0_tok_b_out",
        "L0_tok_edge_index", "L0_attn_Win", "L0_attn_bin_", "L0_attn_Wout", "L0_attn_bout", "L0_attn_A", "L0_attn_Bm",
        "L0_attn_Cm", "L0_attn_Dm", "L0_ffn_wr", "L0_ffn_br", "L0_ffn_w1", "L0_ffn_b1", "L0_ffn_w2", "L0_ffn_b2"]


def _shape_constants():
    import numpy as np
    pos = np.arange(N, dtype=np.float32)[:, None]
    div = np.exp(np.arange(0, CH, 2, dtype=np.float32) * np.float32(-np.log(10000.0) / CH)).astype(np.float32)
    ang = (pos * div).astype(np.float32).astype(np.float64)
    pe = np.zeros((N, CH), np.float32)
    pe[:, 0::2] = np.sin(ang)
    pe[:, 1::2] = np.cos(ang)
    tri = np.triu(np.ones((TT, TT), np.float32), 1)
    same = np.equal(np.arange(128)[:, None] % NB, np.arange(128)[None, :] % NB).astype(np.float32)
    d = (np.arange(128) // NB).astype(np.int64)[:, None]
    digit = np.concatenate([(d << s if s else d & 3) for s in RADIX], 1)
    reach = np.where(d == 0, 0, KK).astype(np.float32)
    digit[:NB] = 0x00800000
    digit = (digit & 0xFFFFFFFF).astype(np.uint32).view(np.int32)
    same = np.concatenate([same, reach], 1)
    i, j = np.divmod(np.arange(N), GRID)
    pairs = []
    for n in range(N):
        if j[n] < GRID - 1:
            pairs.append((n, n + 1))
        if i[n] < GRID - 1:
            pairs.append((n, n + GRID))
    e = np.array(pairs, np.int32).T
    grid_edges = np.concatenate([e, e[::-1]], 1)
    adj = np.eye(N + 2 * TT, dtype=np.float32)
    for n in range(N + 2 * TT - 1):
        if (n + 1) % GRID:
            adj[n, n + 1] = adj[n + 1, n] = 1
        if n + GRID < N + 2 * TT:
            adj[n, n + GRID] = adj[n + GRID, n] = 1
    band = adj[TT:2 * TT, TT - GRID:2 * TT + GRID]
    deg = 1 + np.bincount(grid_edges[1], minlength=N).astype(np.float32)
    deg = deg.reshape(NT, TT).T
    pos = np.concatenate([pe.T, pe.T], 0)
    tables = {"ident": np.eye(128, dtype=np.float32), "tri": tri, "sum": same, "pos": pos, "digit": digit,
              "edges": grid_edges, "band": band, "deg": deg}
    return {k: np.ascontiguousarray(v) for k, v in tables.items()}



def kernel(**inputs):
    import numpy as np
    import concourse.bacc as bacc
    from concourse.bass_utils import run_bass_kernel_spmd

    nc = bacc.Bacc("TRN2", target_bir_lowering=False, num_devices=1)
    arrays, args = {}, []
    given = [(n, inputs[n]) for n in _INS] + list(_shape_constants().items())
    for name, value in given:
        a = np.ascontiguousarray(value)
        arrays[f"in_{name}"] = a
        args.append(nc.dram_tensor(f"in_{name}", a.shape, mybir.dt.from_np(a.dtype), kind="ExternalInput").ap())
    out = nc.dram_tensor("out_0", (NB, N, CH), F32, kind="ExternalOutput").ap()
    tower(nc, *args, out)
    r = run_bass_kernel_spmd(nc, [arrays], core_ids=[0])
    return r.results[0]["out_0"]
```
